# Optimizing a Trainium2 kernel written in Bass

```python
import numpy as np
import jax
import jax.numpy as jnp

def _softmax(x, axis=-1):
    return jax.nn.softmax(x, axis=axis)

def _gelu(x):
    return jax.nn.gelu(x, approximate=True)

def _silu(x):
    return jax.nn.silu(x)

def _sigmoid(x):
    return jax.nn.sigmoid(x)

def _layernorm(x, axis=-1, eps=1e-05):
    m = jnp.mean(x, axis=axis, keepdims=True)
    v = jnp.var(x, axis=axis, keepdims=True)
    return (x - m) / jnp.sqrt(v + eps)

def _scatter_add(tgt, idx, src, axis=0):
    return tgt.at[idx].add(src)

def _segment_sum(src, seg, n):
    return jax.ops.segment_sum(src, seg, n)
kernel_name = 'mk_audio_tower_d1_tok_aud1d1024_r4_e67961'

def setup_inputs(seed: int=0):
    np.random.seed(seed)
    _w = jnp.asarray

    def _rec_inputs():
        import jax
        import jax.numpy as jnp
        _rk = jax.random.key(seed)
        x = -9.80646e-05 + 1.00041 * jax.random.normal(jax.random.fold_in(_rk, 1), (16, 4000), jnp.float32)
        return x
    x = _rec_inputs()

    def _L0_tok_setup():
        import jax, jax.numpy as jnp
        import numpy as np
        TOKEN_LEN = 16
        key = jax.random.key(seed)
        ks = jax.random.split(key, 7)
        B, L = (64, 2048)
        D_IN, D_MID, D_OUT = (2 * TOKEN_LEN, 1024, 256)
        s_in = 1.0 / np.sqrt(D_IN)
        s_mid = 1.0 / np.sqrt(D_MID)
        return {'x': jax.random.normal(ks[0], (B, L), dtype=jnp.float32), 'W_h': jax.random.normal(ks[1], (D_IN, D_MID), dtype=jnp.float32) * s_in, 'b_h': jax.random.normal(ks[2], (D_MID,), dtype=jnp.float32) * s_in, 'W_o': jax.random.normal(ks[3], (D_MID, D_OUT), dtype=jnp.float32) * s_mid, 'b_o': jax.random.normal(ks[4], (D_OUT,), dtype=jnp.float32) * s_mid, 'W_r': jax.random.normal(ks[5], (D_IN, D_OUT), dtype=jnp.float32) * s_in, 'b_r': jax.random.normal(ks[6], (D_OUT,), dtype=jnp.float32) * s_in}
    _L0_tok_all = _L0_tok_setup()
    _L0_tok_in = {k: v for k, v in _L0_tok_all.items() if k in ('W_h', 'b_h', 'W_o', 'b_o', 'W_r', 'b_r')}
    del _L0_tok_all

    def _L0_attn_setup():
        import jax, jax.numpy as jnp
        import numpy as np
        B, S, H = (4, 512, 256)
        EXP_BITS, SIG_BITS = (5, 10)

        def quantize(x):
            bias = 2 ** (EXP_BITS - 1) - 1
            ax = jnp.abs(x)
            e = jnp.floor(jnp.log2(jnp.where(ax > 0, ax, 1.0)))
            e = jnp.clip(e, 1 - bias, bias)
            scale = jnp.exp2(e - SIG_BITS)
            q = jnp.round(x / scale) * scale
            max_val = (2.0 - 2.0 ** (-SIG_BITS)) * 2.0 ** bias
            q = jnp.clip(q, -max_val, max_val)
            return x + jax.lax.stop_gradient(q - x)
        key = jax.random.key(seed)
        ks = jax.random.split(key, 7)
        w_scale = 1.0 / np.sqrt(H)
        return {'x': jax.random.normal(ks[0], (B, S, H), dtype=jnp.float32), 'Wq': jax.random.normal(ks[1], (H, H), dtype=jnp.float32) * w_scale, 'bq': jax.random.normal(ks[2], (H,), dtype=jnp.float32) * 0.01, 'Wk': jax.random.normal(ks[3], (H, H), dtype=jnp.float32) * w_scale, 'bk': jax.random.normal(ks[4], (H,), dtype=jnp.float32) * 0.01, 'Wv': jax.random.normal(ks[5], (H, H), dtype=jnp.float32) * w_scale, 'bv': jax.random.normal(ks[6], (H,), dtype=jnp.float32) * 0.01}
    _L0_attn_all = _L0_attn_setup()
    _L0_attn_in = {k: v for k, v in _L0_attn_all.items() if k in ('Wq', 'bq', 'Wk', 'bk', 'Wv', 'bv')}
    del _L0_attn_all

    def _L0_ffn_setup():
        import jax, jax.numpy as jnp
        import numpy as np
        B, S, D = (2, 512, 256)
        H, HKV = (16, 4)
        HD = D // H
        F, E, K = (512, 8, 2)
        THETA = 10000.0
        EPS = 1e-05

        def _rmsnorm(x, w):
            return x * jax.lax.rsqrt(jnp.mean(x * x, axis=-1, keepdims=True) + EPS) * w

        def _rope_cos_sin(seq_len, head_dim, theta):
            inv_freq = 1.0 / theta ** (jnp.arange(0, head_dim, 2, dtype=jnp.float32) / head_dim)
            freqs = jnp.arange(seq_len, dtype=jnp.float32)[:, None] * inv_freq
            return (jnp.cos(freqs), jnp.sin(freqs))

        def _apply_rope(x, cos, sin):
            x1, x2 = jnp.split(x, 2, axis=-1)
            c = cos[None, :, None, :]
            s = sin[None, :, None, :]
            return jnp.concatenate([x1 * c - x2 * s, x2 * c + x1 * s], axis=-1)
        key = jax.random.key(seed)
        ks = jax.random.split(key, 12)
        s = 0.02
        return {'hidden_states': jax.random.normal(ks[0], (B, S, D), jnp.float32), 'ln1_w': 1.0 + 0.1 * jax.random.normal(ks[1], (D,), jnp.float32), 'ln2_w': 1.0 + 0.1 * jax.random.normal(ks[2], (D,), jnp.float32), 'Wq': s * jax.random.normal(ks[3], (D, H * HD), jnp.float32), 'Wk': s * jax.random.normal(ks[4], (D, HKV * HD), jnp.float32), 'Wv': s * jax.random.normal(ks[5], (D, HKV * HD), jnp.float32), 'Wo': s * jax.random.normal(ks[6], (H * HD, D), jnp.float32), 'Wr': s * jax.random.normal(ks[7], (D, E), jnp.float32), 'Wg': s * jax.random.normal(ks[8], (E, D, F), jnp.float32), 'Wu': s * jax.random.normal(ks[9], (E, D, F), jnp.float32), 'Wd': s * jax.random.normal(ks[10], (E, F, D), jnp.float32)}
    _L0_ffn_all = _L0_ffn_setup()
    _L0_ffn_in = {k: v for k, v in _L0_ffn_all.items() if k in ('ln1_w', 'ln2_w', 'Wq', 'Wk', 'Wv', 'Wo', 'Wr', 'Wg', 'Wu', 'Wd')}
    del _L0_ffn_all
    return {'x': x, 'L0_tok_W_h': _L0_tok_in['W_h'], 'L0_tok_b_h': _L0_tok_in['b_h'], 'L0_tok_W_o': _L0_tok_in['W_o'], 'L0_tok_b_o': _L0_tok_in['b_o'], 'L0_tok_W_r': _L0_tok_in['W_r'], 'L0_tok_b_r': _L0_tok_in['b_r'], 'L0_attn_Wq': _L0_attn_in['Wq'], 'L0_attn_bq': _L0_attn_in['bq'], 'L0_attn_Wk': _L0_attn_in['Wk'], 'L0_attn_bk': _L0_attn_in['bk'], 'L0_attn_Wv': _L0_attn_in['Wv'], 'L0_attn_bv': _L0_attn_in['bv'], 'L0_ffn_ln1_w': _L0_ffn_in['ln1_w'], 'L0_ffn_ln2_w': _L0_ffn_in['ln2_w'], 'L0_ffn_Wq': _L0_ffn_in['Wq'], 'L0_ffn_Wk': _L0_ffn_in['Wk'], 'L0_ffn_Wv': _L0_ffn_in['Wv'], 'L0_ffn_Wo': _L0_ffn_in['Wo'], 'L0_ffn_Wr': _L0_ffn_in['Wr'], 'L0_ffn_Wg': _L0_ffn_in['Wg'], 'L0_ffn_Wu': _L0_ffn_in['Wu'], 'L0_ffn_Wd': _L0_ffn_in['Wd']}

def reference(x, L0_tok_W_h, L0_tok_b_h, L0_tok_W_o, L0_tok_b_o, L0_tok_W_r, L0_tok_b_r, L0_attn_Wq, L0_attn_bq, L0_attn_Wk, L0_attn_bk, L0_attn_Wv, L0_attn_bv, L0_ffn_ln1_w, L0_ffn_ln2_w, L0_ffn_Wq, L0_ffn_Wk, L0_ffn_Wv, L0_ffn_Wo, L0_ffn_Wr, L0_ffn_Wg, L0_ffn_Wu, L0_ffn_Wd):
    import jax
    import jax.numpy as jnp

    def _L0_tok_ref(x, W_h, b_h, W_o, b_o, W_r, b_r):
        import jax, jax.numpy as jnp
        import numpy as np
        TOKEN_LEN = 16
        mask = jnp.ones_like(x)
        L = x.shape[-1]
        pad = -L % TOKEN_LEN
        x = jnp.pad(x, ((0, 0), (pad, 0)))
        mask = jnp.pad(mask, ((0, 0), (pad, 0)))
        B = x.shape[0]
        n = x.shape[-1] // TOKEN_LEN
        xp = x.reshape(B, n, TOKEN_LEN)
        mp = mask.reshape(B, n, TOKEN_LEN)
        xm = jnp.concatenate([xp, mp], axis=-1)
        hid = jax.nn.silu(jnp.einsum('bnd,dm->bnm', xm, W_h) + b_h)
        out = jnp.einsum('bnm,mh->bnh', hid, W_o) + b_o
        res = jnp.einsum('bnd,dh->bnh', xm, W_r) + b_r
        return out + res

    def _L0_attn_ref(x, Wq, bq, Wk, bk, Wv, bv):
        import jax, jax.numpy as jnp
        import numpy as np
        B, S, H = (4, 512, 256)
        EXP_BITS, SIG_BITS = (5, 10)

        def quantize(x):
            bias = 2 ** (EXP_BITS - 1) - 1
            ax = jnp.abs(x)
            e = jnp.floor(jnp.log2(jnp.where(ax > 0, ax, 1.0)))
            e = jnp.clip(e, 1 - bias, bias)
            scale = jnp.exp2(e - SIG_BITS)
            q = jnp.round(x / scale) * scale
            max_val = (2.0 - 2.0 ** (-SIG_BITS)) * 2.0 ** bias
            q = jnp.clip(q, -max_val, max_val)
            return x + jax.lax.stop_gradient(q - x)
        q = quantize(jnp.einsum('bsh,oh->bso', x, Wq) + bq)
        k = quantize(jnp.einsum('bsh,oh->bso', x, Wk) + bk)
        v = quantize(jnp.einsum('bsh,oh->bso', x, Wv) + bv)
        inv_sqrt_h = 1.0 / H ** 0.5
        scores = quantize(jnp.einsum('bsh,bth->bst', q, k) * inv_sqrt_h)
        attn = quantize(jax.nn.softmax(scores, axis=-1))
        return jnp.einsum('bst,bth->bsh', attn, v)

    def _L0_ffn_ref(hidden_states, ln1_w, ln2_w, Wq, Wk, Wv, Wo, Wr, Wg, Wu, Wd):
        import jax, jax.numpy as jnp
        import numpy as np
        B, S, D = (2, 512, 256)
        H, HKV = (16, 4)
        HD = D // H
        F, E, K = (512, 8, 2)
        THETA = 10000.0
        EPS = 1e-05

        def _rmsnorm(x, w):
            return x * jax.lax.rsqrt(jnp.mean(x * x, axis=-1, keepdims=True) + EPS) * w

        def _rope_cos_sin(seq_len, head_dim, theta):
            inv_freq = 1.0 / theta ** (jnp.arange(0, head_dim, 2, dtype=jnp.float32) / head_dim)
            freqs = jnp.arange(seq_len, dtype=jnp.float32)[:, None] * inv_freq
            return (jnp.cos(freqs), jnp.sin(freqs))

        def _apply_rope(x, cos, sin):
            x1, x2 = jnp.split(x, 2, axis=-1)
            c = cos[None, :, None, :]
            s = sin[None, :, None, :]
            return jnp.concatenate([x1 * c - x2 * s, x2 * c + x1 * s], axis=-1)
        b, s, d = hidden_states.shape
        residual = hidden_states
        h = _rmsnorm(hidden_states, ln1_w)
        q = (h @ Wq).reshape(b, s, H, HD)
        k = (h @ Wk).reshape(b, s, HKV, HD)
        v = (h @ Wv).reshape(b, s, HKV, HD)
        cos, sin = _rope_cos_sin(s, HD, THETA)
        q = _apply_rope(q, cos, sin)
        k = _apply_rope(k, cos, sin)
        rep = H // HKV
        k = jnp.repeat(k, rep, axis=2)
        v = jnp.repeat(v, rep, axis=2)
        scores = jnp.einsum('bqhd,bkhd->bhqk', q, k) / np.sqrt(HD).astype(np.float32)
        causal = jnp.tril(jnp.ones((s, s), dtype=bool))
        scores = jnp.where(causal[None, None], scores, jnp.finfo(scores.dtype).min)
        attn = jax.nn.softmax(scores, axis=-1)
        ctx = jnp.einsum('bhqk,bkhd->bqhd', attn, v).reshape(b, s, H * HD)
        attn_out = ctx @ Wo
        h = jnp.clip(residual + attn_out, -100.0, 100.0)
        residual = h
        hn = _rmsnorm(h, ln2_w)
        flat = hn.reshape(b * s, d)
        logits = flat @ Wr
        probs = jax.nn.softmax(logits, axis=-1)
        topv, topi = jax.lax.top_k(probs, K)
        topv = topv / jnp.sum(topv, axis=-1, keepdims=True)
        w = jnp.sum(jax.nn.one_hot(topi, E, dtype=flat.dtype) * topv[..., None], axis=1)
        g = jnp.einsum('td,edf->etf', flat, Wg)
        u = jnp.einsum('td,edf->etf', flat, Wu)
        a = jax.nn.silu(g) * u
        o = jnp.einsum('etf,efd->etd', a, Wd)
        moe_out = jnp.einsum('te,etd->td', w, o).reshape(b, s, d)
        out = jnp.clip(residual + moe_out, -100.0, 100.0)
        return out
    h = _L0_tok_ref(x, L0_tok_W_h, L0_tok_b_h, L0_tok_W_o, L0_tok_b_o, L0_tok_W_r, L0_tok_b_r)
    h = h + _L0_attn_ref(_layernorm(h, axis=-1), L0_attn_Wq, L0_attn_bq, L0_attn_Wk, L0_attn_bk, L0_attn_Wv, L0_attn_bv)
    h = h + _L0_ffn_ref(_layernorm(h, axis=-1), L0_ffn_ln1_w, L0_ffn_ln2_w, L0_ffn_Wq, L0_ffn_Wk, L0_ffn_Wv, L0_ffn_Wo, L0_ffn_Wr, L0_ffn_Wg, L0_ffn_Wu, L0_ffn_Wd)
    return h

_drawn_inputs = setup_inputs


def setup_inputs(seed=0):
    import zlib

    import numpy as np

    out = dict(_drawn_inputs(seed))
    spreads = {}
    factors = {'L0_attn_bq': 8.0,
     'L0_attn_bk': 8.0,
     'L0_attn_bv': 7.764,
     'L0_ffn_ln1_w': 8.0,
     'L0_ffn_ln2_w': 8.0,
     'L0_ffn_Wq': 8.0,
     'L0_ffn_Wk': 8.0,
     'L0_ffn_Wr': 8.0,
     'L0_ffn_Wg': 8.0,
     'L0_ffn_Wu': 8.0,
     'L0_ffn_Wd': 8.0}
    for name, (base, spread) in spreads.items():
        noise = np.random.default_rng([zlib.crc32(name.encode()), seed]).standard_normal(out[name].shape)
        drawn = base * np.exp(spread * noise) if base else spread * noise
        out[name] = jnp.asarray(drawn.astype(out[name].dtype))
    for name, factor in factors.items():
        out[name] = (out[name] * factor).astype(out[name].dtype)
    return out
```

```python
from contextlib import ExitStack

import numpy as np

import concourse.bass as bass
from concourse import mybir

B, SAMPLES, TOK = 16, 4000, 16
S = SAMPLES // TOK
QT = 2
T = S // QT
NT = B * QT
D, MID = 256, 1024
DC, MC = D // 128, MID // 128
NH, NKV, HD = 16, 4, 16
REP = NH // NKV
NE, F, TOPK = 8, 512, 2
FC = F // 128
PARTS = 6 * HD
STACK = PARTS + 3
QKV = (NH + 2 * NKV) * HD
EPS = 1e-5
CLIP = 100.0
F16MAX = 65504.0
NEG = -1e30

REGION = -(-(B * S + 128) // 128) * 128
TILES = (B * S * TOPK + NE * 127) // 128


def constants():
    t = {}
    p = np.arange(128)
    t["ident"] = np.eye(128)
    k = np.arange(T)
    t["mask_q"] = np.where(k[None, :] > p[:, None], NEG, 0.0)
    t["mask_k"] = np.where(k[None, :] < p[:, None], NEG, 0.0)
    t["before"] = (p[:, None] < k[None, :]).astype(float)
    pos = np.arange(S, dtype=np.float32)
    inv = (1.0 / np.float32(10000.0) ** (np.arange(0, HD, 2, dtype=np.float32) / np.float32(HD))).astype(np.float32)
    ang = pos[:, None] * inv
    cos, sin = np.cos(ang).astype(np.float32), np.sin(ang).astype(np.float32)
    for name, tab in (("cos", np.concatenate([cos, cos], 1)), ("sin", np.concatenate([-sin, sin], 1))):
        full = np.zeros((128, QT, HD), np.float32)
        full[:T] = tab.reshape(QT, T, HD).transpose(1, 0, 2)
        t[name] = full.reshape(128, -1)
    t["rev"] = np.tile(NE - np.arange(NE), (128, 1))
    t["ebase"] = np.tile(np.arange(NE) * REGION, (128, 1))
    row = p[:, None]
    head = row % NH
    real = row < 3 * NH
    t["delta"] = (real & (head % REP == np.arange(REP)[None, :])).astype(float)
    sel = real[:, :, None] & (head[:, :, None] // REP == np.arange(NKV)[None, :, None])
    t["sel"] = np.broadcast_to(sel, (128, NKV, T)).astype(float).reshape(128, -1)
    t["tile"] = np.tile(np.arange(TILES), (128, 1))
    where, cols, at = {}, [], 0
    for name, a in t.items():
        where[name] = (at, a.shape[1])
        cols.append(a.astype(np.float32))
        at += a.shape[1]
    return np.ascontiguousarray(np.concatenate(cols, 1)), where


def build(nc, x, tWh, tbh, tWo, tbo, tWr, tbr, aWq, abq, aWk, abk, aWv, abv, ln1, ln2, fWq, fWk, fWv, fWo,
          fWr, fWg, fWu, fWd, const, out):
    f32, f16, bf16 = mybir.dt.float32, mybir.dt.float16, mybir.dt.bfloat16
    i32 = mybir.dt.int32
    ALU, ACT, AX = mybir.AluOpType, mybir.ActivationFunctionType, mybir.AxisListType
    ds = bass.ds
    _, CO = constants()
    NC = const.shape[1]

    ctx = ExitStack()
    with ctx:
        def sb(name, shape, dt):
            return ctx.enter_context(nc.sbuf_tensor(name, shape, dt))

        def sem(name):
            return ctx.enter_context(nc.semaphore(name))

        x_rows = nc.dram_tensor("x_rows", (NE * REGION, D), f32, kind="Internal").ap()
        y_rows = nc.dram_tensor("y_rows", (TILES * 128, D), f32, kind="Internal").ap()
        h2_rows = nc.dram_tensor("h2_rows", (B, T, QT, D), f32, kind="Internal").ap()

        WGU = sb("WGU", [128, NE, DC, 2 * F], f32)
        WD = sb("WD", [128, NE, FC, D], f32)
        H = sb("H", [128, NT, D], f32)
        C = sb("C", [128, NC], f32)
        Wat = sb("Wat", [128, DC, 3 * D], f32)
        Wqkv = sb("Wqkv", [128, DC, QKV], f32)
        Wo = sb("Wo", [128, DC, D], f32)
        Wr = sb("Wr", [128, DC, NE], f32)
        bqk = sb("bqk", [128, 2, DC], f32)
        bv = sb("bv", [128, D], f32)
        w2b = sb("w2b", [128, D], f32)
        lnc = sb("lnc", [128, DC], f32)
        identb = sb("identb", [128, 128], bf16)
        identh = sb("identh", [128, 128], f16)
        maskqb = sb("maskqb", [128, T], bf16)
        maskkb = sb("maskkb", [128, T], bf16)
        beforeb = sb("beforeb", [128, T], bf16)
        onesb = sb("onesb", [128, T], bf16)
        selb = sb("selb", [128, NKV, T], bf16)
        onesf = sb("onesf", [128, 1], f32)
        mhalf = sb("mhalf", [128, 2], f32)
        epsc = sb("epsc", [128, 2], f32)
        gate_v = sb("gate_v", [1, 1], f32)
        gate_p = sb("gate_p", [1, 1], f32)
        wtop = sb("wtop", [128, NT, 2], f32)
        dest = sb("dest", [128, 2, NT], i32)
        run = sb("run", [128, NE], f32)
        counts = sb("counts", [128, NE], i32)
        tile_e = sb("tile_e", [1, TILES], i32)
        tile_in = sb("tile_in", [1, TILES], i32)

        def const_at(name, parts=128):
            a, n = CO[name]
            return C[0:parts, a:a + n]

        ident = const_at("ident")

        POOL = 14640
        pool = sb("pool", [128, POOL], f32)

        class Carve:

            def __init__(self, at=0):
                self.at = at

            def __call__(self, shape, dt=f32):
                n = int(np.prod(shape))
                words = n if dt in (f32, i32) else (n + 1) // 2
                words += words % 2
                a = pool[:, self.at:self.at + words]
                self.at += words
                assert self.at <= POOL, self.at
                if dt != f32:
                    a = a.bitcast(dt)
                a = a[:, 0:n]
                if len(shape) == 2:
                    a = a.rearrange("p (a b) -> p a b", a=shape[0])
                elif len(shape) == 3:
                    a = a.rearrange("p (a b c) -> p a b c", a=shape[0], b=shape[1])
                return a

        c1 = Carve()
        hid = [c1((MC, 4 * T)) for _ in range(2)]
        WoT = c1((MC, D))
        Wst = c1((MID + D,), bf16)
        X = c1((NT, TOK))
        xst = c1((4, 128), bf16)
        xd = c1((4, TOK))
        xT = [c1((4 * T,), bf16) for _ in range(2)]
        Hf = H[:, :, :].rearrange("p t d -> p (t d)")
        rawW = Hf[:, 0:3 * DC * D].rearrange("p (w c h) -> p w c h", w=3, c=DC)
        raw0 = Hf[:, 2048:2048 + MID + D]
        raw1 = Hf[:, 3584:3584 + MID + D]
        rsum = Hf[:, 5120:5120 + MID + D]
        rbias = Hf[:, 6400:6400 + MID + 2 * D]
        WDf = WD[:, :, :, :].rearrange("p e c d -> p (e c d)")
        half = (MID + D) // 2
        sp_h, sp_m, sp_l, rp_h, rp_m, rp_l = (WDf[:, half * i:half * (i + 1)].bitcast(bf16) for i in range(6))
        sp_d = WDf[:, 6 * half:8 * half]
        c2 = Carve()
        xn = c2((QT, D))
        ca = Carve(0)
        att = ca((QT, S), f16)
        attT = ca((QT, S), f16)
        xnT = c2((DC, S))
        qk = c2((2 * DC, S), f16)
        vq = c2((QT, D), f16)
        sq = c2((QT, S), f16)
        ex = c2((QT, S))
        stA = c2((QT, 6))
        mvA = c2((QT, 2))
        smA = c2((16,))
        y = c2((QT, D))
        yT = c2((DC, S))
        cxT, hnT = yT, yT
        qkv_at = c2.at
        qkv = c2((QT, QKV))
        cx = Carve(qkv_at)((QT, D))
        vz = c2((QT, NKV, 128))
        qst = c2((QT * NH, PARTS), bf16)
        kst = c2((QT * NKV, PARTS), bf16)
        qts_at = c2.at
        QTs = c2((NH, S), bf16)
        CT = Carve(qts_at)((REP, S))
        KTs = c2((NKV, S), bf16)
        Dm = c2((REP, S), bf16)
        pt_at = c2.at
        PT = [c2((3, REP * T)) for _ in range(2)]
        cr = Carve(pt_at)
        t1 = cr((QT, (NH + NKV) * HD))
        t2 = cr((QT, (NH + NKV) * HD))
        roq, rok = cr((QT * NH, HD)), cr((QT * NKV, HD))
        dq, dk = cr((QT * NH, HD)), cr((QT * NKV, HD))
        sqj = t1
        hn = c2((QT, D))
        stB = c2((QT, 6))
        mvB = c2((QT, 2))
        smB = c2((16,))
        mxu = c2((3, NH))
        nmx = c2((QT, NH))
        dmx = c2((QT, NH))
        mx3 = c2((QT, 6 * NH), bf16)
        rcx = c2((QT, NH))
        lgx, prob, hit, cand, one1, one2, rest, posn = (c2((QT, NE)) for _ in range(8))
        rmax, rsm, rinv, top1, top2, first, topsum = (c2((QT,)) for _ in range(7))
        both = c2((QT, NE), bf16)
        dsum = c2((2, QT))
        dnow = c2((2, QT), i32)
        c4 = Carve()
        xin = [c4((D,)) for _ in range(2)]
        xTe = c4((DC, 128))
        gs = c4((F,))
        ga = [c4((F,)) for _ in range(2)]
        gaT = c4((FC, 128))
        yo = [c4((D,)) for _ in range(2)]
        zer = c4((D,))
        over = c4((TILES, NE))
        over2 = c4((TILES, NE))
        m_e, m_st, m_ok, m_row = (c4((TILES,)) for _ in range(4))
        cnt, ntil, mend, ones8, shift, dshift = (c4((NE,)) for _ in range(6))
        destf, acc, term = (c4((2 * NT,)) for _ in range(3))
        cnt_i = c4((NE,), i32)
        c5 = Carve(c4.at)
        y1, y2, h2b = ([c5((QT, D)) for _ in range(2)] for _ in range(3))
        gidx = [c5((2, QT), i32) for _ in range(2)]
        wnow = [c5((QT, 2)) for _ in range(2)]

        banks = [ctx.enter_context(nc.psum_tensor(f"bank{i}", [128, 512], f32)) for i in range(8)]

        def bank(i, shape, dt=f32, parts=128):
            a = banks[i][0:parts, :]
            if dt != f32:
                a = a.bitcast(dt)
            a = a[:, 0:int(np.prod(shape))]
            if len(shape) == 2:
                a = a.rearrange("p (a b) -> p a b", a=shape[0])
            elif len(shape) == 3:
                a = a.rearrange("p (a b c) -> p a b c", a=shape[0], b=shape[1])
            return a

        A_T, A_P, A_S, B_T, B_U, R0 = 0, 1, 2, 3, 4, 5
        RING = (R0, R0 + 1, R0 + 2)

        names = """ld_const ld_x ld_tok ld_bias ld_attn ld_ffn ld_vec ld_wgu ld_wd stacked
        setup_dve setup_consts setup_wt_ps setup_wt setup_fold csum_ps split_rows split_bias zeroed
        tok_dve tok_split tok_xT_ps tok_xT tok_hid_ps tok_hid tok_out_ps tok_h0 tok_h1
        a_dve a_var a_rstd a_xn a_xnT_ps a_xnT a_q_ps a_k_ps a_v_ps a_qk16 a_qk a_v a_s_ps a_nmx a_exp a_att
        a_attT_ps a_attT a_av_ps a_h1
        b_dve b_pool b_var b_rstd b_y b_ms b_r1 b_yT_ps b_yT b_qkv_ps b_qkv b_vz b_sinpart b_stacks
        b_T_ps b_T_act b_T_dve b_s_ps b_s_max b_mx3 b_mx3T_ps b_D b_st_ps b_exp b_pv_ps
        b_CT_act b_CT_dve b_ct_ps b_cx b_cxT_ps b_cxT b_o_ps b_h2 b_h2_st b_ms2 b_r2 b_hn b_hnT_ps b_hnT
        b_lg_ps b_lmx b_lexp b_both b_cnt_ps b_dest b_scat b_hn_free
        m_dve m_maps m_dest m_zero m_fill m_x0 m_x1 m_xT_ps0 m_xT_ps1 m_xT m_g_ps m_u_ps m_silu m_a m_aT_ps m_aT_act
        m_aT_dve m_y_ps m_y m_st0 m_st1
        f_h0 f_h1 f_idx f_w f_dve f_y0 f_y1 f_out f_st0 f_st1"""
        s = {n: sem(n) for n in names.split()}

        class Chain:

            def __init__(self, eng, step, i, n):
                self.eng, self.step, self.i, self.n, self.k = eng, step, i, n, 0

            def link(self, ins):
                ins.then_inc(self.step, 1)
                self.k += 1
                assert self.k <= self.n, "more links than stated"
                self.eng.wait_ge(self.step, self.i * self.n + self.k)

            def end(self):
                assert self.k == self.n, (self.k, self.n)

        block = ctx.enter_context(nc.Block())
        NPAIR = B // 2
        UNITS = 3 * NKV

        def flat(a):
            return a.rearrange("p a b -> p (a b)")

        def tile_of(a, i):
            return flat(a[0:T, ds(i, 1), :])

        @block.sync
        def _(sp):
            nkv = NKV * HD
            row = lambda v: v.rearrange("(o n) -> o n", o=1)
            for free, n in ((s["tok_h0"], 1), (s["tok_h1"], 1), (s["b_h2_st"], 16), (s["b_hn_free"], 1), (s["m_y"], 1),
                            (s["m_xT_ps0"], 1), (s["m_xT_ps1"], 1), (s["m_st0"], 16), (s["m_st1"], 16), (s["f_st0"], 16), (s["f_st1"], 16)):
                sp.sem_inc(free, n)
            sp.dma_start(C[:], const).then_inc(s["ld_const"], 16)
            sp.dma_start(raw0[0:TOK, 0:MID], tWh[0:TOK, :]).then_inc(s["ld_tok"], 16)
            sp.dma_start(raw0[0:TOK, MID:MID + D], tWr[0:TOK, :]).then_inc(s["ld_tok"], 16)
            sp.dma_start(raw1[0:TOK, 0:MID], tWh[TOK:2 * TOK, :]).then_inc(s["ld_tok"], 16)
            sp.dma_start(raw1[0:TOK, MID:MID + D], tWr[TOK:2 * TOK, :]).then_inc(s["ld_tok"], 16)
            sp.dma_start(rbias[0:1, 0:MID], row(tbh)).then_inc(s["ld_bias"], 16)
            sp.dma_start(rbias[0:1, MID:MID + D], row(tbo)).then_inc(s["ld_bias"], 16)
            sp.dma_start(rbias[0:1, MID + D:MID + 2 * D], row(tbr)).then_inc(s["ld_bias"], 16)
            sp.dma_start(X[0:T], x.rearrange("b (t p d) -> p (b t) d", t=QT, d=TOK)).then_inc(s["ld_x"], 16)
            sp.dma_start(WoT[:], tWo.rearrange("(c p) d -> p c d", p=128)).then_inc(s["ld_tok"], 16)
            for w, a in enumerate((aWq, aWk, aWv)):
                sp.dma_start(rawW[:, w], a.rearrange("(c p) h -> p c h", p=128)).then_inc(s["ld_attn"], 16)
            for i, v in enumerate((abq, abk)):
                sp.dma_start(bqk[:, i, :], v.rearrange("(c p) -> p c", p=128), allow_slow_non_contiguous=True).then_inc(s["ld_vec"], 16)
            sp.dma_start(lnc[:], ln1.rearrange("(c p) -> p c", p=128), allow_slow_non_contiguous=True).then_inc(s["ld_vec"], 16)
            sp.dma_start(bv[:], row(abv).to_broadcast([128, D])).then_inc(s["ld_vec"], 16)
            sp.dma_start(w2b[:], row(ln2).to_broadcast([128, D])).then_inc(s["ld_vec"], 16)
            sp.dma_start(Wqkv[:, :, 0:D], fWq.rearrange("(c p) n -> p c n", p=128)).then_inc(s["ld_ffn"], 16)
            sp.dma_start(Wqkv[:, :, D:D + nkv], fWk.rearrange("(c p) n -> p c n", p=128)).then_inc(s["ld_ffn"], 16)
            sp.dma_start(Wqkv[:, :, D + nkv:QKV], fWv.rearrange("(c p) n -> p c n", p=128)).then_inc(s["ld_ffn"], 16)
            sp.dma_start(Wo[:], fWo.rearrange("(c p) n -> p c n", p=128)).then_inc(s["ld_ffn"], 16)
            sp.dma_start(Wr[:], fWr.rearrange("(c p) n -> p c n", p=128)).then_inc(s["ld_ffn"], 16)
            sp.wait_ge(s["split_rows"], 1)
            for i, part in enumerate((sp_h, sp_m, sp_l, sp_h, sp_m, sp_h)):
                sp.dma_start(Wst[TOK * i:TOK * (i + 1), :], part[0:TOK, :]).then_inc(s["stacked"], 16)
            sp.wait_ge(s["split_bias"], 1)
            for i, part in enumerate((rp_h, rp_m, rp_l)):
                sp.dma_start(Wst[PARTS + i:PARTS + i + 1, :], part[0:1, :]).then_inc(s["stacked"], 16)
            for e in range(NE):
                sp.dma_start(WGU[:, e, :, 0:F], fWg[e].rearrange("(c p) f -> p c f", p=128)).then_inc(s["ld_wgu"], 16)
                sp.dma_start(WGU[:, e, :, F:2 * F], fWu[e].rearrange("(c p) f -> p c f", p=128)).then_inc(s["ld_wgu"], 16)
            sp.wait_ge(s["stacked"], 16 * 9)
            for e in range(NE):
                sp.dma_start(WD[:, e], fWd[e].rearrange("(c p) d -> p c d", p=128)).then_inc(s["ld_wd"], 16)

            with sp.Fori(0, B) as b:
                sp.wait_ge(s["b_h2"], b + 1)
                sp.dma_start(h2_rows[ds(b, 1)].rearrange("o p t d -> (o p) t d"), y[0:T]).then_inc(s["b_h2_st"], 16)
                sp.wait_ge(s["b_scat"], b * (16 * 2 * QT) + 16 * 2 * QT)
                sp.sem_inc(s["b_hn_free"], 1)

            sp.wait_ge(s["m_maps"], 1)
            sp.wait_ge(s["m_zero"], 1)
            for e in range(NE):
                n = sp.value_load(counts[0:1, e:e + 1], min_val=0, max_val=B * S)
                sp.dma_start(x_rows[ds(n + e * REGION, 128), :], zer[:]).then_inc(s["m_fill"], 16)
            sp.wait_ge(s["m_fill"], 16 * NE)
            sp.wait_ge(s["b_scat"], 16 * 2 * QT * B)
            with sp.Fori(0, TILES // 2) as j:
                for par, (landed, used) in enumerate(((s["m_x0"], s["m_xT_ps0"]), (s["m_x1"], s["m_xT_ps1"]))):
                    sp.wait_ge(used, j + 1)
                    r = sp.value_load(tile_in[0:1, ds(2 * j + par, 1)], min_val=0, max_val=NE * REGION - 128)
                    sp.dma_start(xin[par], x_rows[ds(r, 128), :]).then_inc(landed, 16)

            sp.wait_ge(s["b_h2_st"], 16 * B + 16)
            with sp.Fori(0, B // 2) as j:
                for par, (landed, stored) in enumerate(((s["f_h0"], s["f_st0"]), (s["f_h1"], s["f_st1"]))):
                    sp.wait_ge(stored, 16 * j + 16)
                    sp.dma_start(h2b[par][0:T],
                                 h2_rows[ds(2 * j + par, 1)].rearrange("o p t d -> (o p) t d")).then_inc(landed, 16)
                for par, stored in enumerate((s["f_st0"], s["f_st1"])):
                    sp.wait_ge(s["f_out"], 2 * j + par + 1)
                    sp.dma_start(out[ds(2 * j + par, 1)].rearrange("o (t p) d -> p (o t) d", t=QT),
                                 h2b[par][0:T]).then_inc(stored, 16)
            sp.wait_ge(s["f_st0"], 16 * (B // 2 + 1))
            sp.wait_ge(s["f_st1"], 16 * (B // 2 + 1))

        @block.tensor
        def _(pe):
            mm = nc.tensor.matmul
            tr = nc.tensor.transpose
            pe.wait_ge(s["ld_tok"], 16 * 5)
            pe.wait_ge(s["setup_consts"], 1)
            for i, (a, n) in enumerate(((0, 512), (512, 512), (MID, D))):
                last = mm(bank(i, (512,))[0:1, 0:n], onesf[0:TOK, 0:1], raw1[0:TOK, a:a + n], start=True, stop=True)
            last.then_inc(s["csum_ps"], 1)
            pe.wait_ge(s["ld_attn"], 16 * 3)
            for w in range(3):
                for hc in range(DC):
                    for oc in range(DC):
                        last = tr(bank(3 + w, (DC, DC, 128))[:, hc, oc], rawW[:, w, oc, 128 * hc:128 * (hc + 1)], ident)
            last.then_inc(s["setup_wt_ps"], 1)
            pe.wait_ge(s["setup_wt"], 1)
            pe.wait_ge(s["split_bias"], 1)
            pe.wait_ge(s["stacked"], 16 * 9)

            def tok_x(i, par):
                pe.wait_ge(s["tok_split"], i + 1)
                for q in range(4):
                    last = tr(bank(0, (4, 128), bf16)[0:STACK, q, 0:T], xst[0:T, q, 0:STACK], identb[0:T, 0:T])
                last.then_inc(s["tok_xT_ps"], 1)
                pe.wait_ge(s["tok_xT"], i + 1)

            def tok_hidden(i, par, m):
                if not (isinstance(i, int) and 8 * i + m - 3 <= 0):
                    pe.wait_ge(s["tok_hid"], i * 8 + (m - 3))
                mm(bank(1 + m % 4, (4 * T,)), Wst[0:STACK, 128 * m:128 * (m + 1)], xT[par][0:STACK, :],
                   start=True, stop=True).then_inc(s["tok_hid_ps"], 1)

            def tok_out(i, par, q):
                if q == 0:
                    pe.wait_ge(s["tok_hid"], i * 8 + 8)
                pe.wait_ge((s["tok_h0"], s["tok_h1"])[q % 2], i * 2 + (q // 2 + 1))
                o = bank(5 + q % 2, (D,), parts=T)
                for m in range(MC):
                    mm(o, hid[par][:, m, T * q:T * (q + 1)], WoT[:, m, :], start=(m == 0), stop=False)
                mm(o, xT[par][0:STACK, T * q:T * (q + 1)], Wst[0:STACK, MID:MID + D],
                   start=False, stop=True).then_inc(s["tok_out_ps"], 1)

            def tok_both(i, par):
                tok_x(i, par)
                for q in range(4):
                    tok_hidden(i, par, 2 * q)
                    tok_hidden(i, par, 2 * q + 1)
                    tok_out(i - 1, 1 - par, q)

            tok_x(0, 0)
            for m in range(MC):
                tok_hidden(0, 0, m)
            with pe.Fori(0, (NPAIR - 2) // 2) as j:
                tok_both(2 * j + 1, 1)
                tok_both(2 * j + 2, 0)
            tok_both(NPAIR - 1, 1)
            for q in range(4):
                tok_out(NPAIR - 1, 1, q)

            def a_transpose(a):
                pe.wait_ge(s["a_xn"], a + 1)
                for t in range(QT):
                    for c in range(DC):
                        last = tr(bank(A_T, (DC, S))[:, c, T * t:T * (t + 1)], xn[0:T, t, 128 * c:128 * (c + 1)],
                                  ident[0:T, 0:T])
                last.then_inc(s["a_xnT_ps"], 1)

            def a_project(a):
                pe.wait_ge(s["a_xnT"], a + 1)
                for w, (at, done) in enumerate(((A_P, s["a_q_ps"]), (A_S, s["a_k_ps"]))):
                    for o in range(DC):
                        for c in range(DC):
                            last = mm(bank(at, (DC, S))[:, o], Wat[:, c, D * w + 128 * o:D * w + 128 * (o + 1)],
                                      xnT[:, c], start=(c == 0), stop=(c == DC - 1))
                    last.then_inc(done, 1)
                for t in range(QT):
                    for c in range(DC):
                        last = mm(bank(A_T, (QT, D), parts=T)[:, t], xnT[:, c, T * t:T * (t + 1)], Wat[:, c, 2 * D:3 * D],
                                  start=(c == 0), stop=(c == DC - 1))
                last.then_inc(s["a_v_ps"], 1)

            def a_scores(a):
                pe.wait_ge(s["a_qk"], a + 1)
                for t in range(QT):
                    for c in range(DC):
                        last = mm(bank(A_P, (QT, S), parts=T)[:, t], qk[:, c, T * t:T * (t + 1)], qk[:, DC + c],
                                  start=(c == 0), stop=(c == DC - 1))
                last.then_inc(s["a_s_ps"], 1)

            def a_transpose_probs(a):
                pe.wait_ge(s["a_att"], a + 1)
                for k in range(QT):
                    for t in range(QT):
                        last = tr(bank(A_S, (QT, QT, 128), f16, T)[:, k, t, 0:T], att[0:T, t, T * k:T * (k + 1)],
                                  identh[0:T, 0:T])
                last.then_inc(s["a_attT_ps"], 1)

            def a_values(a):
                pe.wait_ge(s["a_attT"], a + 1)
                pe.wait_ge(s["a_v"], a + 1)
                for t in range(QT):
                    for k in range(QT):
                        last = mm(bank(A_T, (QT, D), parts=T)[:, t], attT[0:T, k, T * t:T * (t + 1)], vq[0:T, k],
                                  start=(k == 0), stop=(k == QT - 1))
                last.then_inc(s["a_av_ps"], 1)

            BLOCKS = ((0, 0), (1, 0), (1, 1))

            def b_transpose(b):
                pe.wait_ge(s["b_y"], b + 1)
                for t in range(QT):
                    for c in range(DC):
                        last = tr(bank(B_T, (DC, S))[:, c, T * t:T * (t + 1)], y[0:T, t, 128 * c:128 * (c + 1)],
                                  ident[0:T, 0:T])
                last.then_inc(s["b_yT_ps"], 1)

            def b_project(b):
                pe.wait_ge(s["b_yT"], b + 1)
                for t in range(QT):
                    for c in range(DC):
                        last = mm(bank(RING[t], (QKV,), parts=T), yT[:, c, T * t:T * (t + 1)], Wqkv[:, c],
                                  start=(c == 0), stop=(c == DC - 1))
                last.then_inc(s["b_qkv_ps"], 1)

            def b_transpose_stacks(b, f):
                if f == 0:
                    pe.wait_ge(s["b_stacks"], b + 1)
                if f == 2:
                    pe.wait_ge(s["b_T_dve"], b * 3 + 1)
                if f == 3:
                    pe.wait_ge(s["b_T_act"], b * 2 + 1)
                if f == 4:
                    pe.wait_ge(s["b_T_dve"], b * 3 + 2)
                o = bank((B_T, B_U)[f % 2], (4, QT, 128), bf16, PARTS)
                for h in range(4):
                    for t in range(QT):
                        src = kst[0:T, NKV * t + h] if f == 0 else qst[0:T, NH * t + REP * (f - 1) + h]
                        last = tr(o[:, h, t, 0:T], src, identb[0:T, 0:T])
                last.then_inc(s["b_T_ps"], 1)

            def b_scores(b, g):
                pe.wait_ge(*((s["b_T_act"], b * 2 + 1 + g // 2) if g % 2 == 0 else (s["b_T_dve"], b * 3 + 2 + g // 2)))
                if g == 0:
                    pe.wait_ge(s["b_T_dve"], b * 3 + 1)
                for u, (t, k) in enumerate(BLOCKS):
                    if g > 0:
                        pe.wait_ge(s["b_s_max"], b * UNITS + 3 * (g - 1) + u + 1)
                    o = bank(RING[u], (REP, T), parts=T)
                    if t == k:
                        mm(flat(o), identb[0:T, 0:T], maskqb[0:T, :].unsqueeze(1).to_broadcast([T, REP, T]),
                           start=True, stop=False, skip_group_check=True)
                    for j in range(REP):
                        last = mm(o[:, j], QTs[0:PARTS, REP * g + j, T * t:T * (t + 1)], KTs[0:PARTS, g, T * k:T * (k + 1)],
                                  start=(t != k), stop=True, skip_group_check=True)
                    last.then_inc(s["b_s_ps"], 1)

            def b_transpose_max(b):
                pe.wait_ge(s["b_mx3"], b + 1)
                for t in range(QT):
                    last = tr(bank(B_T, (QT, 128), bf16)[0:6 * NH, t, 0:T], mx3[0:T, t], identb[0:T, 0:T])
                last.then_inc(s["b_mx3T_ps"], 1)

            def b_scores_shifted(b, g):
                if g == 0:
                    pe.wait_ge(s["b_D"], b + 1)
                for u, (t, k) in enumerate(BLOCKS):
                    if g > 0:
                        pe.wait_ge(s["b_exp"], b * UNITS + 3 * (g - 1) + u + 1)
                    o = bank(RING[u], (REP * T,), parts=T)
                    if t == k:
                        mm(o, identb[0:T, 0:T], maskkb[0:T, :].unsqueeze(1).to_broadcast([T, REP, T]),
                           start=True, stop=False)
                    mm(o, KTs[0:PARTS, g, T * k:T * (k + 1)], QTs[0:PARTS, REP * g:REP * (g + 1), T * t:T * (t + 1)],
                       start=(t != k), stop=False)
                    mm(o, selb[:, g], Dm[:, :, T * t:T * (t + 1)], start=False, stop=True).then_inc(s["b_st_ps"], 1)

            def b_weigh_values(b, g):
                pe.wait_ge(s["b_exp"], b * UNITS + 3 * g + 3)
                if g == 0:
                    pe.wait_ge(s["b_vz"], b + 1)
                for u, (t, k) in enumerate(BLOCKS):
                    last = mm(bank((B_T, B_U)[t], (REP * T,)), vz[0:T, k, g], PT[g % 2][0:T, u],
                              start=(g == 0 and k == 0), stop=(g == NKV - 1 and t == k))
                last.then_inc(s["b_pv_ps"], 1)

            def b_context_back(b):
                pe.wait_ge(s["b_CT_act"], b + 1)
                pe.wait_ge(s["b_CT_dve"], b + 1)
                for t in range(QT):
                    for j in range(REP):
                        last = tr(bank(RING[t], (REP, 128), parts=T)[:, j], CT[:, j, T * t:T * (t + 1)], ident)
                    last.then_inc(s["b_ct_ps"], 1)

            def b_transpose_context(b):
                pe.wait_ge(s["b_cx"], b + 1)
                for t in range(QT):
                    for c in range(DC):
                        last = tr(bank(RING[2], (DC, S))[:, c, T * t:T * (t + 1)], cx[0:T, t, 128 * c:128 * (c + 1)],
                                  ident[0:T, 0:T])
                last.then_inc(s["b_cxT_ps"], 1)

            def b_output(b):
                pe.wait_ge(s["b_cxT"], b + 1)
                for t in range(QT):
                    for c in range(DC):
                        last = mm(bank(B_T, (QT, D), parts=T)[:, t], cxT[:, c, T * t:T * (t + 1)], Wo[:, c],
                                  start=(c == 0), stop=(c == DC - 1))
                last.then_inc(s["b_o_ps"], 1)

            def b_transpose_hn(b):
                pe.wait_ge(s["b_hn"], b + 1)
                for t in range(QT):
                    for c in range(DC):
                        last = tr(bank(B_U, (DC, S))[:, c, T * t:T * (t + 1)], hn[0:T, t, 128 * c:128 * (c + 1)],
                                  ident[0:T, 0:T])
                last.then_inc(s["b_hnT_ps"], 1)

            def b_logits(b):
                pe.wait_ge(s["b_hnT"], b + 1)
                for t in range(QT):
                    for c in range(DC):
                        last = mm(bank(RING[0], (QT, NE), parts=T)[:, t], hnT[:, c, T * t:T * (t + 1)], Wr[:, c],
                                  start=(c == 0), stop=(c == DC - 1))
                last.then_inc(s["b_lg_ps"], 1)

            def b_count(b):
                pe.wait_ge(s["b_both"], b + 1)
                o = bank(RING[1], (3, NE), parts=T)
                mm(o[:, 0], beforeb[0:T, :], both[0:T, 0], start=True, stop=True)
                mm(o[:, 1], onesb[0:T, :], both[0:T, 0], start=True, stop=False)
                mm(o[:, 1], beforeb[0:T, :], both[0:T, 1], start=False, stop=True)
                mm(o[:, 2], onesb[0:T, :], both[0:T, 0], start=True, stop=False)
                mm(o[:, 2], onesb[0:T, :], both[0:T, 1], start=False, stop=True).then_inc(s["b_cnt_ps"], 1)

            def second(b, a=None):
                b_transpose(b)
                if a is not None:
                    a_transpose(a)
                b_project(b)
                if a is not None:
                    a_project(a)
                for f in range(1 + NKV):
                    b_transpose_stacks(b, f)
                    if f >= 1:
                        b_scores(b, f - 1)
                    if f == 2 and a is not None:
                        a_scores(a)
                if a is not None:
                    a_transpose_probs(a)
                b_transpose_max(b)
                b_scores_shifted(b, 0)
                b_scores_shifted(b, 1)
                if a is not None:
                    a_values(a)
                b_weigh_values(b, 0)
                b_scores_shifted(b, 2)
                b_weigh_values(b, 1)
                b_scores_shifted(b, 3)
                b_weigh_values(b, 2)
                b_weigh_values(b, 3)
                b_context_back(b)
                b_transpose_context(b)
                b_output(b)
                b_transpose_hn(b)
                b_logits(b)
                b_count(b)

            pe.wait_ge(s["setup_fold"], 1)
            pe.wait_ge(s["ld_ffn"], 16 * 5)
            a_transpose(0)
            a_project(0)
            a_scores(0)
            a_transpose_probs(0)
            a_values(0)
            with pe.Fori(0, B - 1) as i:
                second(i, i + 1)
            second(B - 1)

            G, U, XT, AT, Y = 0, 1, 2, (3, 5), 4

            def m_transpose_x(par, use):
                pe.wait_ge((s["m_x0"], s["m_x1"])[par], use * 16)
                for c in range(DC):
                    last = tr(bank(XT, (DC, 128))[:, c], xin[par][:, 128 * c:128 * (c + 1)], ident)
                last.then_inc((s["m_xT_ps0"], s["m_xT_ps1"])[par], 1)

            def m_up(i, e, which):
                if which == 0:
                    pe.wait_ge(s["m_xT"], i + 1)
                    pe.wait_ge(s["m_silu"], i)
                else:
                    pe.wait_ge(s["m_a"], i)
                for c in range(DC):
                    last = mm(bank((G, U)[which], (F,)), xTe[:, c],
                              flat(WGU[:, ds(e, 1), c, F * which:F * (which + 1)]), start=(c == 0), stop=(c == DC - 1))
                last.then_inc((s["m_g_ps"], s["m_u_ps"])[which], 1)

            def m_transpose_a(i, par):
                pe.wait_ge(s["m_a"], i + 1)
                for c in range(FC):
                    last = tr(bank(AT[c // 2], (2, 128))[:, c % 2], ga[par][:, 128 * c:128 * (c + 1)], ident)
                last.then_inc(s["m_aT_ps"], 1)

            def m_down(i, e):
                pe.wait_ge(s["m_aT_act"], i + 1)
                pe.wait_ge(s["m_aT_dve"], i + 1)
                pe.wait_ge(s["m_y"], i + 1)
                for c in range(FC):
                    last = mm(bank(Y, (D,)), gaT[:, c], flat(WD[:, ds(e, 1), c, :]), start=(c == 0), stop=(c == FC - 1))
                last.then_inc(s["m_y_ps"], 1)

            def expert(i):
                return pe.value_load(tile_e[0:1, ds(i, 1)], min_val=0, max_val=NE - 1)

            def m_step(i, par, more, use):
                e, before = expert(i), expert(i - 1)
                m_up(i, e, 0)
                m_transpose_a(i - 1, 1 - par)
                m_up(i, e, 1)
                if more:
                    m_transpose_x(1 - par, use)
                m_down(i - 1, before)

            pe.wait_ge(s["ld_wgu"], 16 * 2 * NE)
            pe.wait_ge(s["ld_wd"], 16 * NE)
            pe.wait_ge(s["m_maps"], 1)
            m_transpose_x(0, 1)
            e0 = expert(0)
            m_up(0, e0, 0)
            m_up(0, e0, 1)
            m_transpose_x(1, 1)
            with pe.Fori(0, (TILES - 2) // 2) as j:
                m_step(2 * j + 1, 1, True, j + 2)
                m_step(2 * j + 2, 0, True, j + 2)
            m_step(TILES - 1, 1, False, None)
            m_transpose_a(TILES - 1, 1)
            m_down(TILES - 1, expert(TILES - 1))

        @block.scalar
        def _(act):
            A = nc.scalar.activation
            def tok_copy_x(i, par):
                act.wait_ge(s["tok_xT_ps"], i + 1)
                A(xT[par][0:STACK, :].rearrange("p (q n) -> p q n", q=4), bank(0, (4, 128), bf16)[0:STACK, :, 0:T],
                  ACT.Copy).then_inc(s["tok_xT"], 1)

            def tok_silu(i, par):
                for m in range(MC):
                    act.wait_ge(s["tok_hid_ps"], i * 8 + (m + 1))
                    A(hid[par][:, m], bank(1 + m % 4, (4 * T,)), ACT.Silu).then_inc(s["tok_hid"], 1)

            tok_copy_x(0, 0)
            tok_silu(0, 0)
            with act.Fori(0, (NPAIR - 2) // 2) as j:
                for par in (1, 0):
                    i = 2 * j + 2 - par
                    tok_copy_x(i, par)
                    tok_silu(i, par)
            tok_copy_x(NPAIR - 1, 1)
            tok_silu(NPAIR - 1, 1)

            def a_copy_x(a):
                act.wait_ge(s["a_xnT_ps"], a + 1)
                A(flat(xnT), bank(A_T, (DC * S,)), ACT.Copy).then_inc(s["a_xnT"], 1)

            def a_bias(a):
                for w, (at, ready) in enumerate(((A_P, s["a_q_ps"]), (A_S, s["a_k_ps"]))):
                    act.wait_ge(ready, a + 1)
                    for o in range(DC):
                        last = A(qk[:, DC * w + o], bank(at, (DC, S))[:, o], ACT.Identity, bias=bqk[:, w, o:o + 1])
                last.then_inc(s["a_qk16"], 1)

            def a_exps(a):
                act.wait_ge(s["a_nmx"], a + 1)
                for t in range(QT):
                    last = A(ex[0:T, t], sq[0:T, t], ACT.Exp, bias=smA[0:T, t:t + 1], accum_out=smA[0:T, 2 + t:3 + t])
                last.then_inc(s["a_exp"], 1)

            def a_copy_probs(a):
                act.wait_ge(s["a_attT_ps"], a + 1)
                A(attT[0:T].rearrange("p k (t n) -> p (k t) n", t=QT), bank(A_S, (QT * QT, 128), f16, T)[:, :, 0:T],
                  ACT.Copy).then_inc(s["a_attT"], 1)

            def b_copy_y(b):
                act.wait_ge(s["b_yT_ps"], b + 1)
                A(flat(yT), bank(B_T, (DC * S,)), ACT.Copy).then_inc(s["b_yT"], 1)

            def b_squares(b, ready, done, at):
                act.wait_ge(ready, b + 1)
                for t in range(QT):
                    last = A(sqj[0:T, t, 0:D], y[0:T, t], ACT.Square, scale=float(D) ** -0.5,
                             accum_out=smB[0:T, at + t:at + t + 1])
                last.then_inc(done, 1)

            def b_scale_qkv(b):
                act.wait_ge(s["b_qkv_ps"], b + 1)
                act.wait_ge(s["b_r1"], b + 1)
                for t in range(QT):
                    last = A(qkv[0:T, t], bank(RING[t], (QKV,), parts=T), ACT.Copy, scale=smB[0:T, 2 + t:3 + t])
                last.then_inc(s["b_qkv"], 1)

            def b_copy_stack(b, f):
                act.wait_ge(s["b_T_ps"], b * 5 + (f + 1))
                A(QTs[0:PARTS, REP * (f - 1):REP * f].rearrange("p h (t n) -> p (h t) n", t=QT),
                  bank((B_T, B_U)[f % 2], (4 * QT, 128), bf16, PARTS)[:, :, 0:T], ACT.Copy).then_inc(s["b_T_act"], 1)

            def b_exps(b, g):
                if g >= 2:
                    act.wait_ge(s["b_pv_ps"], b * NKV + (g - 1))
                for u in range(3):
                    act.wait_ge(s["b_st_ps"], b * UNITS + (3 * g + u + 1))
                    A(PT[g % 2][0:T, u], bank(RING[u], (REP * T,), parts=T), ACT.Exp,
                      scale=float(HD) ** -0.5).then_inc(s["b_exp"], 1)

            def b_copy_context(b):
                act.wait_ge(s["b_pv_ps"], b * NKV + NKV)
                A(CT[:, :, 0:T], bank(B_T, (REP, T)), ACT.Copy).then_inc(s["b_CT_act"], 1)

            def b_copy_cx(b):
                act.wait_ge(s["b_cxT_ps"], b + 1)
                A(flat(cxT), bank(RING[2], (DC * S,)), ACT.Copy).then_inc(s["b_cxT"], 1)

            def b_copy_hn(b):
                act.wait_ge(s["b_hnT_ps"], b + 1)
                A(flat(hnT), bank(B_U, (DC * S,)), ACT.Copy).then_inc(s["b_hnT"], 1)

            def b_route_exp(b):
                act.wait_ge(s["b_lmx"], b + 1)
                A(prob[0:T], lgx[0:T], ACT.Exp).then_inc(s["b_lexp"], 1)

            def second(b, a=None):
                b_squares(b, s["b_y"], s["b_ms"], 0)
                b_copy_y(b)
                if a is not None:
                    a_copy_x(a)
                b_scale_qkv(b)
                if a is not None:
                    a_bias(a)
                b_copy_stack(b, 1)
                b_copy_stack(b, 3)
                if a is not None:
                    a_exps(a)
                    a_copy_probs(a)
                for g in range(NKV):
                    b_exps(b, g)
                b_copy_context(b)
                b_copy_cx(b)
                b_squares(b, s["b_h2"], s["b_ms2"], 4)
                b_copy_hn(b)
                b_route_exp(b)

            act.wait_ge(s["ld_vec"], 16 * 5)
            act.wait_ge(s["tok_h0"], NT // 2 + 1)
            act.wait_ge(s["tok_h1"], NT // 2 + 1)
            a_copy_x(0)
            a_bias(0)
            a_exps(0)
            a_copy_probs(0)
            with act.Fori(0, B - 1) as i:
                second(i, i + 1)
            second(B - 1)

            def m_silu(i):
                act.wait_ge(s["m_g_ps"], i + 1)
                act.wait_ge(s["m_a"], i)
                A(gs, bank(0, (F,)), ACT.Silu).then_inc(s["m_silu"], 1)

            def m_copy_a(i):
                act.wait_ge(s["m_aT_ps"], i + 1)
                A(gaT[:, 0:2], bank(3, (2, 128)), ACT.Copy).then_inc(s["m_aT_act"], 1)

            def m_out(i, par, use):
                act.wait_ge(s["m_y_ps"], i + 1)
                act.wait_ge((s["m_st0"], s["m_st1"])[par], use * 16 + 16)
                A(yo[par], bank(4, (D,)), ACT.Copy).then_inc(s["m_y"], 1)
                act.wait_ge(s["m_y"], i + 2)
                act.dma_start(y_rows[ds(128 * i, 128), :], yo[par]).then_inc((s["m_st0"], s["m_st1"])[par], 16)

            act.wait_ge(s["m_maps"], 1)
            m_silu(0)
            with act.Fori(0, (TILES - 2) // 2) as j:
                for par in (1, 0):
                    i = 2 * j + 2 - par
                    m_silu(i)
                    m_copy_a(i - 1)
                    m_out(i - 1, 1 - par, j if par == 1 else j)
            m_silu(TILES - 1)
            m_copy_a(TILES - 2)
            m_out(TILES - 2, 0, TILES // 2 - 1)
            m_copy_a(TILES - 1)
            m_out(TILES - 1, 1, TILES // 2 - 1)

        @block.vector
        def _(dve):
            V = nc.vector
            ch = Chain(dve, s["setup_dve"], 0, 8)
            V.memset(onesf[:], 1.0)
            V.memset(onesb[:], 1.0)
            V.memset(mhalf[:], -0.5)
            V.memset(epsc[:], EPS)
            V.memset(xst[:], 1.0)
            dve.wait_ge(s["ld_const"], 16)
            V.tensor_copy(identb[:], ident)
            V.tensor_copy(identh[:], ident)
            V.tensor_copy(maskqb[:], const_at("mask_q"))
            V.tensor_copy(maskkb[:], const_at("mask_k"))
            V.tensor_copy(beforeb[:], const_at("before"))
            V.tensor_copy(flat(selb), const_at("sel"))
            V.tensor_copy(run[:], const_at("ebase")).then_inc(s["setup_consts"], 1)
            dve.wait_ge(s["ld_tok"], 16 * 5)
            w0, d0 = raw0[0:TOK], sp_d[0:TOK]
            ch.link(V.tensor_copy(sp_h[0:TOK], w0))
            ch.link(V.tensor_tensor(d0, w0, sp_h[0:TOK], ALU.subtract))
            ch.link(V.tensor_copy(sp_m[0:TOK], d0))
            V.tensor_tensor(sp_l[0:TOK], d0, sp_m[0:TOK], ALU.subtract).then_inc(s["split_rows"], 1)
            dve.wait_ge(s["ld_bias"], 16 * 3)
            dve.wait_ge(s["csum_ps"], 1)
            for i, (a, n) in enumerate(((0, 512), (512, 512), (MID, D))):
                last = V.tensor_tensor(rsum[0:1, a:a + n], bank(i, (512,))[0:1, 0:n], rbias[0:1, a:a + n], ALU.add)
            ch.link(last)
            ch.link(V.tensor_tensor(rsum[0:1, MID:], rsum[0:1, MID:], rbias[0:1, MID + D:], ALU.add))
            r0, d1 = rsum[0:1], sp_d[0:1]
            ch.link(V.tensor_copy(rp_h[0:1], r0))
            ch.link(V.tensor_tensor(d1, r0, rp_h[0:1], ALU.subtract))
            ch.link(V.tensor_copy(rp_m[0:1], d1))
            ch.end()
            V.tensor_tensor(rp_l[0:1], d1, rp_m[0:1], ALU.subtract).then_inc(s["split_bias"], 1)
            dve.wait_ge(s["setup_wt_ps"], 1)
            for w in range(3):
                last = V.tensor_copy(Wat[:, :, D * w:D * (w + 1)], bank(3 + w, (DC, D)))
            last.then_inc(s["setup_wt"], 1)
            dve.wait_ge(s["ld_ffn"], 16 * 5)
            dve.wait_ge(s["ld_vec"], 16 * 5)
            for c in range(DC):
                last = V.tensor_scalar(Wqkv[:, c], Wqkv[:, c], lnc[:, c:c + 1], None, ALU.mult)
            last.then_inc(s["setup_fold"], 1)

            dve.wait_ge(s["ld_x"], 16)

            def tok_split(i):
                if not isinstance(i, int):
                    dve.wait_ge(s["tok_xT_ps"], i)
                elif i > 0:
                    dve.wait_ge(s["tok_xT_ps"], i)
                ch = Chain(dve, s["tok_dve"], i, 3)
                xi = X[0:T, ds(4 * i, 4), :]
                part = lambda n: xst[0:T, :, TOK * n:TOK * (n + 1)]
                ch.link(V.tensor_copy(part(0), xi))
                V.tensor_copy(part(1), part(0))
                V.tensor_copy(part(2), part(0))
                ch.link(V.tensor_tensor(xd[0:T], xi, part(0), ALU.subtract))
                ch.link(V.tensor_copy(part(3), xd[0:T]))
                ch.end()
                V.tensor_copy(part(4), part(3))
                V.tensor_tensor(part(5), xd[0:T], part(3), ALU.subtract).then_inc(s["tok_split"], 1)

            def tok_copy(i):
                for q in range(4):
                    dve.wait_ge(s["tok_out_ps"], i * 4 + (q + 1))
                    V.tensor_copy(tile_of(H, 4 * i + q), bank(5 + q % 2, (D,), parts=T)).then_inc((s["tok_h0"], s["tok_h1"])[q % 2], 1)

            tok_split(0)
            with dve.Fori(0, NPAIR - 1) as i:
                tok_split(i + 1)
                tok_copy(i)
            tok_copy(NPAIR - 1)

            def stats(ch, i, st, mv, sm, src, done):
                for t in range(QT):
                    last = V.bn_stats(st[0:T, t], tile_of(src, 2 * i + t))
                ch.link(last)
                V.memset(gate_v[:], 0.0)
                for t in range(QT):
                    last = V.bn_aggr(mv[0:T, t], st[0:T, t])
                ch.link(last)
                V.tensor_scalar(sm[0:T, 8:10], mv[0:T, :, 1], EPS, None, ALU.add).then_inc(done, 1)

            def normed(i, mv, sm, src, dst, done):
                for t in range(QT):
                    last = V.tensor_scalar(dst[0:T, t], tile_of(src, 2 * i + t), mv[0:T, t, 0:1], sm[0:T, 10 + t:11 + t],
                                           ALU.subtract, ALU.mult)
                last.then_inc(done, 1)

            def clip16(a):
                return V.tensor_scalar(a, a, F16MAX, -F16MAX, ALU.min, ALU.max)

            NA, NBL = 6, 35

            class StageA:
                def __init__(self, a):
                    self.a, self.ch = a, Chain(dve, s["a_dve"], a, NA)

                def stats(self):
                    stats(self.ch, self.a, stA, mvA, smA, H, s["a_var"])

                def norm(self):
                    dve.wait_ge(s["a_rstd"], self.a + 1)
                    normed(self.a, mvA, smA, H, xn, s["a_xn"])

                def values(self):
                    dve.wait_ge(s["a_v_ps"], self.a + 1)
                    self.ch.link(V.tensor_tensor(vq[0:T], bank(A_T, (QT, D), parts=T),
                                                 bv[0:T].unsqueeze(1).to_broadcast([T, QT, D]), ALU.add))
                    clip16(vq[0:T]).then_inc(s["a_v"], 1)

                def clip_qk(self):
                    dve.wait_ge(s["a_qk16"], self.a + 1)
                    clip16(flat(qk)).then_inc(s["a_qk"], 1)

                def quantize_scores(self):
                    dve.wait_ge(s["a_s_ps"], self.a + 1)
                    self.ch.link(V.tensor_scalar(flat(sq[0:T]), bank(A_P, (QT * S,), parts=T), float(D) ** -0.5, F16MAX,
                                                 ALU.mult, ALU.min))
                    self.ch.link(V.tensor_scalar(flat(sq[0:T]), flat(sq[0:T]), -F16MAX, None, ALU.max))
                    V.tensor_reduce(smA[0:T, 0:QT], sq[0:T], AX.X, ALU.max, negate=True).then_inc(s["a_nmx"], 1)

                def probs(self):
                    dve.wait_ge(s["a_exp"], self.a + 1)
                    self.ch.link(V.reciprocal(smA[0:T, 4:6], smA[0:T, 2:4]))
                    for t in range(QT):
                        last = V.tensor_scalar(att[0:T, t], ex[0:T, t], smA[0:T, 4 + t:5 + t], None, ALU.mult)
                    last.then_inc(s["a_att"], 1)

                def residual(self):
                    dve.wait_ge(s["a_av_ps"], self.a + 1)
                    h = H[0:T, ds(2 * self.a, QT), :]
                    V.tensor_tensor(h, h, bank(A_T, (QT, D), parts=T), ALU.add).then_inc(s["a_h1"], 1)
                    self.ch.end()

            class StageB:
                def __init__(self, b):
                    self.b, self.ch = b, Chain(dve, s["b_dve"], b, NBL)

                def stats(self):
                    dve.wait_ge(s["a_h1"], self.b + 1)
                    stats(self.ch, self.b, stB, mvB, smB, H, s["b_var"])

                def norm(self):
                    dve.wait_ge(s["b_rstd"], self.b + 1)
                    dve.wait_ge(s["b_h2_st"], self.b * 16 + 16)
                    normed(self.b, mvB, smB, H, y, s["b_y"])

                def rope(self):
                    b, ch = self.b, self.ch
                    dve.wait_ge(s["b_qkv"], b + 1)
                    heads = NH + NKV
                    hv = lambda a: a.rearrange("p t (h d) -> p t h d", d=HD)
                    cos = const_at("cos", T).rearrange("p (t d) -> p t d", t=QT).unsqueeze(2).to_broadcast([T, QT, heads, HD])
                    ch.link(V.tensor_tensor(hv(t1[0:T]), hv(qkv[0:T, :, 0:heads * HD]), cos, ALU.mult))
                    dve.wait_ge(s["b_sinpart"], b + 1)
                    two = lambda a: a.rearrange("p (t h) d -> p t (h d)", t=QT)
                    V.tensor_tensor(two(rok[0:T]), t1[0:T, :, NH * HD:], t2[0:T, :, NH * HD:], ALU.add)
                    ch.link(V.tensor_tensor(two(roq[0:T]), t1[0:T, :, 0:NH * HD], t2[0:T, :, 0:NH * HD], ALU.add))
                    Q = lambda n, m=1: qst[0:T, :, HD * n:HD * (n + m)]
                    K = lambda n, m=1: kst[0:T, :, HD * n:HD * (n + m)]
                    V.tensor_copy(Q(0), roq[0:T])
                    ch.link(V.tensor_copy(K(0), rok[0:T]))
                    V.tensor_tensor(dk[0:T], rok[0:T], K(0), ALU.subtract)
                    V.tensor_tensor(dq[0:T], roq[0:T], Q(0), ALU.subtract)
                    V.tensor_copy(Q(1), Q(0))
                    ch.link(V.tensor_copy(Q(2), Q(0)))
                    V.tensor_copy(K(1), dk[0:T])
                    ch.link(V.tensor_copy(Q(3), dq[0:T]))
                    V.tensor_tensor(K(2), dk[0:T], K(1), ALU.subtract)
                    V.tensor_tensor(Q(5), dq[0:T], Q(3), ALU.subtract)
                    V.tensor_copy(Q(4), Q(3))
                    V.tensor_copy(K(3, 2), K(0, 2))
                    V.tensor_copy(K(5), K(0)).then_inc(s["b_stacks"], 1)

                def copy_stack(self, f):
                    dve.wait_ge(s["b_T_ps"], self.b * 5 + (f + 1))
                    dst = KTs[0:PARTS] if f == 0 else QTs[0:PARTS, REP * (f - 1):REP * f]
                    V.tensor_copy(dst.rearrange("p h (t n) -> p (h t) n", t=QT),
                                  bank((B_T, B_U)[f % 2], (4 * QT, 128), bf16, PARTS)[:, :, 0:T]).then_inc(s["b_T_dve"], 1)

                def maxima(self, g):
                    for u in range(3):
                        dve.wait_ge(s["b_s_ps"], self.b * UNITS + (3 * g + u + 1))
                        V.tensor_reduce(mxu[0:T, u, REP * g:REP * (g + 1)], bank(RING[u], (REP, T), parts=T), AX.X,
                                        ALU.max).then_inc(s["b_s_max"], 1)

                def negate_split_max(self):
                    b, ch = self.b, self.ch
                    dve.wait_ge(s["b_s_max"], b * UNITS + UNITS)
                    ch.link(V.tensor_tensor(mxu[0:T, 1], mxu[0:T, 1], mxu[0:T, 2], ALU.max))
                    part = lambda n: mx3[0:T, :, NH * n:NH * (n + 1)]
                    ch.link(V.tensor_scalar(nmx[0:T], mxu[0:T, 0:2], -1.0, None, ALU.mult))
                    ch.link(V.tensor_copy(part(0), nmx[0:T]))
                    ch.link(V.tensor_tensor(dmx[0:T], nmx[0:T], part(0), ALU.subtract))
                    ch.link(V.tensor_copy(part(1), dmx[0:T]))
                    V.tensor_tensor(part(2), dmx[0:T], part(1), ALU.subtract).then_inc(s["b_mx3"], 1)

                def spread_max(self):
                    dve.wait_ge(s["b_mx3T_ps"], self.b + 1)
                    n = 3 * NH
                    src = bank(B_T, (QT, 128), bf16)[0:n, :, 0:T].unsqueeze(1).to_broadcast([n, REP, QT, T])
                    which = const_at("delta", n).unsqueeze(2).unsqueeze(3).to_broadcast([n, REP, QT, T])
                    V.tensor_tensor(Dm[0:n].rearrange("p j (t n) -> p j t n", t=QT), src, which,
                                    ALU.mult).then_inc(s["b_D"], 1)

                def copy_context(self):
                    dve.wait_ge(s["b_pv_ps"], self.b * NKV + NKV)
                    V.tensor_copy(CT[:, :, T:S], bank(B_U, (REP, T))).then_inc(s["b_CT_dve"], 1)

                def divide_context(self):
                    b, ch = self.b, self.ch
                    for t in range(QT):
                        dve.wait_ge(s["b_ct_ps"], b * QT + (t + 1))
                        src = bank(RING[t], (REP, NKV, 32), parts=T)
                        rc = rcx[0:T, t].rearrange("p (j g) -> p j g", j=REP)
                        ch.link(V.reciprocal(rc, src[:, :, :, HD]))
                        last = V.tensor_tensor(cx[0:T, t].rearrange("p (g j d) -> p j g d", g=NKV, j=REP),
                                               src[:, :, :, 0:HD], rc.unsqueeze(3).to_broadcast([T, REP, NKV, HD]), ALU.mult)
                    last.then_inc(s["b_cx"], 1)

                def residual(self):
                    dve.wait_ge(s["b_o_ps"], self.b + 1)
                    self.ch.link(V.tensor_tensor(y[0:T], y[0:T], bank(B_T, (QT, D), parts=T), ALU.add))
                    V.tensor_scalar(y[0:T], y[0:T], CLIP, -CLIP, ALU.min, ALU.max).then_inc(s["b_h2"], 1)

                def second_norm(self):
                    dve.wait_ge(s["b_r2"], self.b + 1)
                    dve.wait_ge(s["b_hn_free"], self.b + 1)
                    for t in range(QT):
                        last = V.scalar_tensor_tensor(hn[0:T, t], y[0:T, t], smB[0:T, 6 + t:7 + t], w2b[0:T],
                                                      ALU.mult, ALU.mult)
                    last.then_inc(s["b_hn"], 1)

                def route(self):
                    b, ch = self.b, self.ch
                    over_e = lambda a: a[0:T].unsqueeze(2).to_broadcast([T, QT, NE])
                    over_t = lambda a: a.unsqueeze(1).to_broadcast([T, QT, NE])
                    rev = over_t(const_at("rev", T))
                    lg = bank(RING[0], (QT, NE), parts=T)
                    dve.wait_ge(s["b_lg_ps"], b + 1)
                    ch.link(V.tensor_reduce(rmax[0:T], lg, AX.X, ALU.max))
                    V.tensor_tensor(lgx[0:T], lg, over_e(rmax), ALU.subtract).then_inc(s["b_lmx"], 1)
                    dve.wait_ge(s["b_lexp"], b + 1)
                    ch.link(V.tensor_reduce(rsm[0:T], prob[0:T], AX.X, ALU.add))
                    ch.link(V.reciprocal(rinv[0:T], rsm[0:T]))
                    ch.link(V.tensor_tensor(prob[0:T], prob[0:T], over_e(rinv), ALU.mult))

                    def best(p, top, one):
                        ch.link(V.tensor_reduce(top[0:T], p[0:T], AX.X, ALU.max))
                        ch.link(V.tensor_tensor(hit[0:T], p[0:T], over_e(top), ALU.is_equal))
                        ch.link(V.tensor_tensor(cand[0:T], hit[0:T], rev, ALU.mult))
                        ch.link(V.tensor_reduce(first[0:T], cand[0:T], AX.X, ALU.max))
                        ch.link(V.tensor_tensor(one[0:T], rev, over_e(first), ALU.is_equal))

                    best(prob, top1, one1)
                    ch.link(V.scalar_tensor_tensor(rest[0:T], one1[0:T], -2.0, prob[0:T], ALU.mult, ALU.add))
                    best(rest, top2, one2)
                    V.tensor_tensor(both[0:T], one1[0:T], one2[0:T], ALU.add).then_inc(s["b_both"], 1)
                    ch.link(V.tensor_tensor(topsum[0:T], top1[0:T], top2[0:T], ALU.add))
                    ch.link(V.reciprocal(topsum[0:T], topsum[0:T]))
                    V.tensor_tensor(wtop[0:T, ds(2 * b, QT), 0], top1[0:T], topsum[0:T], ALU.mult)
                    V.tensor_tensor(wtop[0:T, ds(2 * b, QT), 1], top2[0:T], topsum[0:T], ALU.mult)
                    cn = bank(RING[1], (3, NE), parts=T)
                    dve.wait_ge(s["b_cnt_ps"], b + 1)
                    ch.link(V.tensor_tensor(posn[0:T], cn[:, 0:2], over_t(run[0:T]), ALU.add))
                    V.tensor_tensor(run[0:T], run[0:T], cn[:, 2], ALU.add)
                    V.tensor_tensor(one1[0:T], one1[0:T], posn[0:T], ALU.mult)
                    ch.link(V.tensor_tensor(one2[0:T], one2[0:T], posn[0:T], ALU.mult))
                    V.tensor_reduce(dsum[0:T, 0], one1[0:T], AX.X, ALU.add)
                    ch.link(V.tensor_reduce(dsum[0:T, 1], one2[0:T], AX.X, ALU.add))
                    V.tensor_copy(dest[0:T, :, ds(2 * b, QT)], dsum[0:T])
                    V.tensor_copy(dnow[0:T], dsum[0:T]).then_inc(s["b_dest"], 1)
                    ch.end()

            def second(b, a=None):
                B2 = StageB(b)
                A2 = StageA(a) if a is not None else None
                B2.stats()
                if A2:
                    A2.stats()
                B2.norm()
                if A2:
                    A2.norm()
                B2.rope()
                if A2:
                    A2.clip_qk()
                B2.copy_stack(0)
                if A2:
                    A2.values()
                B2.copy_stack(2)
                B2.maxima(0)
                if A2:
                    A2.quantize_scores()
                B2.maxima(1)
                B2.copy_stack(4)
                B2.maxima(2)
                if A2:
                    A2.probs()
                B2.maxima(3)
                B2.negate_split_max()
                B2.spread_max()
                if A2:
                    A2.residual()
                B2.copy_context()
                B2.divide_context()
                B2.residual()
                B2.second_norm()
                B2.route()

            dve.wait_ge(s["tok_h0"], NT // 2 + 1)
            dve.wait_ge(s["tok_h1"], NT // 2 + 1)
            V.memset(flat(Dm), 0.0)
            V.memset(flat(mx3), 0.0)
            A0 = StageA(0)
            A0.stats()
            A0.norm()
            A0.clip_qk()
            A0.values()
            A0.quantize_scores()
            A0.probs()
            A0.residual()
            with dve.Fori(0, B - 1) as i:
                second(i, i + 1)
            second(B - 1)

            ch = Chain(dve, s["m_dve"], 0, 30)
            V.memset(zer, 0.0).then_inc(s["m_zero"], 1)
            V.memset(ones8[0:T], 1.0)
            ch.link(V.tensor_tensor(cnt[0:T], run[0:T], const_at("ebase", T), ALU.subtract))
            V.tensor_copy(counts[0:1], cnt[0:1])
            ch.link(V.tensor_scalar(cnt_i[0:T], cnt[0:T], 127.0, None, ALU.add))
            ch.link(V.tensor_scalar(cnt_i[0:T], cnt_i[0:T], 7, None, ALU.arith_shift_right))
            ch.link(V.tensor_copy(ntil[0:T], cnt_i[0:T]))
            ch.link(V.tensor_tensor_scan(mend[0:T], ones8[0:T], ntil[0:T], 0.0, ALU.mult, ALU.add))
            tl = const_at("tile", 1)
            by_tile = tl.unsqueeze(2).to_broadcast([1, TILES, NE])
            by_e = lambda a: a[0:1].unsqueeze(1).to_broadcast([1, TILES, NE])
            ch.link(V.tensor_tensor(over[0:1], by_tile, by_e(mend), ALU.is_ge))
            ch.link(V.tensor_reduce(m_e[0:1], over[0:1], AX.X, ALU.add))
            ch.link(V.tensor_tensor(over2[0:1], over[0:1], by_e(ntil), ALU.mult))
            ch.link(V.tensor_reduce(m_st[0:1], over2[0:1], AX.X, ALU.add))
            V.tensor_scalar(tile_e[:], m_e[0:1], NE - 1.0, None, ALU.min)
            V.tensor_scalar(m_ok[0:1], m_e[0:1], NE - 0.5, None, ALU.is_lt)
            ch.link(V.tensor_tensor(m_st[0:1], tl, m_st[0:1], ALU.subtract))
            ch.link(V.tensor_scalar(m_e[0:1], m_e[0:1], float(REGION), None, ALU.mult))
            ch.link(V.scalar_tensor_tensor(m_row[0:1], m_st[0:1], 128.0, m_e[0:1], ALU.mult, ALU.add))
            ch.link(V.tensor_tensor(m_row[0:1], m_row[0:1], m_ok[0:1], ALU.mult))
            V.tensor_copy(tile_in[:], m_row[0:1]).then_inc(s["m_maps"], 1)

            def result_rows():
                nd = 2 * NT
                d = dest[0:T].rearrange("p k t -> p (k t)")
                ch.link(V.tensor_tensor(shift[0:T], mend[0:T], ntil[0:T], ALU.subtract))
                ch.link(V.scalar_tensor_tensor(shift[0:T], shift[0:T], 128.0, const_at("ebase", T), ALU.mult, ALU.subtract))
                V.tensor_copy(destf[0:T], d)
                V.tensor_copy(acc[0:T], d)
                ch.link(V.tensor_tensor(dshift[0:T, 1:NE], shift[0:T, 1:NE], shift[0:T, 0:NE - 1], ALU.subtract))
                for e in range(1, NE):
                    ch.link(V.tensor_scalar(term[0:T], destf[0:T], float(e * REGION), dshift[0:T, e:e + 1],
                                            ALU.is_ge, ALU.mult))
                    ch.link(V.tensor_tensor(acc[0:T], acc[0:T], term[0:T], ALU.add))
                V.tensor_copy(d, acc[0:T]).then_inc(s["m_dest"], 1)
                ch.end()

            def m_copy_x(par, use, i):
                dve.wait_ge((s["m_xT_ps0"], s["m_xT_ps1"])[par], use + 1)
                V.tensor_copy(flat(xTe), bank(2, (DC * 128,))).then_inc(s["m_xT"], 1)

            def m_gate(i, par):
                dve.wait_ge(s["m_silu"], i + 1)
                dve.wait_ge(s["m_u_ps"], i + 1)
                V.tensor_tensor(ga[par], gs, bank(1, (F,)), ALU.mult).then_inc(s["m_a"], 1)

            def m_copy_a(i):
                dve.wait_ge(s["m_aT_ps"], i + 1)
                V.tensor_copy(gaT[:, 2:4], bank(5, (2, 128))).then_inc(s["m_aT_dve"], 1)

            m_copy_x(0, 1, 0)
            m_gate(0, 0)
            m_copy_x(1, 1, 1)
            result_rows()
            with dve.Fori(0, (TILES - 2) // 2) as j:
                for par in (1, 0):
                    i = 2 * j + 2 - par
                    m_copy_a(i - 1)
                    m_gate(i, par)
                    m_copy_x(1 - par, j + 2, i + 1)
            m_copy_a(TILES - 2)
            m_gate(TILES - 1, 1)
            m_copy_a(TILES - 1)

            with dve.Fori(0, B // 2) as j:
                for par, (landed, got) in enumerate(((s["f_h0"], s["f_y0"]), (s["f_h1"], s["f_y1"]))):
                    i = 2 * j + par
                    ch = Chain(dve, s["f_dve"], i, 3)
                    w = wnow[par]
                    V.tensor_copy(w[0:T], wtop[0:T, ds(2 * i, QT), :]).then_inc(s["f_w"], 1)
                    dve.wait_ge(s["f_w"], i + 1)
                    dve.wait_ge(landed, j * 16 + 16)
                    dve.wait_ge(got, j * (16 * 2 * QT) + 16 * 2 * QT)
                    h = h2b[par]
                    for t in range(QT):
                        last = V.scalar_tensor_tensor(y1[par][0:T, t], y1[par][0:T, t], w[0:T, t, 0:1], h[0:T, t],
                                                      ALU.mult, ALU.add)
                    ch.link(last)
                    for t in range(QT):
                        last = V.scalar_tensor_tensor(h[0:T, t], y2[par][0:T, t], w[0:T, t, 1:2], y1[par][0:T, t],
                                                      ALU.mult, ALU.add)
                    ch.link(last)
                    ch.link(V.tensor_scalar(h[0:T], h[0:T], CLIP, -CLIP, ALU.min, ALU.max))
                    V.tensor_tensor(h[0:T], h[0:T], H[0:T, ds(2 * i, QT), :], ALU.add).then_inc(s["f_out"], 1)
                    ch.end()

        @block.gpsimd
        def _(po):
            P = nc.gpsimd
            half_ = mhalf[0:T]

            def take_wait():
                P.tensor_tensor(gate_p[:], mhalf[0:1, 0:1], mhalf[0:1, 0:1], ALU.add)

            def rstd(i, ready, sm, at, to, done):
                po.wait_ge(ready, i + 1)
                P.tensor_tensor(sm[0:T, to:to + 2], sm[0:T, at:at + 2], half_, ALU.pow).then_inc(done, 1)

            def rms(i, ready, at, to, done, k):
                po.wait_ge(ready, i + 1)
                P.tensor_tensor(smB[0:T, 12:14], smB[0:T, at:at + 2], epsc[0:T], ALU.add).then_inc(s["b_pool"], 1)
                po.wait_ge(s["b_pool"], i * 2 + k)
                P.tensor_tensor(smB[0:T, to:to + 2], smB[0:T, 12:14], half_, ALU.pow).then_inc(done, 1)

            def values(b):
                for g in range(NKV):
                    last = P.tensor_copy(vz[0:T, :, g, 32 * g:32 * g + HD],
                                         qkv[0:T, :, (NH + NKV + g) * HD:(NH + NKV + g + 1) * HD])
                last.then_inc(s["b_vz"], 1)

            def rope_sin(b):
                po.wait_ge(s["b_qkv"], b + 1)
                heads, hh = NH + NKV, HD // 2
                src = qkv[0:T, :, 0:heads * HD].rearrange("p t (h d) -> p t h d", d=HD)
                dst = t2[0:T].rearrange("p t (h d) -> p t h d", d=HD)
                sin = const_at("sin", T).rearrange("p (t d) -> p t d", t=QT)
                for lo, hi in ((0, hh), (hh, 0)):
                    tab = sin[:, :, lo:lo + hh].unsqueeze(2).to_broadcast([T, QT, heads, hh])
                    last = P.tensor_tensor(dst[:, :, :, lo:lo + hh], src[:, :, :, hi:hi + hh], tab, ALU.mult)
                last.then_inc(s["b_sinpart"], 1)

            def scatter(b):
                po.wait_ge(s["b_dest"], b + 1)
                take_wait()
                for k in range(TOPK):
                    for t in range(QT):
                        P.indirect_dma_start(out=x_rows, out_offset=bass.IndirectOffsetOnAxis(ap=dnow[0:T, k, t:t + 1], axis=0),
                                             in_=hn[0:T, t], in_offset=None).then_inc(s["b_scat"], 16)

            def second(b, a=None):
                rstd(b, s["b_var"], smB, 8, 10, s["b_rstd"])
                if a is not None:
                    rstd(a, s["a_var"], smA, 8, 10, s["a_rstd"])
                rms(b, s["b_ms"], 0, 2, s["b_r1"], 1)
                rope_sin(b)
                values(b)
                rms(b, s["b_ms2"], 4, 6, s["b_r2"], 2)
                scatter(b)

            po.wait_ge(s["tok_h0"], NT // 2 + 1)
            po.wait_ge(s["tok_h1"], NT // 2 + 1)
            P.memset(vz[0:T], 0.0).then_inc(s["zeroed"], 1)
            po.wait_ge(s["zeroed"], 1)
            for g in range(NKV):
                P.memset(vz[0:T, :, g, 32 * g + HD:32 * g + HD + 1], 1.0)
            rstd(0, s["a_var"], smA, 8, 10, s["a_rstd"])
            with po.Fori(0, B - 1) as i:
                second(i, i + 1)
            second(B - 1)

            po.wait_ge(s["m_dest"], 1)
            po.wait_ge(s["m_st0"], 16 * (TILES // 2 + 1))
            po.wait_ge(s["m_st1"], 16 * (TILES // 2 + 1))
            with po.Fori(0, B // 2) as j:
                for par, got in enumerate((s["f_y0"], s["f_y1"])):
                    i = 2 * j + par
                    po.wait_ge((s["f_st0"], s["f_st1"])[par], j * 16 + 16)
                    P.tensor_copy(gidx[par][0:T], dest[0:T, :, ds(2 * i, QT)]).then_inc(s["f_idx"], 1)
                    po.wait_ge(s["f_idx"], i + 1)
                    take_wait()
                    for k, y_ in enumerate((y1, y2)):
                        for t in range(QT):
                            P.indirect_dma_start(out=y_[par][0:T, t], out_offset=None, in_=y_rows,
                                                 in_offset=bass.IndirectOffsetOnAxis(ap=gidx[par][0:T, k, t:t + 1], axis=0)
                                                 ).then_inc(got, 16)


_INS = ["x", "L0_tok_W_h", "L0_tok_b_h", "L0_tok_W_o", "L0_tok_b_o", "L0_tok_W_r", "L0_tok_b_r", "L0_attn_Wq",
        "L0_attn_bq", "L0_attn_Wk", "L0_attn_bk", "L0_attn_Wv", "L0_attn_bv", "L0_ffn_ln1_w", "L0_ffn_ln2_w",
        "L0_ffn_Wq", "L0_ffn_Wk", "L0_ffn_Wv", "L0_ffn_Wo", "L0_ffn_Wr", "L0_ffn_Wg", "L0_ffn_Wu", "L0_ffn_Wd"]


def kernel(**inputs):
    import concourse.bacc as _bacc
    from concourse.bass_utils import run_bass_kernel_spmd as _run

    nc = _bacc.Bacc("TRN2", target_bir_lowering=False, num_devices=1)
    arrays, args = {}, []
    for name in _INS:
        a = np.ascontiguousarray(inputs[name])
        arrays[f"in_{name}"] = a
        args.append(nc.dram_tensor(f"in_{name}", a.shape, mybir.dt.from_np(a.dtype), kind="ExternalInput").ap())
    table, _ = constants()
    arrays["in_const"] = table
    args.append(nc.dram_tensor("in_const", table.shape, mybir.dt.float32, kind="ExternalInput").ap())
    args.append(nc.dram_tensor("out", (B, S, D), mybir.dt.float32, kind="ExternalOutput").ap())
    build(nc, *args)
    r = _run(nc, [arrays], core_ids=[0])
    return r.results[0]["out"]
```

```python
from contextlib import ExitStack

import numpy as np

import concourse.bass as bass
from concourse import mybir

B, SAMPLES, TOK = 16, 4000, 16
S = SAMPLES // TOK
QT = 2
T = S // QT
NT = B * QT
D, MID = 256, 1024
DC, MC = D // 128, MID // 128
NH, NKV, HD = 16, 4, 16
REP = NH // NKV
NE, F, TOPK = 8, 512, 2
FC = F // 128
PARTS = 6 * HD
STACK = PARTS + 3
QKV = (NH + 2 * NKV) * HD
EPS = 1e-5
CLIP = 100.0
F16MAX = 65504.0
NEG = -1e30

REGION = -(-(B * S + 128) // 128) * 128
TILES = (B * S * TOPK + NE * 127) // 128


def constants():
    t = {}
    p = np.arange(128)
    t["ident"] = np.eye(128)
    k = np.arange(T)
    t["mask_q"] = np.where(k[None, :] > p[:, None], NEG, 0.0)
    t["mask_k"] = np.where(k[None, :] < p[:, None], NEG, 0.0)
    t["before"] = (p[:, None] < k[None, :]).astype(float)
    pos = np.arange(S, dtype=np.float32)
    inv = (1.0 / np.float32(10000.0) ** (np.arange(0, HD, 2, dtype=np.float32) / np.float32(HD))).astype(np.float32)
    ang = pos[:, None] * inv
    cos, sin = np.cos(ang).astype(np.float32), np.sin(ang).astype(np.float32)
    for name, tab in (("cos", np.concatenate([cos, cos], 1)), ("sin", np.concatenate([-sin, sin], 1))):
        full = np.zeros((128, QT, HD), np.float32)
        full[:T] = tab.reshape(QT, T, HD).transpose(1, 0, 2)
        t[name] = full.reshape(128, -1)
    t["rev"] = np.tile(NE - np.arange(NE), (128, 1))
    t["ebase"] = np.tile(np.arange(NE) * REGION, (128, 1))
    row = p[:, None]
    head = row % NH
    real = row < 3 * NH
    t["delta"] = (real & (head % REP == np.arange(REP)[None, :])).astype(float)
    sel = real[:, :, None] & (head[:, :, None] // REP == np.arange(NKV)[None, :, None])
    t["sel"] = np.broadcast_to(sel, (128, NKV, T)).astype(float).reshape(128, -1)
    t["tile"] = np.tile(np.arange(TILES), (128, 1))
    where, cols, at = {}, [], 0
    for name, a in t.items():
        where[name] = (at, a.shape[1])
        cols.append(a.astype(np.float32))
        at += a.shape[1]
    return np.ascontiguousarray(np.concatenate(cols, 1)), where


def build(nc, x, tWh, tbh, tWo, tbo, tWr, tbr, aWq, abq, aWk, abk, aWv, abv, ln1, ln2, fWq, fWk, fWv, fWo,
          fWr, fWg, fWu, fWd, const, out):
    f32, f16, bf16 = mybir.dt.float32, mybir.dt.float16, mybir.dt.bfloat16
    i32 = mybir.dt.int32
    ALU, ACT, AX = mybir.AluOpType, mybir.ActivationFunctionType, mybir.AxisListType
    ds = bass.ds
    _, CO = constants()
    NC = const.shape[1]

    ctx = ExitStack()
    with ctx:
        def sb(name, shape, dt):
            return ctx.enter_context(nc.sbuf_tensor(name, shape, dt))

        def sem(name):
            return ctx.enter_context(nc.semaphore(name))

        x_rows = nc.dram_tensor("x_rows", (NE * REGION, D), f32, kind="Internal").ap()
        y_rows = nc.dram_tensor("y_rows", (TILES * 128, D), f32, kind="Internal").ap()
        h2_rows = nc.dram_tensor("h2_rows", (B, T, QT, D), f32, kind="Internal").ap()

        WGU = sb("WGU", [128, NE, DC, 2 * F], f32)
        H = sb("H", [128, NT, D], f32)
        C = sb("C", [128, NC], f32)
        Wat = sb("Wat", [128, DC, 3 * D], f32)
        Wqkv = sb("Wqkv", [128, DC, QKV], f32)
        Wo = sb("Wo", [128, DC, D], f32)
        Wr = sb("Wr", [128, DC, NE], f32)
        bqk = sb("bqk", [128, 2, DC], f32)
        bv = sb("bv", [128, D], f32)
        w2b = sb("w2b", [128, D], f32)
        lnc = sb("lnc", [128, DC], f32)
        identb = sb("identb", [128, 128], bf16)
        identh = sb("identh", [128, 128], f16)
        maskqb = sb("maskqb", [128, T], bf16)
        maskkb = sb("maskkb", [128, T], bf16)
        beforeb = sb("beforeb", [128, T], bf16)
        onesb = sb("onesb", [128, T], bf16)
        selb = sb("selb", [128, NKV, T], bf16)
        onesf = sb("onesf", [128, 1], f32)
        mhalf = sb("mhalf", [128, 2], f32)
        epsc = sb("epsc", [128, 2], f32)
        gate_v = sb("gate_v", [1, 1], f32)
        gate_p = sb("gate_p", [1, 4], f32)
        wtop = sb("wtop", [128, NT, 2], f32)
        dest = sb("dest", [128, 2, NT], i32)
        run = sb("run", [128, NE], f32)
        counts = sb("counts", [128, NE], i32)
        tile_e = sb("tile_e", [1, TILES], i32)
        tile_in = sb("tile_in", [1, TILES], i32)

        def const_at(name, parts=128):
            a, n = CO[name]
            return C[0:parts, a:a + n]

        ident = const_at("ident")

        WDW = NE * FC * D
        EARLY = 4
        POOL = 14900 + WDW
        pool = sb("pool", [128, POOL], f32)
        WD = pool[:, 0:WDW].rearrange("p (e c d) -> p e c d", e=NE, c=FC)

        class Carve:

            def __init__(self, at=0):
                self.at = at

            def __call__(self, shape, dt=f32):
                n = int(np.prod(shape))
                words = n if dt in (f32, i32) else (n + 1) // 2
                words += words % 2
                a = pool[:, self.at:self.at + words]
                self.at += words
                assert self.at <= POOL, self.at
                if dt != f32:
                    a = a.bitcast(dt)
                a = a[:, 0:n]
                if len(shape) == 2:
                    a = a.rearrange("p (a b) -> p a b", a=shape[0])
                elif len(shape) == 3:
                    a = a.rearrange("p (a b c) -> p a b c", a=shape[0], b=shape[1])
                return a

        c1 = Carve()
        hid = [c1((MC, 4 * T)) for _ in range(2)]
        WoT = c1((MC, D))
        Wst = c1((MID + D,), bf16)
        X = c1((NT, TOK))
        xst = c1((4, 128), bf16)
        xd = c1((4, TOK))
        xT = [c1((4 * T,), bf16) for _ in range(2)]
        Hf = H[:, :, :].rearrange("p t d -> p (t d)")
        rawW = Hf[:, 0:3 * DC * D].rearrange("p (w c h) -> p w c h", w=3, c=DC)
        raw0 = Hf[:, 2048:2048 + MID + D]
        raw1 = Hf[:, 3584:3584 + MID + D]
        rsum = Hf[:, 5120:5120 + MID + D]
        rbias = Hf[:, 6400:6400 + MID + 2 * D]
        WDf = pool[:, c1.at:]
        half = (MID + D) // 2
        sp_h, sp_m, sp_l, rp_h, rp_m, rp_l = (WDf[:, half * i:half * (i + 1)].bitcast(bf16) for i in range(6))
        sp_d = WDf[:, 6 * half:8 * half]
        c2 = Carve(EARLY * FC * D)
        ca = Carve(c2.at)
        xn = c2((QT, D))
        att = ca((QT, S), f16)
        attT = ca((QT, S), f16)
        xnT = c2((DC, S))
        qk = c2((2 * DC, S), f16)
        vq = c2((QT, D), f16)
        sq = c2((QT, S), f16)
        ex = c2((QT, S))
        stA = c2((QT, 6))
        mvA = c2((QT, 2))
        smA = c2((16,))
        y = c2((QT, D))
        yT = c2((DC, S))
        qkv = c2((QT, QKV))
        cx = c2((QT, D))
        cxT = c2((DC, S))
        hnT = cxT
        h2 = c2((QT, D))
        vz = c2((QT, NKV, 128))
        qst = c2((QT * NH, PARTS), bf16)
        kst = c2((QT * NKV, PARTS), bf16)
        QTs = c2((NH, S), bf16)
        CT = c2((REP, S))
        KTs = c2((NKV, S), bf16)
        Dm = c2((REP, S), bf16)
        PT = [c2((3, REP * T)) for _ in range(2)]
        t1 = c2((QT, (NH + NKV) * HD))
        t2 = c2((QT, (NH + NKV) * HD))
        roq, rok = c2((QT * NH, HD)), c2((QT * NKV, HD))
        dq = roq
        dk = rok
        sqb, sqc = t1, cx
        hn = c2((QT, D))
        stB = c2((QT, 6))
        mvB = c2((QT, 2))
        smB = c2((16,))
        smC = c2((16,))
        meanB = c2((NT,))
        rstdB = c2((NT,))
        mxu = c2((3, NH))
        nmx = c2((QT, NH))
        dmx = c2((QT, NH))
        mx3 = c2((QT, 6 * NH), bf16)
        rcx = c2((QT, NH))
        lgx, prob, hit, cand, one1, one2, rest, posn = (c2((QT, NE)) for _ in range(8))
        rmax, rsm, rinv, top1, top2, first, topsum = (c2((QT,)) for _ in range(7))
        both = c2((QT, NE), bf16)
        dsum = c2((2, QT))
        dnow = c2((2, QT), i32)
        c4 = Carve(WDW)
        xin = [c4((D,)) for _ in range(2)]
        xTe = c4((DC, 128))
        gs = c4((F,))
        ga = [c4((F,)) for _ in range(2)]
        gaT = c4((FC, 128))
        yo = [c4((D,)) for _ in range(2)]
        zer = c4((D,))
        over = c4((TILES, NE))
        over2 = c4((TILES, NE))
        m_e, m_st, m_ok, m_row = (c4((TILES,)) for _ in range(4))
        cnt, ntil, mend, ones8, shift, dshift = (c4((NE,)) for _ in range(6))
        destf, acc, term = (c4((2 * NT,)) for _ in range(3))
        cnt_i = c4((NE,), i32)
        c5 = Carve(c4.at)
        y1, y2, h2b = ([c5((QT, D)) for _ in range(2)] for _ in range(3))
        gidx = [c5((2, QT), i32) for _ in range(2)]
        wnow = [c5((QT, 2)) for _ in range(2)]

        banks = [ctx.enter_context(nc.psum_tensor(f"bank{i}", [128, 512], f32)) for i in range(8)]

        def bank(i, shape, dt=f32, parts=128):
            a = banks[i][0:parts, :]
            if dt != f32:
                a = a.bitcast(dt)
            a = a[:, 0:int(np.prod(shape))]
            if len(shape) == 2:
                a = a.rearrange("p (a b) -> p a b", a=shape[0])
            elif len(shape) == 3:
                a = a.rearrange("p (a b c) -> p a b c", a=shape[0], b=shape[1])
            return a

        YB, CB, B_T, B_U, RING = (1, 2), (0, 7), 3, 4, (5, 6)

        names = """ld_const ld_x ld_tok ld_bias ld_attn ld_ffn ld_vec ld_wgu ld_wd stacked
        setup_dve setup_consts setup_wt_ps setup_wt setup_fold csum_ps split_rows split_bias zeroed
        tok_dve tok_split tok_xT_ps tok_xT tok_hid_ps tok_hid tok_out_ps tok_h0 tok_h1
        a_dve a_var a_rstd a_xn a_xnT_ps a_xnT a_q_ps a_k_ps a_v_ps a_q16 a_k16 a_qk a_v a_s_ps a_nmx a_exp a_att
        a_attT_ps a_attT a_av_ps a_h1
        q_dve z_dve c_dve q_pool c_pool b_mean b_var b_rstd b_y b_ms b_r1 b_yT_ps b_yT b_qkv_ps b_qkv b_vz b_sinpart b_stacks
        b_T_ps b_T b_s_ps b_s_max b_mx3 b_mx3T_ps b_D b_st_ps b_exp b_pv_ps
        b_CT_act b_CT_dve b_ct_ps b_cx b_cxT_ps b_cxT b_o_ps c_stat b_h2 b_h2_st b_ms2 b_r2 b_hn b_hnT_ps b_hnT
        b_lg_ps b_lmx b_lexp b_both b_cnt_ps b_dest b_scat b_hn_free
        m_dve m_maps m_dest m_zero m_fill m_x0 m_x1 m_xT_ps0 m_xT_ps1 m_xT m_g_ps m_u_ps m_silu m_a m_aT_ps m_aT_act
        m_aT_dve m_y_ps m_y m_st0 m_st1
        f_h0 f_h1 f_idx f_w f_dve f_y0 f_y1 f_out f_st0 f_st1"""
        s = {n: sem(n) for n in names.split()}

        class Chain:

            def __init__(self, eng, step, i, n):
                self.eng, self.step, self.i, self.n, self.k = eng, step, i, n, 0

            def link(self, ins):
                ins.then_inc(self.step, 1)
                self.k += 1
                assert self.k <= self.n, "more links than stated"
                self.eng.wait_ge(self.step, self.i * self.n + self.k)

            def end(self):
                assert self.k == self.n, (self.k, self.n)

        def optional(stage):
            return lambda n, *more: None if n is None else stage(n, *more)

        def later(n):
            return not isinstance(n, int) or n > 0

        def pipeline(eng, step):
            step(None, None, None, 0)
            step(None, None, 0, 1)
            step(0, None, 1, 2)
            with eng.Fori(1, B - 2) as z:
                step(z, z - 1, z + 1, z + 2)
            step(B - 2, B - 3, B - 1, None)
            step(B - 1, B - 2, None, None)
            step(None, B - 1, None, None)

        block = ctx.enter_context(nc.Block())
        NPAIR = B // 2
        UNITS = 3 * NKV

        def flat(a):
            return a.rearrange("p a b -> p (a b)")

        def tile_of(a, i):
            return flat(a[0:T, ds(i, 1), :])

        @block.sync
        def _(sp):
            nkv = NKV * HD
            row = lambda v: v.rearrange("(o n) -> o n", o=1)
            for free, n in ((s["tok_h0"], 1), (s["tok_h1"], 1), (s["b_h2_st"], 16), (s["b_hn_free"], 1), (s["m_y"], 1),
                            (s["m_xT_ps0"], 1), (s["m_xT_ps1"], 1), (s["m_st0"], 16), (s["m_st1"], 16), (s["f_st0"], 16), (s["f_st1"], 16)):
                sp.sem_inc(free, n)
            sp.dma_start(C[:], const).then_inc(s["ld_const"], 16)
            sp.dma_start(raw0[0:TOK, 0:MID], tWh[0:TOK, :]).then_inc(s["ld_tok"], 16)
            sp.dma_start(raw0[0:TOK, MID:MID + D], tWr[0:TOK, :]).then_inc(s["ld_tok"], 16)
            sp.dma_start(raw1[0:TOK, 0:MID], tWh[TOK:2 * TOK, :]).then_inc(s["ld_tok"], 16)
            sp.dma_start(raw1[0:TOK, MID:MID + D], tWr[TOK:2 * TOK, :]).then_inc(s["ld_tok"], 16)
            sp.dma_start(rbias[0:1, 0:MID], row(tbh)).then_inc(s["ld_bias"], 16)
            sp.dma_start(rbias[0:1, MID:MID + D], row(tbo)).then_inc(s["ld_bias"], 16)
            sp.dma_start(rbias[0:1, MID + D:MID + 2 * D], row(tbr)).then_inc(s["ld_bias"], 16)
            sp.dma_start(X[0:T], x.rearrange("b (t p d) -> p (b t) d", t=QT, d=TOK)).then_inc(s["ld_x"], 16)
            sp.dma_start(WoT[:], tWo.rearrange("(c p) d -> p c d", p=128)).then_inc(s["ld_tok"], 16)
            for w, a in enumerate((aWq, aWk, aWv)):
                sp.dma_start(rawW[:, w], a.rearrange("(c p) h -> p c h", p=128)).then_inc(s["ld_attn"], 16)
            for i, v in enumerate((abq, abk)):
                sp.dma_start(bqk[:, i, :], v.rearrange("(c p) -> p c", p=128), allow_slow_non_contiguous=True).then_inc(s["ld_vec"], 16)
            sp.dma_start(lnc[:], ln1.rearrange("(c p) -> p c", p=128), allow_slow_non_contiguous=True).then_inc(s["ld_vec"], 16)
            sp.dma_start(bv[:], row(abv).to_broadcast([128, D])).then_inc(s["ld_vec"], 16)
            sp.dma_start(w2b[:], row(ln2).to_broadcast([128, D])).then_inc(s["ld_vec"], 16)
            sp.dma_start(Wqkv[:, :, 0:D], fWq.rearrange("(c p) n -> p c n", p=128)).then_inc(s["ld_ffn"], 16)
            sp.dma_start(Wqkv[:, :, D:D + nkv], fWk.rearrange("(c p) n -> p c n", p=128)).then_inc(s["ld_ffn"], 16)
            sp.dma_start(Wqkv[:, :, D + nkv:QKV], fWv.rearrange("(c p) n -> p c n", p=128)).then_inc(s["ld_ffn"], 16)
            sp.dma_start(Wo[:], fWo.rearrange("(c p) n -> p c n", p=128)).then_inc(s["ld_ffn"], 16)
            sp.dma_start(Wr[:], fWr.rearrange("(c p) n -> p c n", p=128)).then_inc(s["ld_ffn"], 16)
            sp.wait_ge(s["split_rows"], 1)
            for i, part in enumerate((sp_h, sp_m, sp_l, sp_h, sp_m, sp_h)):
                sp.dma_start(Wst[TOK * i:TOK * (i + 1), :], part[0:TOK, :]).then_inc(s["stacked"], 16)
            sp.wait_ge(s["split_bias"], 1)
            for i, part in enumerate((rp_h, rp_m, rp_l)):
                sp.dma_start(Wst[PARTS + i:PARTS + i + 1, :], part[0:1, :]).then_inc(s["stacked"], 16)
            for e in range(NE):
                sp.dma_start(WGU[:, e, :, 0:F], fWg[e].rearrange("(c p) f -> p c f", p=128)).then_inc(s["ld_wgu"], 16)
                sp.dma_start(WGU[:, e, :, F:2 * F], fWu[e].rearrange("(c p) f -> p c f", p=128)).then_inc(s["ld_wgu"], 16)
            sp.wait_ge(s["tok_h0"], NT // 2 + 1)
            sp.wait_ge(s["tok_h1"], NT // 2 + 1)
            for e in range(EARLY):
                sp.dma_start(WD[:, e], fWd[e].rearrange("(c p) d -> p c d", p=128)).then_inc(s["ld_wd"], 16)

            def keep_h2(c):
                sp.wait_ge(s["b_h2"], c + 1)
                sp.dma_start(h2_rows[ds(c, 1)].rearrange("o p t d -> (o p) t d"), h2[0:T]).then_inc(s["b_h2_st"], 16)
                sp.wait_ge(s["b_scat"], c * (16 * 2 * QT) + 16 * 2 * QT)
                sp.sem_inc(s["b_hn_free"], 1)

            with sp.Fori(0, B - 2) as c:
                keep_h2(c)
            sp.wait_ge(s["a_h1"], B)
            sp.wait_ge(s["b_stacks"], B)
            sp.wait_ge(s["b_vz"], B)
            for e in range(EARLY, NE):
                sp.dma_start(WD[:, e], fWd[e].rearrange("(c p) d -> p c d", p=128)).then_inc(s["ld_wd"], 16)
            keep_h2(B - 2)
            keep_h2(B - 1)

            sp.wait_ge(s["m_maps"], 1)
            sp.wait_ge(s["m_zero"], 1)
            for e in range(NE):
                n = sp.value_load(counts[0:1, e:e + 1], min_val=0, max_val=B * S)
                sp.dma_start(x_rows[ds(n + e * REGION, 128), :], zer[:]).then_inc(s["m_fill"], 16)
            sp.wait_ge(s["m_fill"], 16 * NE)
            sp.wait_ge(s["b_scat"], 16 * 2 * QT * B)
            with sp.Fori(0, TILES // 2) as j:
                for par, (landed, used) in enumerate(((s["m_x0"], s["m_xT_ps0"]), (s["m_x1"], s["m_xT_ps1"]))):
                    sp.wait_ge(used, j + 1)
                    r = sp.value_load(tile_in[0:1, ds(2 * j + par, 1)], min_val=0, max_val=NE * REGION - 128)
                    sp.dma_start(xin[par], x_rows[ds(r, 128), :]).then_inc(landed, 16)

            sp.wait_ge(s["b_h2_st"], 16 * B + 16)
            with sp.Fori(0, B // 2) as j:
                for par, (landed, stored) in enumerate(((s["f_h0"], s["f_st0"]), (s["f_h1"], s["f_st1"]))):
                    sp.wait_ge(stored, 16 * j + 16)
                    sp.dma_start(h2b[par][0:T],
                                 h2_rows[ds(2 * j + par, 1)].rearrange("o p t d -> (o p) t d")).then_inc(landed, 16)
                for par, stored in enumerate((s["f_st0"], s["f_st1"])):
                    sp.wait_ge(s["f_out"], 2 * j + par + 1)
                    sp.dma_start(out[ds(2 * j + par, 1)].rearrange("o (t p) d -> p (o t) d", t=QT),
                                 h2b[par][0:T]).then_inc(stored, 16)
            sp.wait_ge(s["f_st0"], 16 * (B // 2 + 1))
            sp.wait_ge(s["f_st1"], 16 * (B // 2 + 1))

        @block.tensor
        def _(pe):
            mm = nc.tensor.matmul
            tr = nc.tensor.transpose
            pe.wait_ge(s["ld_tok"], 16 * 5)
            pe.wait_ge(s["setup_consts"], 1)
            for i, (a, n) in enumerate(((0, 512), (512, 512), (MID, D))):
                last = mm(bank(i, (512,))[0:1, 0:n], onesf[0:TOK, 0:1], raw1[0:TOK, a:a + n], start=True, stop=True)
            last.then_inc(s["csum_ps"], 1)
            pe.wait_ge(s["ld_attn"], 16 * 3)
            for w in range(3):
                for hc in range(DC):
                    for oc in range(DC):
                        last = tr(bank(3 + w, (DC, DC, 128))[:, hc, oc], rawW[:, w, oc, 128 * hc:128 * (hc + 1)], ident)
            last.then_inc(s["setup_wt_ps"], 1)
            pe.wait_ge(s["setup_wt"], 1)
            pe.wait_ge(s["split_bias"], 1)
            pe.wait_ge(s["stacked"], 16 * 9)

            def tok_x(i, par):
                pe.wait_ge(s["tok_split"], i + 1)
                for q in range(4):
                    last = tr(bank(0, (4, 128), bf16)[0:STACK, q, 0:T], xst[0:T, q, 0:STACK], identb[0:T, 0:T])
                last.then_inc(s["tok_xT_ps"], 1)
                pe.wait_ge(s["tok_xT"], i + 1)

            def tok_hidden(i, par, m):
                if not (isinstance(i, int) and 8 * i + m - 3 <= 0):
                    pe.wait_ge(s["tok_hid"], i * 8 + (m - 3))
                mm(bank(1 + m % 4, (4 * T,)), Wst[0:STACK, 128 * m:128 * (m + 1)], xT[par][0:STACK, :],
                   start=True, stop=True).then_inc(s["tok_hid_ps"], 1)

            def tok_out(i, par, q):
                if q == 0:
                    pe.wait_ge(s["tok_hid"], i * 8 + 8)
                pe.wait_ge((s["tok_h0"], s["tok_h1"])[q % 2], i * 2 + (q // 2 + 1))
                o = bank(5 + q % 2, (D,), parts=T)
                for m in range(MC):
                    mm(o, hid[par][:, m, T * q:T * (q + 1)], WoT[:, m, :], start=(m == 0), stop=False)
                mm(o, xT[par][0:STACK, T * q:T * (q + 1)], Wst[0:STACK, MID:MID + D],
                   start=False, stop=True).then_inc(s["tok_out_ps"], 1)

            def tok_both(i, par):
                tok_x(i, par)
                for q in range(4):
                    tok_hidden(i, par, 2 * q)
                    tok_hidden(i, par, 2 * q + 1)
                    tok_out(i - 1, 1 - par, q)

            tok_x(0, 0)
            for m in range(MC):
                tok_hidden(0, 0, m)
            with pe.Fori(0, (NPAIR - 2) // 2) as j:
                tok_both(2 * j + 1, 1)
                tok_both(2 * j + 2, 0)
            tok_both(NPAIR - 1, 1)
            for q in range(4):
                tok_out(NPAIR - 1, 1, q)

            @optional
            def a_transpose(a):
                pe.wait_ge(s["a_xn"], a + 1)
                if later(a):
                    pe.wait_ge(s["b_qkv"], a)
                for t in range(QT):
                    for c in range(DC):
                        last = tr(bank(YB[0], (DC, S))[:, c, T * t:T * (t + 1)], xn[0:T, t, 128 * c:128 * (c + 1)],
                                  ident[0:T, 0:T])
                last.then_inc(s["a_xnT_ps"], 1)

            @optional
            def a_project(a):
                pe.wait_ge(s["a_xnT"], a + 1)
                for w, (at, done) in enumerate(((YB[1], s["a_q_ps"]), (YB[0], s["a_k_ps"]))):
                    for o in range(DC):
                        for c in range(DC):
                            last = mm(bank(at, (DC, S))[:, o], Wat[:, c, D * w + 128 * o:D * w + 128 * (o + 1)],
                                      xnT[:, c], start=(c == 0), stop=(c == DC - 1))
                    last.then_inc(done, 1)
                pe.wait_ge(s["a_q16"], a + 1)
                for t in range(QT):
                    for c in range(DC):
                        last = mm(bank(YB[1], (QT, D), parts=T)[:, t], xnT[:, c, T * t:T * (t + 1)], Wat[:, c, 2 * D:3 * D],
                                  start=(c == 0), stop=(c == DC - 1))
                last.then_inc(s["a_v_ps"], 1)

            @optional
            def a_scores(a):
                pe.wait_ge(s["a_qk"], a + 1)
                for t in range(QT):
                    for c in range(DC):
                        last = mm(bank(YB[0], (QT, S), parts=T)[:, t], qk[:, c, T * t:T * (t + 1)], qk[:, DC + c],
                                  start=(c == 0), stop=(c == DC - 1))
                last.then_inc(s["a_s_ps"], 1)

            @optional
            def a_transpose_probs(a):
                pe.wait_ge(s["a_v"], a + 1)
                pe.wait_ge(s["a_att"], a + 1)
                for k in range(QT):
                    for t in range(QT):
                        last = tr(bank(YB[1], (QT, QT, 128), f16, T)[:, k, t, 0:T], att[0:T, t, T * k:T * (k + 1)],
                                  identh[0:T, 0:T])
                last.then_inc(s["a_attT_ps"], 1)

            @optional
            def a_values(a):
                pe.wait_ge(s["a_attT"], a + 1)
                for t in range(QT):
                    for k in range(QT):
                        last = mm(bank(YB[0], (QT, D), parts=T)[:, t], attT[0:T, k, T * t:T * (t + 1)], vq[0:T, k],
                                  start=(k == 0), stop=(k == QT - 1))
                last.then_inc(s["a_av_ps"], 1)

            @optional
            def b_transpose(b):
                pe.wait_ge(s["b_y"], b + 1)
                for t in range(QT):
                    for c in range(DC):
                        last = tr(bank(YB[1], (DC, S))[:, c, T * t:T * (t + 1)], y[0:T, t, 128 * c:128 * (c + 1)],
                                  ident[0:T, 0:T])
                last.then_inc(s["b_yT_ps"], 1)

            @optional
            def b_project(b):
                pe.wait_ge(s["b_yT"], b + 1)
                for t in range(QT):
                    for c in range(DC):
                        last = mm(bank(YB[t], (QKV,), parts=T), yT[:, c, T * t:T * (t + 1)], Wqkv[:, c],
                                  start=(c == 0), stop=(c == DC - 1))
                last.then_inc(s["b_qkv_ps"], 1)

            BLOCKS = ((0, 0), (1, 0), (1, 1))

            @optional
            def z_transpose_stacks(z, f):
                if f == 0:
                    pe.wait_ge(s["b_stacks"], z + 1)
                    if later(z):
                        pe.wait_ge(s["b_CT_act"], z)
                        pe.wait_ge(s["b_CT_dve"], z)
                if f >= 2:
                    pe.wait_ge(s["b_T"], z * 5 + (f - 1))
                o = bank((B_T, B_U)[f % 2], (4, QT, 128), bf16, PARTS)
                for h in range(4):
                    for t in range(QT):
                        src = kst[0:T, NKV * t + h] if f == 0 else qst[0:T, NH * t + REP * (f - 1) + h]
                        last = tr(o[:, h, t, 0:T], src, identb[0:T, 0:T])
                last.then_inc(s["b_T_ps"], 1)

            @optional
            def z_scores(z, g):
                pe.wait_ge(s["b_T"], z * 5 + (g + 2))
                for u, (t, k) in enumerate(BLOCKS):
                    n = 3 * g + u
                    if n >= 2:
                        pe.wait_ge(s["b_s_max"], z * UNITS + (n - 1))
                    o = bank(RING[n % 2], (REP, T), parts=T)
                    if t == k:
                        mm(flat(o), identb[0:T, 0:T], maskqb[0:T, :].unsqueeze(1).to_broadcast([T, REP, T]),
                           start=True, stop=False, skip_group_check=True)
                    for j in range(REP):
                        last = mm(o[:, j], QTs[0:PARTS, REP * g + j, T * t:T * (t + 1)], KTs[0:PARTS, g, T * k:T * (k + 1)],
                                  start=(t != k), stop=True, skip_group_check=True)
                    last.then_inc(s["b_s_ps"], 1)

            @optional
            def z_transpose_max(z):
                pe.wait_ge(s["b_mx3"], z + 1)
                for t in range(QT):
                    last = tr(bank(B_T, (QT, 128), bf16)[0:6 * NH, t, 0:T], mx3[0:T, t], identb[0:T, 0:T])
                last.then_inc(s["b_mx3T_ps"], 1)

            @optional
            def z_scores_shifted(z, g):
                if g == 0:
                    pe.wait_ge(s["b_D"], z + 1)
                for u, (t, k) in enumerate(BLOCKS):
                    n = 3 * g + u
                    if n >= 2:
                        pe.wait_ge(s["b_exp"], z * UNITS + (n - 1))
                    o = bank(RING[n % 2], (REP * T,), parts=T)
                    if t == k:
                        mm(o, identb[0:T, 0:T], maskkb[0:T, :].unsqueeze(1).to_broadcast([T, REP, T]),
                           start=True, stop=False)
                    mm(o, KTs[0:PARTS, g, T * k:T * (k + 1)], QTs[0:PARTS, REP * g:REP * (g + 1), T * t:T * (t + 1)],
                       start=(t != k), stop=False)
                    mm(o, selb[:, g], Dm[:, :, T * t:T * (t + 1)], start=False, stop=True).then_inc(s["b_st_ps"], 1)

            @optional
            def z_weigh_values(z, g):
                pe.wait_ge(s["b_exp"], z * UNITS + (3 * g + 3))
                if g == 0:
                    pe.wait_ge(s["b_vz"], z + 1)
                for u, (t, k) in enumerate(BLOCKS):
                    last = mm(bank((B_T, B_U)[t], (REP * T,)), vz[0:T, k, g], PT[g % 2][0:T, u],
                              start=(g == 0 and k == 0), stop=(g == NKV - 1 and t == k))
                last.then_inc(s["b_pv_ps"], 1)

            @optional
            def c_context_back(c):
                pe.wait_ge(s["b_CT_act"], c + 1)
                pe.wait_ge(s["b_CT_dve"], c + 1)
                for t in range(QT):
                    for j in range(REP):
                        last = tr(bank(CB[t], (REP, 128), parts=T)[:, j], CT[:, j, T * t:T * (t + 1)], ident)
                    last.then_inc(s["b_ct_ps"], 1)

            @optional
            def c_transpose_context(c):
                pe.wait_ge(s["b_cx"], c + 1)
                for t in range(QT):
                    for k in range(DC):
                        last = tr(bank(CB[0], (DC, S))[:, k, T * t:T * (t + 1)], cx[0:T, t, 128 * k:128 * (k + 1)],
                                  ident[0:T, 0:T])
                last.then_inc(s["b_cxT_ps"], 1)

            @optional
            def c_output(c):
                pe.wait_ge(s["b_cxT"], c + 1)
                for t in range(QT):
                    for k in range(DC):
                        last = mm(bank(CB[1], (QT, D), parts=T)[:, t], cxT[:, k, T * t:T * (t + 1)], Wo[:, k],
                                  start=(k == 0), stop=(k == DC - 1))
                last.then_inc(s["b_o_ps"], 1)

            @optional
            def c_transpose_hn(c):
                pe.wait_ge(s["b_hn"], c + 1)
                for t in range(QT):
                    for k in range(DC):
                        last = tr(bank(CB[0], (DC, S))[:, k, T * t:T * (t + 1)], hn[0:T, t, 128 * k:128 * (k + 1)],
                                  ident[0:T, 0:T])
                last.then_inc(s["b_hnT_ps"], 1)

            @optional
            def c_logits(c):
                pe.wait_ge(s["b_hnT"], c + 1)
                for t in range(QT):
                    for k in range(DC):
                        last = mm(bank(CB[1], (QT, NE), parts=T)[:, t], hnT[:, k, T * t:T * (t + 1)], Wr[:, k],
                                  start=(k == 0), stop=(k == DC - 1))
                last.then_inc(s["b_lg_ps"], 1)

            @optional
            def c_count(c):
                pe.wait_ge(s["b_both"], c + 1)
                o = bank(CB[0], (3, NE), parts=T)
                mm(o[:, 0], beforeb[0:T, :], both[0:T, 0], start=True, stop=True)
                mm(o[:, 1], onesb[0:T, :], both[0:T, 0], start=True, stop=False)
                mm(o[:, 1], beforeb[0:T, :], both[0:T, 1], start=False, stop=True)
                mm(o[:, 2], onesb[0:T, :], both[0:T, 0], start=True, stop=False)
                mm(o[:, 2], onesb[0:T, :], both[0:T, 1], start=False, stop=True).then_inc(s["b_cnt_ps"], 1)

            def step(z, c, b, a):
                z_transpose_stacks(z, 0)
                z_transpose_stacks(z, 1)
                c_context_back(c)
                z_scores(z, 0)
                b_transpose(b)
                z_transpose_stacks(z, 2)
                c_transpose_context(c)
                z_scores(z, 1)
                b_project(b)
                z_transpose_stacks(z, 3)
                c_output(c)
                a_transpose(a)
                z_scores(z, 2)
                z_transpose_stacks(z, 4)
                a_project(a)
                c_transpose_hn(c)
                c_logits(c)
                z_scores(z, 3)
                z_transpose_max(z)
                a_scores(a)
                z_scores_shifted(z, 0)
                z_scores_shifted(z, 1)
                c_count(c)
                z_weigh_values(z, 0)
                a_transpose_probs(a)
                z_scores_shifted(z, 2)
                z_weigh_values(z, 1)
                a_values(a)
                z_scores_shifted(z, 3)
                z_weigh_values(z, 2)
                z_weigh_values(z, 3)

            pe.wait_ge(s["setup_fold"], 1)
            pe.wait_ge(s["ld_ffn"], 16 * 5)
            pipeline(pe, step)

            G, U, XT, AT, Y = 0, 1, 2, (3, 5), 4

            def m_transpose_x(par, use):
                pe.wait_ge((s["m_x0"], s["m_x1"])[par], use * 16)
                for c in range(DC):
                    last = tr(bank(XT, (DC, 128))[:, c], xin[par][:, 128 * c:128 * (c + 1)], ident)
                last.then_inc((s["m_xT_ps0"], s["m_xT_ps1"])[par], 1)

            def m_up(i, e, which):
                if which == 0:
                    pe.wait_ge(s["m_xT"], i + 1)
                    pe.wait_ge(s["m_silu"], i)
                else:
                    pe.wait_ge(s["m_a"], i)
                for c in range(DC):
                    last = mm(bank((G, U)[which], (F,)), xTe[:, c],
                              flat(WGU[:, ds(e, 1), c, F * which:F * (which + 1)]), start=(c == 0), stop=(c == DC - 1))
                last.then_inc((s["m_g_ps"], s["m_u_ps"])[which], 1)

            def m_transpose_a(i, par):
                pe.wait_ge(s["m_a"], i + 1)
                for c in range(FC):
                    last = tr(bank(AT[c // 2], (2, 128))[:, c % 2], ga[par][:, 128 * c:128 * (c + 1)], ident)
                last.then_inc(s["m_aT_ps"], 1)

            def m_down(i, e):
                pe.wait_ge(s["m_aT_act"], i + 1)
                pe.wait_ge(s["m_aT_dve"], i + 1)
                pe.wait_ge(s["m_y"], i + 1)
                for c in range(FC):
                    last = mm(bank(Y, (D,)), gaT[:, c], flat(WD[:, ds(e, 1), c, :]), start=(c == 0), stop=(c == FC - 1))
                last.then_inc(s["m_y_ps"], 1)

            def expert(i):
                return pe.value_load(tile_e[0:1, ds(i, 1)], min_val=0, max_val=NE - 1)

            def m_step(i, par, more, use):
                e, before = expert(i), expert(i - 1)
                m_up(i, e, 0)
                m_transpose_a(i - 1, 1 - par)
                m_up(i, e, 1)
                if more:
                    m_transpose_x(1 - par, use)
                m_down(i - 1, before)

            pe.wait_ge(s["ld_wgu"], 16 * 2 * NE)
            pe.wait_ge(s["ld_wd"], 16 * NE)
            pe.wait_ge(s["m_maps"], 1)
            m_transpose_x(0, 1)
            e0 = expert(0)
            m_up(0, e0, 0)
            m_up(0, e0, 1)
            m_transpose_x(1, 1)
            with pe.Fori(0, (TILES - 2) // 2) as j:
                m_step(2 * j + 1, 1, True, j + 2)
                m_step(2 * j + 2, 0, True, j + 2)
            m_step(TILES - 1, 1, False, None)
            m_transpose_a(TILES - 1, 1)
            m_down(TILES - 1, expert(TILES - 1))

        @block.scalar
        def _(act):
            A = nc.scalar.activation
            def tok_copy_x(i, par):
                act.wait_ge(s["tok_xT_ps"], i + 1)
                A(xT[par][0:STACK, :].rearrange("p (q n) -> p q n", q=4), bank(0, (4, 128), bf16)[0:STACK, :, 0:T],
                  ACT.Copy).then_inc(s["tok_xT"], 1)

            def tok_silu(i, par):
                for m in range(MC):
                    act.wait_ge(s["tok_hid_ps"], i * 8 + (m + 1))
                    A(hid[par][:, m], bank(1 + m % 4, (4 * T,)), ACT.Silu).then_inc(s["tok_hid"], 1)

            tok_copy_x(0, 0)
            tok_silu(0, 0)
            with act.Fori(0, (NPAIR - 2) // 2) as j:
                for par in (1, 0):
                    i = 2 * j + 2 - par
                    tok_copy_x(i, par)
                    tok_silu(i, par)
            tok_copy_x(NPAIR - 1, 1)
            tok_silu(NPAIR - 1, 1)

            @optional
            def a_copy_x(a):
                act.wait_ge(s["a_xnT_ps"], a + 1)
                A(flat(xnT), bank(YB[0], (DC * S,)), ACT.Copy).then_inc(s["a_xnT"], 1)

            @optional
            def a_bias(a):
                for w, (at, ready, done) in enumerate(((YB[1], s["a_q_ps"], s["a_q16"]), (YB[0], s["a_k_ps"], s["a_k16"]))):
                    act.wait_ge(ready, a + 1)
                    for o in range(DC):
                        last = A(qk[:, DC * w + o], bank(at, (DC, S))[:, o], ACT.Identity, bias=bqk[:, w, o:o + 1])
                    last.then_inc(done, 1)

            @optional
            def a_exps(a):
                act.wait_ge(s["a_nmx"], a + 1)
                for t in range(QT):
                    last = A(ex[0:T, t], sq[0:T, t], ACT.Exp, bias=smA[0:T, t:t + 1], accum_out=smA[0:T, 2 + t:3 + t])
                last.then_inc(s["a_exp"], 1)

            @optional
            def a_copy_probs(a):
                act.wait_ge(s["a_attT_ps"], a + 1)
                A(attT[0:T].rearrange("p k (t n) -> p (k t) n", t=QT), bank(YB[1], (QT * QT, 128), f16, T)[:, :, 0:T],
                  ACT.Copy).then_inc(s["a_attT"], 1)

            @optional
            def b_squares(b):
                act.wait_ge(s["b_y"], b + 1)
                for t in range(QT):
                    last = A(sqb[0:T, t, 0:D], y[0:T, t], ACT.Square, scale=float(D) ** -0.5, accum_out=smB[0:T, t:t + 1])
                last.then_inc(s["b_ms"], 1)

            @optional
            def b_copy_y(b):
                act.wait_ge(s["b_yT_ps"], b + 1)
                A(flat(yT), bank(YB[1], (DC * S,)), ACT.Copy).then_inc(s["b_yT"], 1)

            @optional
            def b_scale_qkv(b):
                act.wait_ge(s["b_qkv_ps"], b + 1)
                act.wait_ge(s["b_r1"], b + 1)
                if later(b):
                    act.wait_ge(s["b_vz"], b)
                for t in range(QT):
                    last = A(qkv[0:T, t], bank(YB[t], (QKV,), parts=T), ACT.Copy, scale=smB[0:T, 2 + t:3 + t])
                last.then_inc(s["b_qkv"], 1)

            @optional
            def z_copy_stack(z, f):
                act.wait_ge(s["b_T_ps"], z * 5 + (f + 1))
                dst = KTs[0:PARTS] if f == 0 else QTs[0:PARTS, REP * (f - 1):REP * f]
                A(dst.rearrange("p h (t n) -> p (h t) n", t=QT), bank((B_T, B_U)[f % 2], (4 * QT, 128), bf16, PARTS)[:, :, 0:T],
                  ACT.Copy).then_inc(s["b_T"], 1)

            @optional
            def z_exps(z, g):
                if g >= 2:
                    act.wait_ge(s["b_pv_ps"], z * NKV + (g - 1))
                for u in range(3):
                    n = 3 * g + u
                    act.wait_ge(s["b_st_ps"], z * UNITS + (n + 1))
                    A(PT[g % 2][0:T, u], bank(RING[n % 2], (REP * T,), parts=T), ACT.Exp,
                      scale=float(HD) ** -0.5).then_inc(s["b_exp"], 1)

            @optional
            def z_copy_context(z):
                act.wait_ge(s["b_pv_ps"], z * NKV + NKV)
                A(CT[:, :, 0:T], bank(B_T, (REP, T)), ACT.Copy).then_inc(s["b_CT_act"], 1)

            @optional
            def c_copy_cx(c):
                act.wait_ge(s["b_cxT_ps"], c + 1)
                A(flat(cxT), bank(CB[0], (DC * S,)), ACT.Copy).then_inc(s["b_cxT"], 1)

            @optional
            def c_squares(c):
                act.wait_ge(s["b_h2"], c + 1)
                for t in range(QT):
                    last = A(sqc[0:T, t], h2[0:T, t], ACT.Square, scale=float(D) ** -0.5, accum_out=smC[0:T, t:t + 1])
                last.then_inc(s["b_ms2"], 1)

            @optional
            def c_copy_hn(c):
                act.wait_ge(s["b_hnT_ps"], c + 1)
                A(flat(hnT), bank(CB[0], (DC * S,)), ACT.Copy).then_inc(s["b_hnT"], 1)

            @optional
            def c_route_exp(c):
                act.wait_ge(s["b_lmx"], c + 1)
                A(prob[0:T], lgx[0:T], ACT.Exp).then_inc(s["b_lexp"], 1)

            def step(z, c, b, a):
                z_copy_stack(z, 0)
                z_copy_stack(z, 1)
                b_squares(b)
                b_copy_y(b)
                z_copy_stack(z, 2)
                c_copy_cx(c)
                b_scale_qkv(b)
                z_copy_stack(z, 3)
                a_copy_x(a)
                z_copy_stack(z, 4)
                c_squares(c)
                a_bias(a)
                c_copy_hn(c)
                c_route_exp(c)
                z_exps(z, 0)
                z_exps(z, 1)
                a_exps(a)
                z_exps(z, 2)
                a_copy_probs(a)
                z_exps(z, 3)
                z_copy_context(z)

            act.wait_ge(s["ld_vec"], 16 * 5)
            act.wait_ge(s["tok_h0"], NT // 2 + 1)
            act.wait_ge(s["tok_h1"], NT // 2 + 1)
            pipeline(act, step)

            def m_silu(i):
                act.wait_ge(s["m_g_ps"], i + 1)
                act.wait_ge(s["m_a"], i)
                A(gs, bank(0, (F,)), ACT.Silu).then_inc(s["m_silu"], 1)

            def m_copy_a(i):
                act.wait_ge(s["m_aT_ps"], i + 1)
                A(gaT[:, 0:2], bank(3, (2, 128)), ACT.Copy).then_inc(s["m_aT_act"], 1)

            def m_out(i, par, use):
                act.wait_ge(s["m_y_ps"], i + 1)
                act.wait_ge((s["m_st0"], s["m_st1"])[par], use * 16 + 16)
                A(yo[par], bank(4, (D,)), ACT.Copy).then_inc(s["m_y"], 1)
                act.wait_ge(s["m_y"], i + 2)
                act.dma_start(y_rows[ds(128 * i, 128), :], yo[par]).then_inc((s["m_st0"], s["m_st1"])[par], 16)

            act.wait_ge(s["m_maps"], 1)
            m_silu(0)
            with act.Fori(0, (TILES - 2) // 2) as j:
                for par in (1, 0):
                    i = 2 * j + 2 - par
                    m_silu(i)
                    m_copy_a(i - 1)
                    m_out(i - 1, 1 - par, j if par == 1 else j)
            m_silu(TILES - 1)
            m_copy_a(TILES - 2)
            m_out(TILES - 2, 0, TILES // 2 - 1)
            m_copy_a(TILES - 1)
            m_out(TILES - 1, 1, TILES // 2 - 1)

        @block.vector
        def _(dve):
            V = nc.vector
            ch = Chain(dve, s["setup_dve"], 0, 8)
            V.memset(onesf[:], 1.0)
            V.memset(onesb[:], 1.0)
            V.memset(mhalf[:], -0.5)
            V.memset(epsc[:], EPS)
            V.memset(xst[:], 1.0)
            dve.wait_ge(s["ld_const"], 16)
            V.tensor_copy(identb[:], ident)
            V.tensor_copy(identh[:], ident)
            V.tensor_copy(maskqb[:], const_at("mask_q"))
            V.tensor_copy(maskkb[:], const_at("mask_k"))
            V.tensor_copy(beforeb[:], const_at("before"))
            V.tensor_copy(flat(selb), const_at("sel"))
            V.tensor_copy(run[:], const_at("ebase")).then_inc(s["setup_consts"], 1)
            dve.wait_ge(s["ld_tok"], 16 * 5)
            w0, d0 = raw0[0:TOK], sp_d[0:TOK]
            ch.link(V.tensor_copy(sp_h[0:TOK], w0))
            ch.link(V.tensor_tensor(d0, w0, sp_h[0:TOK], ALU.subtract))
            ch.link(V.tensor_copy(sp_m[0:TOK], d0))
            V.tensor_tensor(sp_l[0:TOK], d0, sp_m[0:TOK], ALU.subtract).then_inc(s["split_rows"], 1)
            dve.wait_ge(s["ld_bias"], 16 * 3)
            dve.wait_ge(s["csum_ps"], 1)
            for i, (a, n) in enumerate(((0, 512), (512, 512), (MID, D))):
                last = V.tensor_tensor(rsum[0:1, a:a + n], bank(i, (512,))[0:1, 0:n], rbias[0:1, a:a + n], ALU.add)
            ch.link(last)
            ch.link(V.tensor_tensor(rsum[0:1, MID:], rsum[0:1, MID:], rbias[0:1, MID + D:], ALU.add))
            r0, d1 = rsum[0:1], sp_d[0:1]
            ch.link(V.tensor_copy(rp_h[0:1], r0))
            ch.link(V.tensor_tensor(d1, r0, rp_h[0:1], ALU.subtract))
            ch.link(V.tensor_copy(rp_m[0:1], d1))
            ch.end()
            V.tensor_tensor(rp_l[0:1], d1, rp_m[0:1], ALU.subtract).then_inc(s["split_bias"], 1)
            dve.wait_ge(s["setup_wt_ps"], 1)
            for w in range(3):
                last = V.tensor_copy(Wat[:, :, D * w:D * (w + 1)], bank(3 + w, (DC, D)))
            last.then_inc(s["setup_wt"], 1)
            dve.wait_ge(s["ld_ffn"], 16 * 5)
            dve.wait_ge(s["ld_vec"], 16 * 5)
            for c in range(DC):
                last = V.tensor_scalar(Wqkv[:, c], Wqkv[:, c], lnc[:, c:c + 1], None, ALU.mult)
            last.then_inc(s["setup_fold"], 1)

            dve.wait_ge(s["ld_x"], 16)

            def tok_split(i):
                if not isinstance(i, int):
                    dve.wait_ge(s["tok_xT_ps"], i)
                elif i > 0:
                    dve.wait_ge(s["tok_xT_ps"], i)
                ch = Chain(dve, s["tok_dve"], i, 3)
                xi = X[0:T, ds(4 * i, 4), :]
                part = lambda n: xst[0:T, :, TOK * n:TOK * (n + 1)]
                ch.link(V.tensor_copy(part(0), xi))
                V.tensor_copy(part(1), part(0))
                V.tensor_copy(part(2), part(0))
                ch.link(V.tensor_tensor(xd[0:T], xi, part(0), ALU.subtract))
                ch.link(V.tensor_copy(part(3), xd[0:T]))
                ch.end()
                V.tensor_copy(part(4), part(3))
                V.tensor_tensor(part(5), xd[0:T], part(3), ALU.subtract).then_inc(s["tok_split"], 1)

            def tok_copy(i):
                for q in range(4):
                    dve.wait_ge(s["tok_out_ps"], i * 4 + (q + 1))
                    V.tensor_copy(tile_of(H, 4 * i + q), bank(5 + q % 2, (D,), parts=T)).then_inc((s["tok_h0"], s["tok_h1"])[q % 2], 1)

            tok_split(0)
            with dve.Fori(0, NPAIR - 1) as i:
                tok_split(i + 1)
                tok_copy(i)
            tok_copy(NPAIR - 1)

            def stats(ch, i, st, mv, sm, src, done):
                for t in range(QT):
                    last = V.bn_stats(st[0:T, t], tile_of(src, 2 * i + t))
                ch.link(last)
                V.memset(gate_v[:], 0.0)
                for t in range(QT):
                    last = V.bn_aggr(mv[0:T, t], st[0:T, t])
                ch.link(last)
                V.tensor_scalar(sm[0:T, 8:10], mv[0:T, :, 1], EPS, None, ALU.add).then_inc(done, 1)

            def normed(i, mv, sm, src, dst, done):
                for t in range(QT):
                    last = V.tensor_scalar(dst[0:T, t], tile_of(src, 2 * i + t), mv[0:T, t, 0:1], sm[0:T, 10 + t:11 + t],
                                           ALU.subtract, ALU.mult)
                last.then_inc(done, 1)

            def clip16(a):
                return V.tensor_scalar(a, a, F16MAX, -F16MAX, ALU.min, ALU.max)

            def optional_stage(stage):
                return lambda self, *more: None if self.i is None else stage(self, *more)

            class StageA:
                def __init__(self, i):
                    self.i, self.ch = i, Chain(dve, s["a_dve"], i, 6)

                @optional_stage
                def stats(self):
                    stats(self.ch, self.i, stA, mvA, smA, H, s["a_var"])

                @optional_stage
                def norm(self):
                    dve.wait_ge(s["a_rstd"], self.i + 1)
                    normed(self.i, mvA, smA, H, xn, s["a_xn"])

                @optional_stage
                def values(self):
                    dve.wait_ge(s["a_v_ps"], self.i + 1)
                    self.ch.link(V.tensor_tensor(vq[0:T], bank(YB[1], (QT, D), parts=T),
                                                 bv[0:T].unsqueeze(1).to_broadcast([T, QT, D]), ALU.add))
                    clip16(vq[0:T]).then_inc(s["a_v"], 1)

                @optional_stage
                def clip_qk(self):
                    dve.wait_ge(s["a_k16"], self.i + 1)
                    clip16(flat(qk)).then_inc(s["a_qk"], 1)

                @optional_stage
                def quantize_scores(self):
                    dve.wait_ge(s["a_s_ps"], self.i + 1)
                    self.ch.link(V.tensor_scalar(flat(sq[0:T]), bank(YB[0], (QT * S,), parts=T), float(D) ** -0.5, F16MAX,
                                                 ALU.mult, ALU.min))
                    self.ch.link(V.tensor_scalar(flat(sq[0:T]), flat(sq[0:T]), -F16MAX, None, ALU.max))
                    V.tensor_reduce(smA[0:T, 0:QT], sq[0:T], AX.X, ALU.max, negate=True).then_inc(s["a_nmx"], 1)

                @optional_stage
                def probs(self):
                    dve.wait_ge(s["a_exp"], self.i + 1)
                    self.ch.link(V.reciprocal(smA[0:T, 4:6], smA[0:T, 2:4]))
                    for t in range(QT):
                        last = V.tensor_scalar(att[0:T, t], ex[0:T, t], smA[0:T, 4 + t:5 + t], None, ALU.mult)
                    last.then_inc(s["a_att"], 1)

                @optional_stage
                def residual(self):
                    dve.wait_ge(s["a_av_ps"], self.i + 1)
                    h = H[0:T, ds(2 * self.i, QT), :]
                    V.tensor_tensor(h, h, bank(YB[0], (QT, D), parts=T), ALU.add).then_inc(s["a_h1"], 1)
                    self.ch.end()

            class StageB:
                def __init__(self, i):
                    self.i, self.ch = i, Chain(dve, s["q_dve"], i, 7)

                @optional_stage
                def stats(self):
                    dve.wait_ge(s["a_h1"], self.i + 1)
                    stats(self.ch, self.i, stB, mvB, smB, H, s["b_var"])

                @optional_stage
                def norm(self):
                    dve.wait_ge(s["b_rstd"], self.i + 1)
                    normed(self.i, mvB, smB, H, y, s["b_y"])

                @optional_stage
                def rope(self):
                    b, ch = self.i, self.ch
                    dve.wait_ge(s["b_qkv"], b + 1)
                    if later(b):
                        dve.wait_ge(s["b_T_ps"], b * 5)
                    heads = NH + NKV
                    hv = lambda a: a.rearrange("p t (h d) -> p t h d", d=HD)
                    cos = const_at("cos", T).rearrange("p (t d) -> p t d", t=QT).unsqueeze(2).to_broadcast([T, QT, heads, HD])
                    ch.link(V.tensor_tensor(hv(t1[0:T]), hv(qkv[0:T, :, 0:heads * HD]), cos, ALU.mult))
                    dve.wait_ge(s["b_sinpart"], b + 1)
                    two = lambda a: a.rearrange("p (t h) d -> p t (h d)", t=QT)
                    V.tensor_tensor(two(rok[0:T]), t1[0:T, :, NH * HD:], t2[0:T, :, NH * HD:], ALU.add)
                    ch.link(V.tensor_tensor(two(roq[0:T]), t1[0:T, :, 0:NH * HD], t2[0:T, :, 0:NH * HD], ALU.add))
                    Q = lambda n, m=1: qst[0:T, :, HD * n:HD * (n + m)]
                    K = lambda n, m=1: kst[0:T, :, HD * n:HD * (n + m)]
                    V.tensor_copy(Q(0), roq[0:T])
                    ch.link(V.tensor_copy(K(0), rok[0:T]))
                    V.tensor_tensor(dk[0:T], rok[0:T], K(0), ALU.subtract)
                    V.tensor_tensor(dq[0:T], roq[0:T], Q(0), ALU.subtract)
                    V.tensor_copy(Q(1), Q(0))
                    ch.link(V.tensor_copy(Q(2), Q(0)))
                    V.tensor_copy(K(1), dk[0:T])
                    ch.link(V.tensor_copy(Q(3), dq[0:T]))
                    V.tensor_tensor(K(2), dk[0:T], K(1), ALU.subtract)
                    V.tensor_tensor(Q(5), dq[0:T], Q(3), ALU.subtract)
                    V.tensor_copy(Q(4), Q(3))
                    V.tensor_copy(K(3, 2), K(0, 2))
                    V.tensor_copy(K(5), K(0)).then_inc(s["b_stacks"], 1)
                    ch.end()

            class StageZ:
                def __init__(self, i):
                    self.i, self.ch = i, Chain(dve, s["z_dve"], i, 5)

                @optional_stage
                def maxima(self, g):
                    for u in range(3):
                        n = 3 * g + u
                        dve.wait_ge(s["b_s_ps"], self.i * UNITS + (n + 1))
                        V.tensor_reduce(mxu[0:T, u, REP * g:REP * (g + 1)], bank(RING[n % 2], (REP, T), parts=T), AX.X,
                                        ALU.max).then_inc(s["b_s_max"], 1)

                @optional_stage
                def negate_split_max(self):
                    z, ch = self.i, self.ch
                    dve.wait_ge(s["b_s_max"], z * UNITS + UNITS)
                    ch.link(V.tensor_tensor(mxu[0:T, 1], mxu[0:T, 1], mxu[0:T, 2], ALU.max))
                    part = lambda n: mx3[0:T, :, NH * n:NH * (n + 1)]
                    ch.link(V.tensor_scalar(nmx[0:T], mxu[0:T, 0:2], -1.0, None, ALU.mult))
                    ch.link(V.tensor_copy(part(0), nmx[0:T]))
                    ch.link(V.tensor_tensor(dmx[0:T], nmx[0:T], part(0), ALU.subtract))
                    ch.link(V.tensor_copy(part(1), dmx[0:T]))
                    V.tensor_tensor(part(2), dmx[0:T], part(1), ALU.subtract).then_inc(s["b_mx3"], 1)
                    ch.end()

                @optional_stage
                def spread_max(self):
                    dve.wait_ge(s["b_mx3T_ps"], self.i + 1)
                    n = 3 * NH
                    src = bank(B_T, (QT, 128), bf16)[0:n, :, 0:T].unsqueeze(1).to_broadcast([n, REP, QT, T])
                    which = const_at("delta", n).unsqueeze(2).unsqueeze(3).to_broadcast([n, REP, QT, T])
                    V.tensor_tensor(Dm[0:n].rearrange("p j (t n) -> p j t n", t=QT), src, which,
                                    ALU.mult).then_inc(s["b_D"], 1)

                @optional_stage
                def copy_context(self):
                    dve.wait_ge(s["b_pv_ps"], self.i * NKV + NKV)
                    V.tensor_copy(CT[:, :, T:S], bank(B_U, (REP, T))).then_inc(s["b_CT_dve"], 1)

            over_e = lambda a: a[0:T].unsqueeze(2).to_broadcast([T, QT, NE])
            over_t = lambda a: a.unsqueeze(1).to_broadcast([T, QT, NE])
            rev = over_t(const_at("rev", T))

            class StageC:
                def __init__(self, i):
                    self.i, self.ch = i, Chain(dve, s["c_dve"], i, 24)

                @optional_stage
                def divide_context(self):
                    c, ch = self.i, self.ch
                    for t in range(QT):
                        dve.wait_ge(s["b_ct_ps"], c * QT + (t + 1))
                        src = bank(CB[t], (REP, NKV, 32), parts=T)
                        rc = rcx[0:T, t].rearrange("p (j g) -> p j g", j=REP)
                        ch.link(V.reciprocal(rc, src[:, :, :, HD]))
                        last = V.tensor_tensor(cx[0:T, t].rearrange("p (g j d) -> p j g d", g=NKV, j=REP),
                                               src[:, :, :, 0:HD], rc.unsqueeze(3).to_broadcast([T, REP, NKV, HD]), ALU.mult)
                    last.then_inc(s["b_cx"], 1)

                @optional_stage
                def residual(self):
                    c, ch = self.i, self.ch
                    dve.wait_ge(s["c_stat"], c + 1)
                    dve.wait_ge(s["b_h2_st"], c * 16 + 16)
                    for t in range(QT):
                        last = V.tensor_scalar(h2[0:T, t], tile_of(H, 2 * c + t), smC[0:T, 8 + t:9 + t],
                                               smC[0:T, 10 + t:11 + t], ALU.subtract, ALU.mult)
                    ch.link(last)
                    dve.wait_ge(s["b_o_ps"], c + 1)
                    ch.link(V.tensor_tensor(h2[0:T], h2[0:T], bank(CB[1], (QT, D), parts=T), ALU.add))
                    V.tensor_scalar(h2[0:T], h2[0:T], CLIP, -CLIP, ALU.min, ALU.max).then_inc(s["b_h2"], 1)

                @optional_stage
                def second_norm(self):
                    dve.wait_ge(s["b_r2"], self.i + 1)
                    dve.wait_ge(s["b_hn_free"], self.i + 1)
                    for t in range(QT):
                        last = V.scalar_tensor_tensor(hn[0:T, t], h2[0:T, t], smC[0:T, 6 + t:7 + t], w2b[0:T],
                                                      ALU.mult, ALU.mult)
                    last.then_inc(s["b_hn"], 1)

                @optional_stage
                def logits(self):
                    lg = bank(CB[1], (QT, NE), parts=T)
                    dve.wait_ge(s["b_lg_ps"], self.i + 1)
                    self.ch.link(V.tensor_reduce(rmax[0:T], lg, AX.X, ALU.max))
                    V.tensor_tensor(lgx[0:T], lg, over_e(rmax), ALU.subtract).then_inc(s["b_lmx"], 1)

                @optional_stage
                def choose(self):
                    c, ch = self.i, self.ch
                    dve.wait_ge(s["b_lexp"], c + 1)
                    ch.link(V.tensor_reduce(rsm[0:T], prob[0:T], AX.X, ALU.add))
                    ch.link(V.reciprocal(rinv[0:T], rsm[0:T]))
                    ch.link(V.tensor_tensor(prob[0:T], prob[0:T], over_e(rinv), ALU.mult))

                    def best(p, top, one):
                        ch.link(V.tensor_reduce(top[0:T], p[0:T], AX.X, ALU.max))
                        ch.link(V.tensor_tensor(hit[0:T], p[0:T], over_e(top), ALU.is_equal))
                        ch.link(V.tensor_tensor(cand[0:T], hit[0:T], rev, ALU.mult))
                        ch.link(V.tensor_reduce(first[0:T], cand[0:T], AX.X, ALU.max))
                        ch.link(V.tensor_tensor(one[0:T], rev, over_e(first), ALU.is_equal))

                    best(prob, top1, one1)
                    ch.link(V.scalar_tensor_tensor(rest[0:T], one1[0:T], -2.0, prob[0:T], ALU.mult, ALU.add))
                    best(rest, top2, one2)
                    V.tensor_tensor(both[0:T], one1[0:T], one2[0:T], ALU.add).then_inc(s["b_both"], 1)
                    ch.link(V.tensor_tensor(topsum[0:T], top1[0:T], top2[0:T], ALU.add))
                    ch.link(V.reciprocal(topsum[0:T], topsum[0:T]))
                    V.tensor_tensor(wtop[0:T, ds(2 * c, QT), 0], top1[0:T], topsum[0:T], ALU.mult)
                    V.tensor_tensor(wtop[0:T, ds(2 * c, QT), 1], top2[0:T], topsum[0:T], ALU.mult)

                @optional_stage
                def place(self):
                    c, ch = self.i, self.ch
                    cn = bank(CB[0], (3, NE), parts=T)
                    dve.wait_ge(s["b_cnt_ps"], c + 1)
                    ch.link(V.tensor_tensor(posn[0:T], cn[:, 0:2], over_t(run[0:T]), ALU.add))
                    V.tensor_tensor(run[0:T], run[0:T], cn[:, 2], ALU.add)
                    V.tensor_tensor(one1[0:T], one1[0:T], posn[0:T], ALU.mult)
                    ch.link(V.tensor_tensor(one2[0:T], one2[0:T], posn[0:T], ALU.mult))
                    V.tensor_reduce(dsum[0:T, 0], one1[0:T], AX.X, ALU.add)
                    ch.link(V.tensor_reduce(dsum[0:T, 1], one2[0:T], AX.X, ALU.add))
                    V.tensor_copy(dest[0:T, :, ds(2 * c, QT)], dsum[0:T])
                    V.tensor_copy(dnow[0:T], dsum[0:T]).then_inc(s["b_dest"], 1)
                    ch.end()

            def step(z, c, b, a):
                A, B1, Z, C1 = StageA(a), StageB(b), StageZ(z), StageC(c)
                B1.stats()
                C1.divide_context()
                B1.norm()
                Z.maxima(0)
                A.stats()
                Z.maxima(1)
                A.norm()
                C1.residual()
                Z.maxima(2)
                C1.second_norm()
                A.clip_qk()
                A.values()
                Z.maxima(3)
                Z.negate_split_max()
                C1.logits()
                A.quantize_scores()
                Z.spread_max()
                C1.choose()
                A.probs()
                B1.rope()
                C1.place()
                A.residual()
                Z.copy_context()

            dve.wait_ge(s["tok_h0"], NT // 2 + 1)
            dve.wait_ge(s["tok_h1"], NT // 2 + 1)
            V.memset(flat(Dm), 0.0)
            V.memset(flat(mx3), 0.0)
            pipeline(dve, step)

            ch = Chain(dve, s["m_dve"], 0, 30)
            V.memset(zer, 0.0).then_inc(s["m_zero"], 1)
            V.memset(ones8[0:T], 1.0)
            ch.link(V.tensor_tensor(cnt[0:T], run[0:T], const_at("ebase", T), ALU.subtract))
            V.tensor_copy(counts[0:1], cnt[0:1])
            ch.link(V.tensor_scalar(cnt_i[0:T], cnt[0:T], 127.0, None, ALU.add))
            ch.link(V.tensor_scalar(cnt_i[0:T], cnt_i[0:T], 7, None, ALU.arith_shift_right))
            ch.link(V.tensor_copy(ntil[0:T], cnt_i[0:T]))
            ch.link(V.tensor_tensor_scan(mend[0:T], ones8[0:T], ntil[0:T], 0.0, ALU.mult, ALU.add))
            tl = const_at("tile", 1)
            by_tile = tl.unsqueeze(2).to_broadcast([1, TILES, NE])
            by_e = lambda a: a[0:1].unsqueeze(1).to_broadcast([1, TILES, NE])
            ch.link(V.tensor_tensor(over[0:1], by_tile, by_e(mend), ALU.is_ge))
            ch.link(V.tensor_reduce(m_e[0:1], over[0:1], AX.X, ALU.add))
            ch.link(V.tensor_tensor(over2[0:1], over[0:1], by_e(ntil), ALU.mult))
            ch.link(V.tensor_reduce(m_st[0:1], over2[0:1], AX.X, ALU.add))
            V.tensor_scalar(tile_e[:], m_e[0:1], NE - 1.0, None, ALU.min)
            V.tensor_scalar(m_ok[0:1], m_e[0:1], NE - 0.5, None, ALU.is_lt)
            ch.link(V.tensor_tensor(m_st[0:1], tl, m_st[0:1], ALU.subtract))
            ch.link(V.tensor_scalar(m_e[0:1], m_e[0:1], float(REGION), None, ALU.mult))
            ch.link(V.scalar_tensor_tensor(m_row[0:1], m_st[0:1], 128.0, m_e[0:1], ALU.mult, ALU.add))
            ch.link(V.tensor_tensor(m_row[0:1], m_row[0:1], m_ok[0:1], ALU.mult))
            V.tensor_copy(tile_in[:], m_row[0:1]).then_inc(s["m_maps"], 1)

            def result_rows():
                nd = 2 * NT
                d = dest[0:T].rearrange("p k t -> p (k t)")
                ch.link(V.tensor_tensor(shift[0:T], mend[0:T], ntil[0:T], ALU.subtract))
                ch.link(V.scalar_tensor_tensor(shift[0:T], shift[0:T], 128.0, const_at("ebase", T), ALU.mult, ALU.subtract))
                V.tensor_copy(destf[0:T], d)
                V.tensor_copy(acc[0:T], d)
                ch.link(V.tensor_tensor(dshift[0:T, 1:NE], shift[0:T, 1:NE], shift[0:T, 0:NE - 1], ALU.subtract))
                for e in range(1, NE):
                    ch.link(V.tensor_scalar(term[0:T], destf[0:T], float(e * REGION), dshift[0:T, e:e + 1],
                                            ALU.is_ge, ALU.mult))
                    ch.link(V.tensor_tensor(acc[0:T], acc[0:T], term[0:T], ALU.add))
                V.tensor_copy(d, acc[0:T]).then_inc(s["m_dest"], 1)
                ch.end()

            def m_copy_x(par, use, i):
                dve.wait_ge((s["m_xT_ps0"], s["m_xT_ps1"])[par], use + 1)
                V.tensor_copy(flat(xTe), bank(2, (DC * 128,))).then_inc(s["m_xT"], 1)

            def m_gate(i, par):
                dve.wait_ge(s["m_silu"], i + 1)
                dve.wait_ge(s["m_u_ps"], i + 1)
                V.tensor_tensor(ga[par], gs, bank(1, (F,)), ALU.mult).then_inc(s["m_a"], 1)

            def m_copy_a(i):
                dve.wait_ge(s["m_aT_ps"], i + 1)
                V.tensor_copy(gaT[:, 2:4], bank(5, (2, 128))).then_inc(s["m_aT_dve"], 1)

            m_copy_x(0, 1, 0)
            m_gate(0, 0)
            m_copy_x(1, 1, 1)
            result_rows()
            with dve.Fori(0, (TILES - 2) // 2) as j:
                for par in (1, 0):
                    i = 2 * j + 2 - par
                    m_copy_a(i - 1)
                    m_gate(i, par)
                    m_copy_x(1 - par, j + 2, i + 1)
            m_copy_a(TILES - 2)
            m_gate(TILES - 1, 1)
            m_copy_a(TILES - 1)

            with dve.Fori(0, B // 2) as j:
                for par, (landed, got) in enumerate(((s["f_h0"], s["f_y0"]), (s["f_h1"], s["f_y1"]))):
                    i = 2 * j + par
                    ch = Chain(dve, s["f_dve"], i, 3)
                    w = wnow[par]
                    V.tensor_copy(w[0:T], wtop[0:T, ds(2 * i, QT), :]).then_inc(s["f_w"], 1)
                    dve.wait_ge(s["f_w"], i + 1)
                    dve.wait_ge(landed, j * 16 + 16)
                    dve.wait_ge(got, j * (16 * 2 * QT) + 16 * 2 * QT)
                    h = h2b[par]
                    for t in range(QT):
                        last = V.scalar_tensor_tensor(y1[par][0:T, t], y1[par][0:T, t], w[0:T, t, 0:1], h[0:T, t],
                                                      ALU.mult, ALU.add)
                    ch.link(last)
                    for t in range(QT):
                        last = V.scalar_tensor_tensor(h[0:T, t], y2[par][0:T, t], w[0:T, t, 1:2], y1[par][0:T, t],
                                                      ALU.mult, ALU.add)
                    ch.link(last)
                    ch.link(V.tensor_scalar(h[0:T], h[0:T], CLIP, -CLIP, ALU.min, ALU.max))
                    V.tensor_tensor(h[0:T], h[0:T], H[0:T, ds(2 * i, QT), :], ALU.add).then_inc(s["f_out"], 1)
                    ch.end()

        @block.gpsimd
        def _(po):
            P = nc.gpsimd
            half_ = mhalf[0:T]

            def take_wait(word=0):
                P.tensor_tensor(gate_p[:, word:word + 1], mhalf[0:1, 0:1], mhalf[0:1, 0:1], ALU.add)

            def rstd(i, ready, sm, at, to, done):
                po.wait_ge(ready, i + 1)
                P.tensor_tensor(sm[0:T, to:to + 2], sm[0:T, at:at + 2], half_, ALU.pow).then_inc(done, 1)

            def rms(i, ready, sm, step_done, done, at, to):
                po.wait_ge(ready, i + 1)
                P.tensor_tensor(sm[0:T, 12:14], sm[0:T, at:at + 2], epsc[0:T], ALU.add).then_inc(step_done, 1)
                po.wait_ge(step_done, i + 1)
                P.tensor_tensor(sm[0:T, to:to + 2], sm[0:T, 12:14], half_, ALU.pow).then_inc(done, 1)

            @optional
            def z_values(z):
                po.wait_ge(s["b_qkv"], z + 1)
                if later(z):
                    po.wait_ge(s["b_pv_ps"], z * NKV)
                take_wait(1)
                for g in range(NKV):
                    last = P.tensor_copy(vz[0:T, :, g, 32 * g:32 * g + HD],
                                         qkv[0:T, :, (NH + NKV + g) * HD:(NH + NKV + g + 1) * HD])
                last.then_inc(s["b_vz"], 1)

            @optional
            def b_rstd(b):
                rstd(b, s["b_var"], smB, 8, 10, s["b_rstd"])
                po.wait_ge(s["b_rstd"], b + 1)
                take_wait(2)
                P.tensor_copy(rstdB[0:T, ds(2 * b, QT)], smB[0:T, 10:12])
                P.tensor_copy(meanB[0:T, ds(2 * b, QT)], mvB[0:T, :, 0]).then_inc(s["b_mean"], 1)

            @optional
            def b_rms(b):
                rms(b, s["b_ms"], smB, s["q_pool"], s["b_r1"], 0, 2)

            @optional
            def b_rope_sin(b):
                po.wait_ge(s["b_qkv"], b + 1)
                heads, hh = NH + NKV, HD // 2
                src = qkv[0:T, :, 0:heads * HD].rearrange("p t (h d) -> p t h d", d=HD)
                dst = t2[0:T].rearrange("p t (h d) -> p t h d", d=HD)
                sin = const_at("sin", T).rearrange("p (t d) -> p t d", t=QT)
                for lo, hi in ((0, hh), (hh, 0)):
                    tab = sin[:, :, lo:lo + hh].unsqueeze(2).to_broadcast([T, QT, heads, hh])
                    last = P.tensor_tensor(dst[:, :, :, lo:lo + hh], src[:, :, :, hi:hi + hh], tab, ALU.mult)
                last.then_inc(s["b_sinpart"], 1)

            @optional
            def a_rstd(a):
                rstd(a, s["a_var"], smA, 8, 10, s["a_rstd"])

            @optional
            def c_stat(c):
                po.wait_ge(s["b_mean"], c + 1)
                take_wait(3)
                P.tensor_copy(smC[0:T, 8:10], meanB[0:T, ds(2 * c, QT)])
                P.tensor_copy(smC[0:T, 10:12], rstdB[0:T, ds(2 * c, QT)]).then_inc(s["c_stat"], 1)

            @optional
            def c_rms(c):
                rms(c, s["b_ms2"], smC, s["c_pool"], s["b_r2"], 0, 6)

            @optional
            def c_scatter(c):
                po.wait_ge(s["b_dest"], c + 1)
                take_wait()
                for k in range(TOPK):
                    for t in range(QT):
                        P.indirect_dma_start(out=x_rows, out_offset=bass.IndirectOffsetOnAxis(ap=dnow[0:T, k, t:t + 1], axis=0),
                                             in_=hn[0:T, t], in_offset=None).then_inc(s["b_scat"], 16)

            def step(z, c, b, a):
                z_values(z)
                c_stat(c)
                b_rstd(b)
                b_rms(b)
                a_rstd(a)
                c_rms(c)
                b_rope_sin(b)
                c_scatter(c)

            po.wait_ge(s["tok_h0"], NT // 2 + 1)
            po.wait_ge(s["tok_h1"], NT // 2 + 1)
            P.memset(vz[0:T], 0.0).then_inc(s["zeroed"], 1)
            po.wait_ge(s["zeroed"], 1)
            for g in range(NKV):
                P.memset(vz[0:T, :, g, 32 * g + HD:32 * g + HD + 1], 1.0)
            pipeline(po, step)

            po.wait_ge(s["m_dest"], 1)
            po.wait_ge(s["m_st0"], 16 * (TILES // 2 + 1))
            po.wait_ge(s["m_st1"], 16 * (TILES // 2 + 1))
            with po.Fori(0, B // 2) as j:
                for par, got in enumerate((s["f_y0"], s["f_y1"])):
                    i = 2 * j + par
                    po.wait_ge((s["f_st0"], s["f_st1"])[par], j * 16 + 16)
                    P.tensor_copy(gidx[par][0:T], dest[0:T, :, ds(2 * i, QT)]).then_inc(s["f_idx"], 1)
                    po.wait_ge(s["f_idx"], i + 1)
                    take_wait()
                    for k, y_ in enumerate((y1, y2)):
                        for t in range(QT):
                            P.indirect_dma_start(out=y_[par][0:T, t], out_offset=None, in_=y_rows,
                                                 in_offset=bass.IndirectOffsetOnAxis(ap=gidx[par][0:T, k, t:t + 1], axis=0)
                                                 ).then_inc(got, 16)


_INS = ["x", "L0_tok_W_h", "L0_tok_b_h", "L0_tok_W_o", "L0_tok_b_o", "L0_tok_W_r", "L0_tok_b_r", "L0_attn_Wq",
        "L0_attn_bq", "L0_attn_Wk", "L0_attn_bk", "L0_attn_Wv", "L0_attn_bv", "L0_ffn_ln1_w", "L0_ffn_ln2_w",
        "L0_ffn_Wq", "L0_ffn_Wk", "L0_ffn_Wv", "L0_ffn_Wo", "L0_ffn_Wr", "L0_ffn_Wg", "L0_ffn_Wu", "L0_ffn_Wd"]


def kernel(**inputs):
    import concourse.bacc as _bacc
    from concourse.bass_utils import run_bass_kernel_spmd as _run

    nc = _bacc.Bacc("TRN2", target_bir_lowering=False, num_devices=1)
    arrays, args = {}, []
    for name in _INS:
        a = np.ascontiguousarray(inputs[name])
        arrays[f"in_{name}"] = a
        args.append(nc.dram_tensor(f"in_{name}", a.shape, mybir.dt.from_np(a.dtype), kind="ExternalInput").ap())
    table, _ = constants()
    arrays["in_const"] = table
    args.append(nc.dram_tensor("in_const", table.shape, mybir.dt.float32, kind="ExternalInput").ap())
    args.append(nc.dram_tensor("out", (B, S, D), mybir.dt.float32, kind="ExternalOutput").ap())
    build(nc, *args)
    r = _run(nc, [arrays], core_ids=[0])
    return r.results[0]["out"]
```

```python
from contextlib import ExitStack

import numpy as np

import concourse.bass as bass
from concourse import mybir

B, SAMPLES, TOK = 16, 4000, 16
S = SAMPLES // TOK
QT = 2
T = S // QT
NT = B * QT
D, MID = 256, 1024
DC, MC = D // 128, MID // 128
NH, NKV, HD = 16, 4, 16
REP = NH // NKV
NE, F, TOPK = 8, 512, 2
FC = F // 128
PARTS = 6 * HD
STACK = PARTS + 3
QKV = (NH + 2 * NKV) * HD
EPS = 1e-5
CLIP = 100.0
F16MAX = 65504.0
NEG = -1e30
WS = 256.0
AS = 1.0 / 16

REGION = -(-(B * S + 128) // 128) * 128
TILES = (B * S * TOPK + NE * 127) // 128


def constants():
    t = {}
    p = np.arange(128)
    t["ident"] = np.eye(128)
    k = np.arange(T)
    t["mask_q"] = np.where(k[None, :] > p[:, None], NEG, 0.0)
    t["mask_k"] = np.where(k[None, :] < p[:, None], NEG, 0.0)
    t["before"] = (p[:, None] < k[None, :]).astype(float)
    pos = np.arange(S, dtype=np.float32)
    inv = (1.0 / np.float32(10000.0) ** (np.arange(0, HD, 2, dtype=np.float32) / np.float32(HD))).astype(np.float32)
    ang = pos[:, None] * inv
    cos, sin = np.cos(ang).astype(np.float32), np.sin(ang).astype(np.float32)
    for name, tab in (("cos", np.concatenate([cos, cos], 1)), ("sin", np.concatenate([-sin, sin], 1))):
        full = np.zeros((128, QT, HD), np.float32)
        full[:T] = tab.reshape(QT, T, HD).transpose(1, 0, 2)
        t[name] = full.reshape(128, -1)
    t["rev"] = np.tile(NE - np.arange(NE), (128, 1))
    t["ebase"] = np.tile(np.arange(NE) * REGION, (128, 1))
    row = p[:, None]
    head = row % NH
    real = row < 3 * NH
    t["delta"] = (real & (head % REP == np.arange(REP)[None, :])).astype(float)
    sel = real[:, :, None] & (head[:, :, None] // REP == np.arange(NKV)[None, :, None])
    t["sel"] = np.broadcast_to(sel, (128, NKV, T)).astype(float).reshape(128, -1)
    t["tile"] = np.tile(np.arange(TILES), (128, 1))
    where, cols, at = {}, [], 0
    for name, a in t.items():
        where[name] = (at, a.shape[1])
        cols.append(a.astype(np.float32))
        at += a.shape[1]
    return np.ascontiguousarray(np.concatenate(cols, 1)), where


def build(nc, x, tWh, tbh, tWo, tbo, tWr, tbr, aWq, abq, aWk, abk, aWv, abv, ln1, ln2, fWq, fWk, fWv, fWo,
          fWr, fWg, fWu, fWd, const, out):
    f32, f16, bf16 = mybir.dt.float32, mybir.dt.float16, mybir.dt.bfloat16
    i32 = mybir.dt.int32
    ALU, ACT, AX = mybir.AluOpType, mybir.ActivationFunctionType, mybir.AxisListType
    ds = bass.ds
    _, CO = constants()
    NC = const.shape[1]

    ctx = ExitStack()
    with ctx:
        def sb(name, shape, dt):
            return ctx.enter_context(nc.sbuf_tensor(name, shape, dt))

        def sem(name):
            return ctx.enter_context(nc.semaphore(name))

        x_rows = nc.dram_tensor("x_rows", (NE * REGION, D), f32, kind="Internal").ap()
        y_rows = nc.dram_tensor("y_rows", (TILES * 128, D), f32, kind="Internal").ap()
        h2_rows = nc.dram_tensor("h2_rows", (B, T, QT, D), f32, kind="Internal").ap()

        WH = sb("WH", [128, NE, DC, 2 * F], f16)
        WL = sb("WL", [128, NE, DC, 2 * F], f16)
        H = sb("H", [128, NT, D], f32)
        C = sb("C", [128, NC], f32)
        WatH, WatL = (sb(n, [128, DC, 3 * D], f16) for n in ("WatH", "WatL"))
        WqkvH, WqkvL = (sb(n, [128, DC, QKV], f16) for n in ("WqkvH", "WqkvL"))
        Wo = sb("Wo", [128, DC, D], f32)
        Wr = sb("Wr", [128, DC, NE], f32)
        bqk = sb("bqk", [128, 2, DC], f32)
        bv = sb("bv", [128, D], f32)
        w2b = sb("w2b", [128, D], f32)
        lnc = sb("lnc", [128, DC], f32)
        identb = sb("identb", [128, 128], bf16)
        identh = sb("identh", [128, 128], f16)
        maskqb = sb("maskqb", [128, T], bf16)
        maskkb = sb("maskkb", [128, T], bf16)
        beforeb = sb("beforeb", [128, T], bf16)
        onesb = sb("onesb", [128, T], bf16)
        selb = sb("selb", [128, NKV, T], bf16)
        onesf = sb("onesf", [128, 1], f32)
        mhalf = sb("mhalf", [128, 2], f32)
        epsc = sb("epsc", [128, 2, 2], f32)
        gate_v = sb("gate_v", [1, 2], f32)
        gate_p = sb("gate_p", [1, 4], f32)
        wtop = sb("wtop", [128, NT, 2], f32)
        dest = sb("dest", [128, 2, NT], i32)
        run = sb("run", [128, NE], f32)
        counts = sb("counts", [128, NE], i32)
        tile_e = sb("tile_e", [1, TILES], i32)
        tile_in = sb("tile_in", [1, TILES], i32)

        def const_at(name, parts=128):
            a, n = CO[name]
            return C[0:parts, a:a + n]

        ident = const_at("ident")

        WDW = NE * FC * D
        POOL = 14900 + WDW
        pool = sb("pool", [128, POOL], f32)
        WDH, WDL = (pool[:, n * WDW // 2:(n + 1) * WDW // 2].bitcast(f16).rearrange("p (e c d) -> p e c d", e=NE, c=FC)
                    for n in range(2))
        wraw = pool[:, 0:2 * F]

        class Carve:

            def __init__(self, at=0):
                self.at = at

            def __call__(self, shape, dt=f32):
                n = int(np.prod(shape))
                words = n if dt in (f32, i32) else (n + 1) // 2
                words += words % 2
                a = pool[:, self.at:self.at + words]
                self.at += words
                assert self.at <= POOL, self.at
                if dt != f32:
                    a = a.bitcast(dt)
                a = a[:, 0:n]
                if len(shape) == 2:
                    a = a.rearrange("p (a b) -> p a b", a=shape[0])
                elif len(shape) == 3:
                    a = a.rearrange("p (a b c) -> p a b c", a=shape[0], b=shape[1])
                return a

        c1 = Carve()
        hidH, hidL = ([c1((MC, 4 * T), f16) for _ in range(2)] for _ in range(2))
        hid = c1((4, 4 * T))
        WoT = c1((MC, D))
        WoH, WoL = c1((MC, D), f16), c1((MC, D), f16)
        Wst = c1((MID + D,), bf16)
        X = c1((NT, TOK))
        Wqkv = c1((DC, QKV))
        xst = c1((4, 128), bf16)
        xd = c1((4, TOK))
        xT = [c1((4 * T,), bf16) for _ in range(2)]
        Hf = H[:, :, :].rearrange("p t d -> p (t d)")
        rawW = Hf[:, 0:3 * DC * D].rearrange("p (w c h) -> p w c h", w=3, c=DC)
        raw0 = Hf[:, 2048:2048 + MID + D]
        raw1 = Hf[:, 3584:3584 + MID + D]
        rsum = Hf[:, 5120:5120 + MID + D]
        rbias = Hf[:, 6400:6400 + MID + 2 * D]
        WDf = pool[:, c1.at:]
        half = (MID + D) // 2
        sp_h, sp_m, sp_l, rp_h, rp_m, rp_l = (WDf[:, half * i:half * (i + 1)].bitcast(bf16) for i in range(6))
        sp_d = WDf[:, 6 * half:8 * half]
        c2 = Carve(WDW // 2)
        ca = Carve(c2.at)
        xn = c2((QT, D))
        att = ca((QT, S), f16)
        attT = ca((QT, S), f16)
        xnTH, xnTL = c2((DC, S), f16), c2((DC, S), f16)
        qk = c2((2 * DC, S), f16)
        vq = c2((QT, D), f16)
        sq = c2((QT, S), f16)
        ex = c2((QT, S))
        stA = c2((QT, 6))
        mvA = c2((QT, 2))
        smA = c2((16,))
        y = c2((QT, D))
        yTH, yTL = c2((DC, S), f16), c2((DC, S), f16)
        qkv = c2((QT, QKV))
        cx = c2((QT, D))
        cxT = c2((DC, S))
        hnT = cxT
        h2 = c2((QT, D))
        vz = c2((QT, NKV, 128))
        qst = c2((QT * NH, PARTS), bf16)
        kst = c2((QT * NKV, PARTS), bf16)
        QTs = c2((NH, S), bf16)
        CT = c2((REP, S))
        KTs = c2((NKV, S), bf16)
        Dm = c2((REP, S), bf16)
        PT = [c2((3, REP * T)) for _ in range(2)]
        t12 = c2((2 * QT, (NH + NKV) * HD))
        t1, t2 = t12[:, 0:QT], t12[:, QT:2 * QT]
        roq, rok = c2((QT * NH, HD)), c2((QT * NKV, HD))
        dq = roq
        dk = rok
        sqb, sqc = t1, cx
        hn = c2((QT, D))
        stB = c2((QT, 6))
        mvB = c2((QT, 2))
        smB = c2((16,))
        smC = c2((16,))
        meanB = c2((NT,))
        rstdB = c2((NT,))
        mxu = c2((3, NH))
        nmx = c2((QT, NH))
        dmx = c2((QT, NH))
        mx3 = c2((QT, 6 * NH), bf16)
        rcx = c2((QT, NH))
        lgx, prob, hit, cand, one1, one2, rest, posn = (c2((QT, NE)) for _ in range(8))
        rmax, rsm, rinv, top1, top2, first, topsum = (c2((QT,)) for _ in range(7))
        both = c2((QT, NE), bf16)
        dsum = c2((2, QT))
        dnow = c2((2, QT), i32)
        DRAW = (t12.rearrange("p t n -> p (t n)")[:, 0:FC * D], qst.bitcast(f32).rearrange("p h d -> p (h d)")[:, 0:FC * D])
        c4 = Carve(WDW)
        xin = [c4((D,)) for _ in range(2)]
        xTh, xTl = ([c4((DC, 128), f16) for _ in range(2)] for _ in range(2))
        gs = c4((F,))
        ga = [c4((F,)) for _ in range(2)]
        gaTh, gaTl = c4((FC, 128), f16), c4((FC, 128), f16)
        yo = [c4((D,)) for _ in range(2)]
        zer = c4((D,))
        over = c4((TILES, NE))
        over2 = c4((TILES, NE))
        m_e, m_st, m_ok, m_row = (c4((TILES,)) for _ in range(4))
        cnt, ntil, mend, ones8, shift, dshift = (c4((NE,)) for _ in range(6))
        destf, acc, term = (c4((2 * NT,)) for _ in range(3))
        cnt_i = c4((NE,), i32)
        c5 = Carve(c4.at)
        WAYS = 4
        y1, y2, h2b = ([c5((QT, D)) for _ in range(WAYS)] for _ in range(3))
        gidx = [c5((2, QT), i32) for _ in range(WAYS)]
        wnow = [c5((QT, 2)) for _ in range(WAYS)]

        banks = [ctx.enter_context(nc.psum_tensor(f"bank{i}", [128, 512], f32)) for i in range(8)]

        def bank(i, shape, dt=f32, parts=128):
            a = banks[i][0:parts, :]
            if dt != f32:
                a = a.bitcast(dt)
            a = a[:, 0:int(np.prod(shape))]
            if len(shape) == 2:
                a = a.rearrange("p (a b) -> p a b", a=shape[0])
            elif len(shape) == 3:
                a = a.rearrange("p (a b c) -> p a b c", a=shape[0], b=shape[1])
            return a

        YB, CB, VB, RING = (1, 2), (0, 7), (3, 4), (5, 6)

        names = """ld_const ld_x ld_tok ld_bias ld_attn ld_ffn ld_vec ld_wgu w_high w_split d_high d_split ld_wd0 ld_wd1 stacked
        setup_dve setup_consts setup_wt_ps setup_wt_high setup_wt setup_scaled setup_fold setup_wo_high setup_wo csum_ps split_rows split_bias zeroed
        tok_dve tok_split tok_xT_ps tok_xT tok_hid_ps tok_hid tok_low tok_out_ps tok_h0 tok_h1
        a_dve a_st a_var a_rstd a_xn a_xnT_ps a_xnT_high a_xnT a_q_ps a_k_ps a_v_ps a_q16 a_k16 a_qk a_v a_s_ps a_nmx a_exp a_att
        a_attT_ps a_attT a_av_ps a_h1
        q_dve r_dve z_dve c_dve q_pool c_pool b_mean b_var b_rstd b_y b_ms b_r1 b_yT_ps b_yT_high b_yT b_qkv_ps b_qkv b_vz b_sinpart b_stacks
        b_T_ps b_T b_s_ps b_s_max b_mx3 b_mx3T_ps b_D b_st_ps b_exp b_pv_ps
        b_CT_act b_CT_dve b_ct_ps b_cx b_cxT_ps b_cxT b_o_ps c_stat c_y b_h2 b_h2_st b_ms2 b_r2 b_hn b_hnT_ps b_hnT
        b_lg_ps b_lmx b_lexp b_both b_cnt_ps b_dest b_scat b_hn_free
        m_dve m_counts m_maps m_dest m_zero m_fill m_x0 m_x1 m_xT_ps0 m_xT_ps1 m_xT_high m_xT m_g_ps m_u_ps m_silu m_a m_aT_ps m_aT_high
        m_aT m_y_ps m_y m_st0 m_st1
        f_h0 f_h1 f_h2 f_h3 f_idx f_w f_dve f_y0 f_y1 f_y2 f_y3 f_out f_st0 f_st1 f_st2 f_st3"""
        s = {n: sem(n) for n in names.split()}

        class Chain:

            def __init__(self, eng, step, i, n):
                self.eng, self.step, self.i, self.n, self.k = eng, step, i, n, 0

            def link(self, ins):
                ins.then_inc(self.step, 1)
                self.k += 1
                assert self.k <= self.n, "more links than stated"
                self.eng.wait_ge(self.step, self.i * self.n + self.k)

            def end(self):
                assert self.k == self.n, (self.k, self.n)

        def optional(stage):
            return lambda n, *more: None if n is None else stage(n, *more)

        def later(n):
            return not isinstance(n, int) or n > 0

        LAST = B - 1

        def pipeline(eng, step):
            step(None, None, None, 0, 1)
            step(None, None, 0, 1, 2)
            step(0, None, 1, 2, 3)
            with eng.Fori(1, B - 3) as z:
                step(z, z - 1, z + 1, z + 2, z + 3)
            step(B - 3, B - 4, B - 2, B - 1)
            step(B - 2, B - 3, B - 1, None)
            step(LAST, B - 2, None, None)
            step(None, B - 1, None, None)

        DOWN = [*range(2, NE), 0, 1]

        block = ctx.enter_context(nc.Block())
        NPAIR = B // 2
        TOK_CHUNKS = ((0, 1, 2, 3), (4, 5), (6, 7), ())
        BLOCKS = ((0, 0), (1, 0), (1, 1))
        UNITS = len(BLOCKS) * NKV

        def flat(a):
            return a.rearrange("p a b -> p (a b)")

        def tile_of(a, i):
            return flat(a[0:T, ds(i, 1), :])

        @block.sync
        def _(sp):
            nkv = NKV * HD
            row = lambda v: v.rearrange("(o n) -> o n", o=1)
            for free, n in ((s["tok_h0"], 1), (s["tok_h1"], 1), (s["b_h2_st"], 16), (s["b_hn_free"], 1), (s["m_y"], 1),
                            (s["m_xT_ps0"], 1), (s["m_xT_ps1"], 1), (s["m_st0"], 16), (s["m_st1"], 16), *((s[f"f_st{n}"], 16) for n in range(WAYS))):
                sp.sem_inc(free, n)
            sp.dma_start(C[:], const).then_inc(s["ld_const"], 16)
            sp.dma_start(raw0[0:TOK, 0:MID], tWh[0:TOK, :]).then_inc(s["ld_tok"], 16)
            sp.dma_start(raw0[0:TOK, MID:MID + D], tWr[0:TOK, :]).then_inc(s["ld_tok"], 16)
            sp.dma_start(raw1[0:TOK, 0:MID], tWh[TOK:2 * TOK, :]).then_inc(s["ld_tok"], 16)
            sp.dma_start(raw1[0:TOK, MID:MID + D], tWr[TOK:2 * TOK, :]).then_inc(s["ld_tok"], 16)
            sp.dma_start(rbias[0:1, 0:MID], row(tbh)).then_inc(s["ld_bias"], 16)
            sp.dma_start(rbias[0:1, MID:MID + D], row(tbo)).then_inc(s["ld_bias"], 16)
            sp.dma_start(rbias[0:1, MID + D:MID + 2 * D], row(tbr)).then_inc(s["ld_bias"], 16)
            sp.dma_start(X[0:T], x.rearrange("b (t p d) -> p (b t) d", t=QT, d=TOK)).then_inc(s["ld_x"], 16)
            sp.dma_start(WoT[:], tWo.rearrange("(c p) d -> p c d", p=128)).then_inc(s["ld_tok"], 16)
            for w, a in enumerate((aWq, aWk, aWv)):
                sp.dma_start(rawW[:, w], a.rearrange("(c p) h -> p c h", p=128)).then_inc(s["ld_attn"], 16)
            for i, v in enumerate((abq, abk)):
                sp.dma_start(bqk[:, i, :], v.rearrange("(c p) -> p c", p=128), allow_slow_non_contiguous=True).then_inc(s["ld_vec"], 16)
            sp.dma_start(lnc[:], ln1.rearrange("(c p) -> p c", p=128), allow_slow_non_contiguous=True).then_inc(s["ld_vec"], 16)
            sp.dma_start(bv[:], row(abv).to_broadcast([128, D])).then_inc(s["ld_vec"], 16)
            sp.dma_start(w2b[:], row(ln2).to_broadcast([128, D])).then_inc(s["ld_vec"], 16)
            sp.dma_start(Wqkv[:, :, 0:D], fWq.rearrange("(c p) n -> p c n", p=128)).then_inc(s["ld_ffn"], 16)
            sp.dma_start(Wqkv[:, :, D:D + nkv], fWk.rearrange("(c p) n -> p c n", p=128)).then_inc(s["ld_ffn"], 16)
            sp.dma_start(Wqkv[:, :, D + nkv:QKV], fWv.rearrange("(c p) n -> p c n", p=128)).then_inc(s["ld_ffn"], 16)
            sp.dma_start(Wo[:], fWo.rearrange("(c p) n -> p c n", p=128)).then_inc(s["ld_ffn"], 16)
            sp.dma_start(Wr[:], fWr.rearrange("(c p) n -> p c n", p=128)).then_inc(s["ld_ffn"], 16)
            sp.wait_ge(s["split_rows"], 1)
            for i, part in enumerate((sp_h, sp_m, sp_l, sp_h, sp_m, sp_h)):
                sp.dma_start(Wst[TOK * i:TOK * (i + 1), :], part[0:TOK, :]).then_inc(s["stacked"], 16)
            sp.wait_ge(s["split_bias"], 1)
            for i, part in enumerate((rp_h, rp_m, rp_l)):
                sp.dma_start(Wst[PARTS + i:PARTS + i + 1, :], part[0:1, :]).then_inc(s["stacked"], 16)
            sp.wait_ge(s["tok_h0"], NT // 2 + 1)
            sp.wait_ge(s["tok_h1"], NT // 2 + 1)
            by_chunk = lambda w, n: w.rearrange("e (c p) f -> (e c) p f", p=128)[ds(n, 1)].rearrange("o p f -> (o p) f")

            def load_raw(n):
                sp.dma_start(wraw[:, 0:F], by_chunk(fWg, n)).then_inc(s["ld_wgu"], 16)
                sp.dma_start(wraw[:, F:2 * F], by_chunk(fWu, n)).then_inc(s["ld_wgu"], 16)

            load_raw(0)

            def keep_h2(c):
                sp.wait_ge(s["b_h2"], c + 1)
                sp.dma_start(h2_rows[ds(c, 1)].rearrange("o p t d -> (o p) t d"), h2[0:T]).then_inc(s["b_h2_st"], 16)

            def free_hn(c):
                sp.wait_ge(s["b_scat"], c * (16 * 2 * QT) + 16 * 2 * QT)
                sp.sem_inc(s["b_hn_free"], 1)

            with sp.Fori(0, B - 2) as c:
                sp.wait_ge(s["w_split"], c + 1)
                load_raw(c + 1)
                keep_h2(c)
                free_hn(c)
            sp.wait_ge(s["w_split"], B - 1)
            load_raw(B - 1)
            sp.wait_ge(s["a_h1"], B)
            sp.wait_ge(s["b_stacks"], B)
            sp.wait_ge(s["b_vz"], B)

            def load_down(n):
                if n == 1:
                    sp.wait_ge(s["b_T_ps"], B * 5)
                if n >= 2:
                    sp.wait_ge(s["d_split"], n - 1)
                sp.dma_start(DRAW[n % 2].rearrange("p (c d) -> p c d", c=FC),
                             fWd[DOWN[n]].rearrange("(c p) d -> p c d", p=128)).then_inc(s[f"ld_wd{n % 2}"], 16)

            for n in range(3):
                load_down(n)
            keep_h2(B - 2)
            for n in range(3, NE):
                load_down(n)
            free_hn(B - 2)
            keep_h2(B - 1)

            sp.wait_ge(s["m_counts"], 1)
            sp.wait_ge(s["m_zero"], 1)
            for e in range(NE // 2):
                n = sp.value_load(counts[0:1, e:e + 1], min_val=0, max_val=B * S)
                sp.dma_start(x_rows[ds(n + e * REGION, 128), :], zer[:]).then_inc(s["m_fill"], 16)
            sp.wait_ge(s["m_fill"], 16 * NE)
            sp.wait_ge(s["b_scat"], 16 * 2 * QT * B)
            sp.wait_ge(s["m_maps"], 1)
            with sp.Fori(0, TILES // 2) as j:
                for par, (landed, used) in enumerate(((s["m_x0"], s["m_xT_ps0"]), (s["m_x1"], s["m_xT_ps1"]))):
                    sp.wait_ge(used, j + 1)
                    r = sp.value_load(tile_in[0:1, ds(2 * j + par, 1)], min_val=0, max_val=NE * REGION - 128)
                    sp.dma_start(xin[par], x_rows[ds(r, 128), :]).then_inc(landed, 16)

            sp.wait_ge(s["b_h2_st"], 16 * B + 16)
            def load_h2(j, way):
                sp.wait_ge(s[f"f_st{way}"], 16 * j + 16)
                sp.dma_start(h2b[way][0:T],
                             h2_rows[ds(WAYS * j + way, 1)].rearrange("o p t d -> (o p) t d")).then_inc(s[f"f_h{way}"], 16)

            def store(j, way):
                sp.wait_ge(s["f_out"], WAYS * j + (way + 1))
                sp.dma_start(out[ds(WAYS * j + way, 1)].rearrange("o (t p) d -> p (o t) d", t=QT),
                             h2b[way][0:T]).then_inc(s[f"f_st{way}"], 16)

            for way in range(WAYS - 1):
                load_h2(0, way)
            with sp.Fori(0, B // WAYS - 1) as j:
                for way in range(WAYS):
                    load_h2(j + (way + WAYS - 1) // WAYS, (way + WAYS - 1) % WAYS)
                    store(j, way)
            load_h2(B // WAYS - 1, WAYS - 1)
            for way in range(WAYS):
                store(B // WAYS - 1, way)
            for way in range(WAYS):
                sp.wait_ge(s[f"f_st{way}"], 16 * (B // WAYS + 1))

        @block.tensor
        def _(pe):
            mm = nc.tensor.matmul
            tr = nc.tensor.transpose
            pe.wait_ge(s["ld_tok"], 16 * 5)
            pe.wait_ge(s["setup_consts"], 1)
            for i, (a, n) in enumerate(((0, 512), (512, 512), (MID, D))):
                last = mm(bank(i, (512,))[0:1, 0:n], onesf[0:TOK, 0:1], raw1[0:TOK, a:a + n], start=True, stop=True)
            last.then_inc(s["csum_ps"], 1)
            pe.wait_ge(s["ld_attn"], 16 * 3)
            for w in range(3):
                for hc in range(DC):
                    for oc in range(DC):
                        last = tr(bank(3 + w, (DC, DC, 128))[:, hc, oc], rawW[:, w, oc, 128 * hc:128 * (hc + 1)], ident)
            last.then_inc(s["setup_wt_ps"], 1)
            pe.wait_ge(s["setup_wt"], 1)
            pe.wait_ge(s["split_bias"], 1)
            pe.wait_ge(s["stacked"], 16 * 9)

            def tok_x(i, par):
                pe.wait_ge(s["tok_split"], i + 1)
                for q in range(4):
                    last = tr(bank(0, (4, 128), bf16)[0:STACK, q, 0:T], xst[0:T, q, 0:STACK], identb[0:T, 0:T])
                last.then_inc(s["tok_xT_ps"], 1)

            def tok_hidden(i, par, m):
                if m == 0:
                    pe.wait_ge(s["tok_xT"], i + 1)
                if not (isinstance(i, int) and 8 * i + m - 3 <= 0):
                    pe.wait_ge(s["tok_hid"], i * 8 + (m - 3))
                mm(bank(1 + m % 4, (4 * T,)), Wst[0:STACK, 128 * m:128 * (m + 1)], xT[par][0:STACK, :],
                   start=True, stop=True).then_inc(s["tok_hid_ps"], 1)

            def tok_out(i, par, q):
                if q == 0:
                    pe.wait_ge(s["tok_low"], i * 8 + 8)
                pe.wait_ge((s["tok_h0"], s["tok_h1"])[q % 2], i * 2 + (q // 2 + 1))
                o = bank(5 + q % 2, (D,), parts=T)
                for m in range(MC):
                    for n, (hp, wp) in enumerate(((hidH, WoH), (hidH, WoL), (hidL, WoH))):
                        mm(o, hp[par][:, m, T * q:T * (q + 1)], wp[:, m, :], start=(m == 0 and n == 0), stop=False)
                mm(o, xT[par][0:STACK, T * q:T * (q + 1)], Wst[0:STACK, MID:MID + D],
                   start=False, stop=True).then_inc(s["tok_out_ps"], 1)

            def tok_both(i, par):
                tok_x(i, par)
                for q in range(4):
                    tok_out(i - 1, 1 - par, q)
                    for m in TOK_CHUNKS[q]:
                        tok_hidden(i, par, m)

            tok_x(0, 0)
            for m in range(MC):
                tok_hidden(0, 0, m)
            pe.wait_ge(s["setup_wo"], 1)
            with pe.Fori(0, (NPAIR - 2) // 2) as j:
                tok_both(2 * j + 1, 1)
                tok_both(2 * j + 2, 0)
            tok_both(NPAIR - 1, 1)
            for q in range(4):
                tok_out(NPAIR - 1, 1, q)

            @optional
            def a_transpose(a):
                pe.wait_ge(s["a_xn"], a + 1)
                if later(a):
                    pe.wait_ge(s["b_qkv"], a)
                for t in range(QT):
                    for c in range(DC):
                        last = tr(bank(YB[0], (DC, S))[:, c, T * t:T * (t + 1)], xn[0:T, t, 128 * c:128 * (c + 1)],
                                  ident[0:T, 0:T])
                last.then_inc(s["a_xnT_ps"], 1)

            def a_project(w, at, done, halves=range(DC)):
                for o in halves:
                    for c in range(DC):
                        for n, (wp, xp) in enumerate(((WatH, xnTH), (WatL, xnTH), (WatH, xnTL))):
                            last = mm(bank(at, (DC, S))[:, o], wp[:, c, D * w + 128 * o:D * w + 128 * (o + 1)],
                                      xp[:, c], start=(c == 0 and n == 0), stop=(c == DC - 1 and n == 2))
                if DC - 1 in halves:
                    last.then_inc(done, 1)

            @optional
            def a_project_q(a):
                pe.wait_ge(s["a_xnT"], a + 1)
                a_project(0, YB[1], s["a_q_ps"])

            @optional
            def a_project_k(a, half):
                a_project(1, YB[0], s["a_k_ps"], [half])

            @optional
            def a_project_v(a):
                pe.wait_ge(s["a_q16"], a + 1)
                for t in range(QT):
                    for c in range(DC):
                        for n, (xp, wp) in enumerate(((xnTH, WatH), (xnTH, WatL), (xnTL, WatH))):
                            last = mm(bank(YB[1], (QT, D), parts=T)[:, t], xp[:, c, T * t:T * (t + 1)], wp[:, c, 2 * D:3 * D],
                                      start=(c == 0 and n == 0), stop=(c == DC - 1 and n == 2))
                last.then_inc(s["a_v_ps"], 1)

            @optional
            def a_scores(a):
                pe.wait_ge(s["a_qk"], a + 1)
                for t in range(QT):
                    for c in range(DC):
                        last = mm(bank(YB[0], (QT, S), parts=T)[:, t], qk[:, c, T * t:T * (t + 1)], qk[:, DC + c],
                                  start=(c == 0), stop=(c == DC - 1))
                last.then_inc(s["a_s_ps"], 1)

            @optional
            def a_transpose_probs(a):
                pe.wait_ge(s["a_v"], a + 1)
                pe.wait_ge(s["a_att"], a + 1)
                for k in range(QT):
                    for t in range(QT):
                        last = tr(bank(YB[1], (QT, QT, 128), f16, T)[:, k, t, 0:T], att[0:T, t, T * k:T * (k + 1)],
                                  identh[0:T, 0:T])
                last.then_inc(s["a_attT_ps"], 1)

            @optional
            def a_values(a):
                pe.wait_ge(s["a_attT"], a + 1)
                for t in range(QT):
                    for k in range(QT):
                        last = mm(bank(YB[0], (QT, D), parts=T)[:, t], attT[0:T, k, T * t:T * (t + 1)], vq[0:T, k],
                                  start=(k == 0), stop=(k == QT - 1))
                last.then_inc(s["a_av_ps"], 1)

            @optional
            def b_transpose(b):
                pe.wait_ge(s["b_y"], b + 1)
                for t in range(QT):
                    for c in range(DC):
                        last = tr(bank(YB[1], (DC, S))[:, c, T * t:T * (t + 1)], y[0:T, t, 128 * c:128 * (c + 1)],
                                  ident[0:T, 0:T])
                last.then_inc(s["b_yT_ps"], 1)

            @optional
            def b_project(b):
                pe.wait_ge(s["b_yT"], b + 1)
                for t in range(QT):
                    for c in range(DC):
                        for n, (yp, wp) in enumerate(((yTH, WqkvH), (yTH, WqkvL), (yTL, WqkvH))):
                            last = mm(bank(YB[t], (QKV,), parts=T), yp[:, c, T * t:T * (t + 1)], wp[:, c],
                                      start=(c == 0 and n == 0), stop=(c == DC - 1 and n == 2))
                last.then_inc(s["b_qkv_ps"], 1)

            @optional
            def z_transpose_stacks(z, f):
                if f == 0:
                    pe.wait_ge(s["b_stacks"], z + 1)
                if f >= 2:
                    pe.wait_ge(s["b_T"], z * 5 + (f - 1))
                o = bank(CB[f % 2], (4, QT, 128), bf16, PARTS)
                for h in range(4):
                    for t in range(QT):
                        src = kst[0:T, NKV * t + h] if f == 0 else qst[0:T, NH * t + REP * (f - 1) + h]
                        last = tr(o[:, h, t, 0:T], src, identb[0:T, 0:T])
                last.then_inc(s["b_T_ps"], 1)

            @optional
            def z_scores(z, *units):
                for n in units:
                    g, (t, k) = n // 3, BLOCKS[n % 3]
                    if n % 3 == 0:
                        pe.wait_ge(s["b_T"], z * 5 + (g + 2))
                    if n >= 2:
                        pe.wait_ge(s["b_s_max"], z * UNITS + (n - 1))
                    o = bank(RING[n % 2], (REP, T), parts=T)
                    if t == k:
                        mm(flat(o), identb[0:T, 0:T], maskqb[0:T, :].unsqueeze(1).to_broadcast([T, REP, T]),
                           start=True, stop=False, skip_group_check=True)
                    for j in range(REP):
                        last = mm(o[:, j], QTs[0:PARTS, REP * g + j, T * t:T * (t + 1)], KTs[0:PARTS, g, T * k:T * (k + 1)],
                                  start=(t != k), stop=True, skip_group_check=True)
                    last.then_inc(s["b_s_ps"], 1)

            @optional
            def z_transpose_max(z):
                pe.wait_ge(s["b_mx3"], z + 1)
                for t in range(QT):
                    last = tr(bank(CB[1], (QT, 128), bf16)[0:6 * NH, t, 0:T], mx3[0:T, t], identb[0:T, 0:T])
                last.then_inc(s["b_mx3T_ps"], 1)

            @optional
            def z_scores_shifted(z, n):
                g, (t, k) = n // 3, BLOCKS[n % 3]
                if n == 0:
                    pe.wait_ge(s["b_D"], z + 1)
                if n >= 2:
                    pe.wait_ge(s["b_exp"], z * UNITS + (n - 1))
                o = bank(RING[n % 2], (REP * T,), parts=T)
                if t == k:
                    mm(o, identb[0:T, 0:T], maskkb[0:T, :].unsqueeze(1).to_broadcast([T, REP, T]),
                       start=True, stop=False)
                mm(o, KTs[0:PARTS, g, T * k:T * (k + 1)], QTs[0:PARTS, REP * g:REP * (g + 1), T * t:T * (t + 1)],
                   start=(t != k), stop=False)
                mm(o, selb[:, g], Dm[:, :, T * t:T * (t + 1)], start=False, stop=True).then_inc(s["b_st_ps"], 1)

            @optional
            def z_weigh_values(z, n):
                g, (t, k) = n // 3, BLOCKS[n % 3]
                pe.wait_ge(s["b_exp"], z * UNITS + (n + 1))
                if n == 0:
                    pe.wait_ge(s["b_vz"], z + 1)
                    if later(z):
                        pe.wait_ge(s["b_lmx"], z)
                mm(bank(VB[t], (REP * T,)), vz[0:T, k, g], PT[g % 2][0:T, n % 3],
                   start=(g == 0 and k == 0), stop=(g == NKV - 1 and t == k)).then_inc(s["b_pv_ps"], 1)

            @optional
            def z_shift_and_weigh(z, first, last):
                for n in range(first, last):
                    if n < UNITS:
                        z_scores_shifted(z, n)
                    if n >= 2:
                        z_weigh_values(z, n - 2)

            @optional
            def c_context_back(c):
                pe.wait_ge(s["b_CT_act"], c + 1)
                pe.wait_ge(s["b_CT_dve"], c + 1)
                for t in range(QT):
                    for j in range(REP):
                        last = tr(bank(VB[t], (REP, 128), parts=T)[:, j], CT[:, j, T * t:T * (t + 1)], ident)
                    last.then_inc(s["b_ct_ps"], 1)

            @optional
            def c_transpose_context(c):
                pe.wait_ge(s["b_cx"], c + 1)
                for t in range(QT):
                    for k in range(DC):
                        last = tr(bank(VB[0], (DC, S))[:, k, T * t:T * (t + 1)], cx[0:T, t, 128 * k:128 * (k + 1)],
                                  ident[0:T, 0:T])
                last.then_inc(s["b_cxT_ps"], 1)

            @optional
            def c_output(c):
                pe.wait_ge(s["b_cxT"], c + 1)
                for t in range(QT):
                    for k in range(DC):
                        last = mm(bank(VB[1], (QT, D), parts=T)[:, t], cxT[:, k, T * t:T * (t + 1)], Wo[:, k],
                                  start=(k == 0), stop=(k == DC - 1))
                last.then_inc(s["b_o_ps"], 1)

            @optional
            def c_transpose_hn(c):
                pe.wait_ge(s["b_hn"], c + 1)
                for t in range(QT):
                    for k in range(DC):
                        last = tr(bank(VB[0], (DC, S))[:, k, T * t:T * (t + 1)], hn[0:T, t, 128 * k:128 * (k + 1)],
                                  ident[0:T, 0:T])
                last.then_inc(s["b_hnT_ps"], 1)

            @optional
            def c_logits(c):
                pe.wait_ge(s["b_hnT"], c + 1)
                for t in range(QT):
                    for k in range(DC):
                        last = mm(bank(VB[1], (QT, NE), parts=T)[:, t], hnT[:, k, T * t:T * (t + 1)], Wr[:, k],
                                  start=(k == 0), stop=(k == DC - 1))
                last.then_inc(s["b_lg_ps"], 1)

            @optional
            def c_count(c):
                pe.wait_ge(s["b_both"], c + 1)
                o = bank(CB[0], (3, NE), parts=T)
                mm(o[:, 0], beforeb[0:T, :], both[0:T, 0], start=True, stop=True)
                mm(o[:, 1], onesb[0:T, :], both[0:T, 0], start=True, stop=False)
                mm(o[:, 1], beforeb[0:T, :], both[0:T, 1], start=False, stop=True)
                mm(o[:, 2], onesb[0:T, :], both[0:T, 0], start=True, stop=False)
                mm(o[:, 2], onesb[0:T, :], both[0:T, 1], start=False, stop=True).then_inc(s["b_cnt_ps"], 1)

            def step(z, c, b, a, n=None):
                z_scores(z, 0, 1)
                z_transpose_stacks(z, 2)
                c_context_back(c)
                b_transpose(b)
                z_scores(z, 2)
                z_transpose_stacks(z, 3)
                c_transpose_context(c)
                z_scores(z, 3, 4)
                b_project(b)
                z_scores(z, 5)
                c_output(c)
                a_transpose(a)
                z_scores(z, 6)
                z_transpose_stacks(z, 4)
                z_scores(z, 7)
                a_project_q(a)
                z_scores(z, 8, 9)
                a_project_k(a, 0)
                z_scores(z, 10)
                a_project_k(a, 1)
                z_scores(z, 11)
                a_project_v(a)
                c_transpose_hn(c)
                z_transpose_max(z)
                c_logits(c)
                a_scores(a)
                z_shift_and_weigh(z, 0, 6)
                c_count(c)
                z_shift_and_weigh(z, 6, 9)
                a_transpose_probs(a)
                z_shift_and_weigh(z, 9, 12)
                a_values(a)
                if b is not None and c is not None:
                    pe.wait_ge(s["b_dest"], c + 1)
                z_transpose_stacks(b, 0)
                z_transpose_stacks(b, 1)
                z_shift_and_weigh(z, 12, UNITS + 2)

            pe.wait_ge(s["setup_fold"], 1)
            pe.wait_ge(s["ld_ffn"], 16 * 5)
            pipeline(pe, step)

            G, U, XT, AT, Y = 0, 1, 2, (3, 5), 4

            def m_transpose_x(par, use):
                pe.wait_ge((s["m_x0"], s["m_x1"])[par], use * 16)
                for c in range(DC):
                    last = tr(bank(XT, (DC, 128))[:, c], xin[par][:, 128 * c:128 * (c + 1)], ident)
                last.then_inc((s["m_xT_ps0"], s["m_xT_ps1"])[par], 1)

            def m_up(i, par, e, which):
                if which == 0:
                    pe.wait_ge(s["m_xT"], i + 1)
                    pe.wait_ge(s["m_silu"], i)
                else:
                    pe.wait_ge(s["m_a"], i)
                for c in range(DC):
                    for n, (xp, wp) in enumerate(((xTh[par], WH), (xTh[par], WL), (xTl[par], WH))):
                        last = mm(bank((G, U)[which], (F,)), xp[:, c], flat(wp[:, ds(e, 1), c, F * which:F * (which + 1)]),
                                  start=(c == 0 and n == 0), stop=(c == DC - 1 and n == 2))
                last.then_inc((s["m_g_ps"], s["m_u_ps"])[which], 1)

            def m_transpose_a(i, par):
                pe.wait_ge(s["m_a"], i + 1)
                for c in range(FC):
                    last = tr(bank(AT[c // 2], (2, 128))[:, c % 2], ga[par][:, 128 * c:128 * (c + 1)], ident)
                last.then_inc(s["m_aT_ps"], 1)

            def m_down(i, e):
                pe.wait_ge(s["m_aT"], i + 1)
                pe.wait_ge(s["m_y"], i + 1)
                for c in range(FC):
                    for n, (ap, wp) in enumerate(((gaTh, WDH), (gaTh, WDL), (gaTl, WDH))):
                        last = mm(bank(Y, (D,)), ap[:, c], flat(wp[:, ds(e, 1), c, :]),
                                  start=(c == 0 and n == 0), stop=(c == FC - 1 and n == 2))
                last.then_inc(s["m_y_ps"], 1)

            def expert(i):
                return pe.value_load(tile_e[0:1, ds(i, 1)], min_val=0, max_val=NE - 1)

            def m_first_half(i, par, use, e):
                m_up(i, par, e, 0)
                if later(i):
                    m_transpose_a(i - 1, 1 - par)
                if use is not None:
                    pe.wait_ge(s["m_xT"], i + 1)
                    m_transpose_x(1 - par, use)
                m_up(i, par, e, 1)

            pe.wait_ge(s["w_split"], NE * DC)
            pe.wait_ge(s["d_split"], NE)
            pe.wait_ge(s["m_maps"], 1)
            m_transpose_x(0, 1)
            m_first_half(0, 0, 1, expert(0))
            m_first_half(1, 1, 2, expert(1))

            def m_four_steps(j, last=False):
                e = {0: expert(4 * j), 2: expert(4 * j + 2)}
                for k in range(1, 5):
                    m_down(4 * j + (k - 1), e[k - 1])
                    m_first_half(4 * j + (k + 1), (k + 1) % 2, None if last and k == 4 else 2 * j + (k + 4) // 2, e[k + 1])
                    for n in {1: (1, 3), 2: (4,), 3: (5,), 4: ()}[k]:
                        e[n] = expert(4 * j + n)

            with pe.Fori(0, (TILES - 2) // 4 - 1) as j:
                m_four_steps(j)
            m_four_steps((TILES - 2) // 4 - 1, last=True)
            m_down(TILES - 2, expert(TILES - 2))
            m_transpose_a(TILES - 1, 1)
            m_down(TILES - 1, expert(TILES - 1))

        @block.scalar
        def _(act):
            A = nc.scalar.activation
            def tok_copy_x(i, par):
                act.wait_ge(s["tok_xT_ps"], i + 1)
                A(xT[par][0:STACK, :].rearrange("p (q n) -> p q n", q=4), bank(0, (4, 128), bf16)[0:STACK, :, 0:T],
                  ACT.Copy).then_inc(s["tok_xT"], 1)

            def tok_silu(i, par):
                for m in range(MC):
                    if later(i) or m >= 4:
                        act.wait_ge(s["tok_low"], i * 8 + (m - 3))
                    act.wait_ge(s["tok_hid_ps"], i * 8 + (m + 1))
                    A(hid[:, m % 4], bank(1 + m % 4, (4 * T,)), ACT.Silu)
                    A(hidH[par][:, m], bank(1 + m % 4, (4 * T,)), ACT.Silu).then_inc(s["tok_hid"], 1)

            act.wait_ge(s["ld_tok"], 16 * 5)
            A(flat(WoH), flat(WoT), ACT.Copy, scale=WS).then_inc(s["setup_wo_high"], 1)
            tok_copy_x(0, 0)
            tok_silu(0, 0)
            with act.Fori(0, (NPAIR - 2) // 2) as j:
                for par in (1, 0):
                    i = 2 * j + 2 - par
                    tok_copy_x(i, par)
                    tok_silu(i, par)
            tok_copy_x(NPAIR - 1, 1)
            tok_silu(NPAIR - 1, 1)

            @optional
            def a_copy_x(a):
                act.wait_ge(s["a_xnT_ps"], a + 1)
                A(flat(xnTH), bank(YB[0], (DC * S,)), ACT.Copy).then_inc(s["a_xnT_high"], 1)

            @optional
            def a_bias(a):
                for w, (at, ready, done) in enumerate(((YB[1], s["a_q_ps"], s["a_q16"]), (YB[0], s["a_k_ps"], s["a_k16"]))):
                    act.wait_ge(ready, a + 1)
                    for o in range(DC):
                        last = A(qk[:, DC * w + o], bank(at, (DC, S))[:, o], ACT.Identity, bias=bqk[:, w, o:o + 1],
                                 scale=1.0 / WS)
                    last.then_inc(done, 1)

            @optional
            def a_exps(a):
                act.wait_ge(s["a_nmx"], a + 1)
                for t in range(QT):
                    last = A(ex[0:T, t], sq[0:T, t], ACT.Exp, bias=smA[0:T, t:t + 1], accum_out=smA[0:T, 2 + t:3 + t])
                last.then_inc(s["a_exp"], 1)

            @optional
            def a_copy_probs(a):
                act.wait_ge(s["a_attT_ps"], a + 1)
                A(attT[0:T].rearrange("p k (t n) -> p (k t) n", t=QT), bank(YB[1], (QT * QT, 128), f16, T)[:, :, 0:T],
                  ACT.Copy).then_inc(s["a_attT"], 1)

            @optional
            def b_squares(b):
                act.wait_ge(s["b_y"], b + 1)
                for t in range(QT):
                    last = A(sqb[0:T, t, 0:D], y[0:T, t], ACT.Square, scale=WS * float(D) ** -0.5, accum_out=smB[0:T, t:t + 1])
                last.then_inc(s["b_ms"], 1)

            @optional
            def b_copy_y(b):
                act.wait_ge(s["b_yT_ps"], b + 1)
                A(flat(yTH), bank(YB[1], (DC * S,)), ACT.Copy).then_inc(s["b_yT_high"], 1)

            @optional
            def b_scale_qkv(b):
                act.wait_ge(s["b_qkv_ps"], b + 1)
                act.wait_ge(s["b_r1"], b + 1)
                if later(b):
                    act.wait_ge(s["b_vz"], b)
                for t in range(QT):
                    last = A(qkv[0:T, t], bank(YB[t], (QKV,), parts=T), ACT.Copy, scale=smB[0:T, 2 + t:3 + t])
                last.then_inc(s["b_qkv"], 1)

            @optional
            def z_copy_stack(z, f):
                act.wait_ge(s["b_T_ps"], z * 5 + (f + 1))
                dst = KTs[0:PARTS] if f == 0 else QTs[0:PARTS, REP * (f - 1):REP * f]
                A(dst.rearrange("p h (t n) -> p (h t) n", t=QT), bank(CB[f % 2], (4 * QT, 128), bf16, PARTS)[:, :, 0:T],
                  ACT.Copy).then_inc(s["b_T"], 1)

            @optional
            def z_exps(z, first, last):
                for n in range(first, last):
                    if n >= 6:
                        act.wait_ge(s["b_pv_ps"], z * UNITS + (n - 5))
                    act.wait_ge(s["b_st_ps"], z * UNITS + (n + 1))
                    A(PT[n // 3 % 2][0:T, n % 3], bank(RING[n % 2], (REP * T,), parts=T), ACT.Exp,
                      scale=float(HD) ** -0.5).then_inc(s["b_exp"], 1)

            @optional
            def z_copy_context(z):
                act.wait_ge(s["b_pv_ps"], z * UNITS + (UNITS - 2))
                A(CT[:, :, 0:T], bank(VB[0], (REP, T)), ACT.Copy).then_inc(s["b_CT_act"], 1)

            @optional
            def c_copy_cx(c):
                act.wait_ge(s["b_cxT_ps"], c + 1)
                A(flat(cxT), bank(VB[0], (DC * S,)), ACT.Copy).then_inc(s["b_cxT"], 1)

            @optional
            def c_squares(c):
                act.wait_ge(s["b_h2"], c + 1)
                for t in range(QT):
                    last = A(sqc[0:T, t], h2[0:T, t], ACT.Square, scale=float(D) ** -0.5, accum_out=smC[0:T, t:t + 1])
                last.then_inc(s["b_ms2"], 1)

            @optional
            def c_copy_hn(c):
                act.wait_ge(s["b_hnT_ps"], c + 1)
                A(flat(hnT), bank(VB[0], (DC * S,)), ACT.Copy).then_inc(s["b_hnT"], 1)

            @optional
            def c_route_exp(c):
                act.wait_ge(s["b_lmx"], c + 1)
                A(prob[0:T], lgx[0:T], ACT.Exp).then_inc(s["b_lexp"], 1)

            @optional
            def w_first_part(n):
                act.wait_ge(s["ld_wgu"], n * 32 + 32)
                A(WH[:, :, :, :].rearrange("p e c f -> p (e c) f")[:, ds(n, 1), :].rearrange("p o f -> p (o f)"), wraw, ACT.Copy, scale=WS).then_inc(s["w_high"], 1)

            def d_first_part(z, n):
                if z is LAST:
                    act.wait_ge(s[f"ld_wd{n % 2}"], 16 * (n // 2) + 16)
                    if n == NE - 2:
                        act.wait_ge(s["w_split"], NE * DC)
                    A(WDH[:, DOWN[n]].rearrange("p c d -> p (c d)"), DRAW[n % 2],
                      ACT.Copy, scale=WS).then_inc(s["d_high"], 1)

            def step(z, c, b, a, n=None):
                z_copy_stack(z, 2)
                b_squares(b)
                b_copy_y(b)
                z_copy_stack(z, 3)
                c_copy_cx(c)
                d_first_part(z, 0)
                b_scale_qkv(b)
                a_copy_x(a)
                c_squares(c)
                z_copy_stack(z, 4)
                d_first_part(z, 1)
                a_bias(a)
                c_copy_hn(c)
                c_route_exp(c)
                d_first_part(z, 2)
                z_exps(z, 0, 4)
                a_exps(a)
                d_first_part(z, 3)
                z_exps(z, 4, 6)
                d_first_part(z, 4)
                z_exps(z, 6, 8)
                w_first_part(z)
                d_first_part(z, 5)
                z_exps(z, 8, 9)
                a_copy_probs(a)
                z_exps(z, 9, 10)
                d_first_part(z, 6)
                z_exps(z, 10, UNITS)
                z_copy_stack(b, 0)
                z_copy_stack(b, 1)
                z_copy_context(z)
                d_first_part(z, 7)

            act.wait_ge(s["ld_vec"], 16 * 5)
            act.wait_ge(s["tok_h0"], NT // 2 + 1)
            act.wait_ge(s["tok_h1"], NT // 2 + 1)
            pipeline(act, step)

            def m_silu(i):
                act.wait_ge(s["m_g_ps"], i + 1)
                act.wait_ge(s["m_a"], i)
                A(gs, bank(0, (F,)), ACT.Silu, scale=1.0 / WS).then_inc(s["m_silu"], 1)

            def m_copy_a(i):
                act.wait_ge(s["m_aT_ps"], i + 1)
                for n in range(2):
                    A(gaTh[:, 2 * n:2 * n + 2], bank((3, 5)[n], (2, 128)), ACT.Copy).then_inc(s["m_aT_high"], 1)

            def m_out(i, par, use):
                act.wait_ge(s["m_y_ps"], i + 1)
                act.wait_ge((s["m_st0"], s["m_st1"])[par], use * 16 + 16)
                A(yo[par], bank(4, (D,)), ACT.Copy, scale=1.0 / (AS * WS)).then_inc(s["m_y"], 1)
                act.wait_ge(s["m_y"], i + 2)
                act.dma_start(y_rows[ds(128 * i, 128), :], yo[par]).then_inc((s["m_st0"], s["m_st1"])[par], 16)

            act.wait_ge(s["m_counts"], 1)
            act.wait_ge(s["m_zero"], 1)
            for e in range(NE // 2, NE):
                n = act.value_load(counts[0:1, e:e + 1], min_val=0, max_val=B * S)
                act.dma_start(x_rows[ds(n + e * REGION, 128), :], zer[:]).then_inc(s["m_fill"], 16)
            act.wait_ge(s["m_maps"], 1)
            m_silu(0)
            with act.Fori(0, (TILES - 2) // 2) as j:
                for par in (1, 0):
                    i = 2 * j + 2 - par
                    m_copy_a(i - 1)
                    m_silu(i)
                    m_out(i - 1, 1 - par, j if par == 1 else j)
            m_copy_a(TILES - 2)
            m_silu(TILES - 1)
            m_out(TILES - 2, 0, TILES // 2 - 1)
            m_copy_a(TILES - 1)
            m_out(TILES - 1, 1, TILES // 2 - 1)

        @block.vector
        def _(dve):
            V = nc.vector
            ch = Chain(dve, s["setup_dve"], 0, 10)
            V.memset(onesf[:], 1.0)
            V.memset(onesb[:], 1.0)
            V.memset(mhalf[:], -0.5)
            V.memset(epsc[:, 0], EPS)
            V.memset(epsc[:, 1], EPS * WS * WS)
            V.memset(xst[:], 1.0)
            dve.wait_ge(s["ld_const"], 16)
            V.tensor_copy(identb[:], ident)
            V.tensor_copy(identh[:], ident)
            V.tensor_copy(maskqb[:], const_at("mask_q"))
            V.tensor_copy(maskkb[:], const_at("mask_k"))
            V.tensor_copy(beforeb[:], const_at("before"))
            V.tensor_copy(flat(selb), const_at("sel"))
            V.tensor_copy(run[:], const_at("ebase")).then_inc(s["setup_consts"], 1)
            dve.wait_ge(s["ld_tok"], 16 * 5)
            w0, d0 = raw0[0:TOK], sp_d[0:TOK]
            ch.link(V.tensor_scalar(w0[:, MID:], w0[:, MID:], WS, None, ALU.mult))
            ch.link(V.tensor_copy(sp_h[0:TOK], w0))
            ch.link(V.tensor_tensor(d0, w0, sp_h[0:TOK], ALU.subtract))
            ch.link(V.tensor_copy(sp_m[0:TOK], d0))
            V.tensor_tensor(sp_l[0:TOK], d0, sp_m[0:TOK], ALU.subtract).then_inc(s["split_rows"], 1)
            dve.wait_ge(s["ld_x"], 16)

            def tok_split(i):
                if not isinstance(i, int):
                    dve.wait_ge(s["tok_xT_ps"], i)
                elif i > 0:
                    dve.wait_ge(s["tok_xT_ps"], i)
                ch = Chain(dve, s["tok_dve"], i, 3)
                xi = X[0:T, ds(4 * i, 4), :]
                part = lambda n: xst[0:T, :, TOK * n:TOK * (n + 1)]
                ch.link(V.tensor_copy(part(0), xi))
                V.tensor_copy(part(1), part(0))
                V.tensor_copy(part(2), part(0))
                ch.link(V.tensor_tensor(xd[0:T], xi, part(0), ALU.subtract))
                ch.link(V.tensor_copy(part(3), xd[0:T]))
                ch.end()
                V.tensor_copy(part(4), part(3))
                V.tensor_tensor(part(5), xd[0:T], part(3), ALU.subtract).then_inc(s["tok_split"], 1)

            tok_split(0)
            dve.wait_ge(s["ld_bias"], 16 * 3)
            dve.wait_ge(s["csum_ps"], 1)
            for i, (a, n) in enumerate(((0, 512), (512, 512), (MID, D))):
                last = V.tensor_tensor(rsum[0:1, a:a + n], bank(i, (512,))[0:1, 0:n], rbias[0:1, a:a + n], ALU.add)
            ch.link(last)
            ch.link(V.tensor_tensor(rsum[0:1, MID:], rsum[0:1, MID:], rbias[0:1, MID + D:], ALU.add))
            ch.link(V.tensor_scalar(rsum[0:1, MID:], rsum[0:1, MID:], WS, None, ALU.mult))
            r0, d1 = rsum[0:1], sp_d[0:1]
            ch.link(V.tensor_copy(rp_h[0:1], r0))
            ch.link(V.tensor_tensor(d1, r0, rp_h[0:1], ALU.subtract))
            ch.link(V.tensor_copy(rp_m[0:1], d1))
            ch.end()
            V.tensor_tensor(rp_l[0:1], d1, rp_m[0:1], ALU.subtract).then_inc(s["split_bias"], 1)
            dve.wait_ge(s["setup_wt_ps"], 1)
            for w in range(3):
                last = V.tensor_scalar(WatH[:, :, D * w:D * (w + 1)], bank(3 + w, (DC, D)), WS, None, ALU.mult)
            last.then_inc(s["setup_wt_high"], 1)
            dve.wait_ge(s["setup_wt_high"], 1)
            for w in range(3):
                last = V.scalar_tensor_tensor(WatL[:, :, D * w:D * (w + 1)], bank(3 + w, (DC, D)), WS,
                                              WatH[:, :, D * w:D * (w + 1)], ALU.mult, ALU.subtract)
            last.then_inc(s["setup_wt"], 1)

            def tok_second_part(i, par, m):
                dve.wait_ge(s["tok_hid"], i * 8 + (m + 1))
                V.tensor_tensor(hidL[par][:, m], hid[:, m % 4], hidH[par][:, m], ALU.subtract).then_inc(s["tok_low"], 1)

            def tok_copy(i, q):
                dve.wait_ge(s["tok_out_ps"], i * 4 + (q + 1))
                V.tensor_scalar(tile_of(H, 4 * i + q), bank(5 + q % 2, (D,), parts=T), 1.0 / WS, None,
                                ALU.mult).then_inc((s["tok_h0"], s["tok_h1"])[q % 2], 1)

            def tok_both(i, par, more=True):
                for q in range(4):
                    if q == 2 and more:
                        tok_split(i + 1)
                    tok_copy(i - 1, q)
                    for m in TOK_CHUNKS[q]:
                        tok_second_part(i, par, m)

            dve.wait_ge(s["setup_wo_high"], 1)
            V.scalar_tensor_tensor(flat(WoL), flat(WoT), WS, flat(WoH), ALU.mult, ALU.subtract).then_inc(s["setup_wo"], 1)
            for m in range(MC):
                if m == 1:
                    tok_split(1)
                tok_second_part(0, 0, m)
            dve.wait_ge(s["ld_ffn"], 16 * 5)
            dve.wait_ge(s["ld_vec"], 16 * 5)
            for c in range(DC):
                last = V.tensor_scalar(Wqkv[:, c], Wqkv[:, c], lnc[:, c:c + 1], WS, ALU.mult, ALU.mult)
            last.then_inc(s["setup_scaled"], 1)
            dve.wait_ge(s["setup_scaled"], 1)
            V.tensor_copy(flat(WqkvH), flat(Wqkv)).then_inc(s["setup_scaled"], 1)
            dve.wait_ge(s["setup_scaled"], 2)
            V.tensor_tensor(flat(WqkvL), flat(Wqkv), flat(WqkvH), ALU.subtract).then_inc(s["setup_fold"], 1)
            with dve.Fori(0, (NPAIR - 2) // 2) as j:
                tok_both(2 * j + 1, 1)
                tok_both(2 * j + 2, 0)
            tok_both(NPAIR - 1, 1, more=False)
            for q in range(4):
                tok_copy(NPAIR - 1, q)

            def stats(ch, i, st, mv, sm, src, done):
                for t in range(QT):
                    last = V.bn_stats(st[0:T, t], tile_of(src, 2 * i + t))
                ch.link(last)
                V.memset(gate_v[:, 0:1], 0.0)
                for t in range(QT):
                    last = V.bn_aggr(mv[0:T, t], st[0:T, t])
                ch.link(last)
                V.tensor_scalar(sm[0:T, 8:10], mv[0:T, :, 1], EPS, None, ALU.add).then_inc(done, 1)

            def normed(i, mv, sm, src, dst, done):
                for t in range(QT):
                    last = V.tensor_scalar(dst[0:T, t], tile_of(src, 2 * i + t), mv[0:T, t, 0:1], sm[0:T, 10 + t:11 + t],
                                           ALU.subtract, ALU.mult)
                last.then_inc(done, 1)

            def clip16(a):
                return V.tensor_scalar(a, a, F16MAX, -F16MAX, ALU.min, ALU.max)

            def optional_stage(stage):
                return lambda self, *more: None if self.i is None else stage(self, *more)

            class StageA:
                def __init__(self, i):
                    self.i, self.ch_stats, self.ch = i, Chain(dve, s["a_st"], i, 2), Chain(dve, s["a_dve"], i, 4)

                @optional_stage
                def stats(self):
                    stats(self.ch_stats, self.i, stA, mvA, smA, H, s["a_var"])
                    self.ch_stats.end()

                @optional_stage
                def norm(self):
                    dve.wait_ge(s["a_rstd"], self.i + 1)
                    normed(self.i, mvA, smA, H, xn, s["a_xn"])

                @optional_stage
                def second_part(self):
                    dve.wait_ge(s["a_xnT_high"], self.i + 1)
                    V.tensor_tensor(flat(xnTL), bank(YB[0], (DC * S,)), flat(xnTH), ALU.subtract).then_inc(s["a_xnT"], 1)

                @optional_stage
                def values(self):
                    dve.wait_ge(s["a_v_ps"], self.i + 1)
                    self.ch.link(V.scalar_tensor_tensor(vq[0:T], bank(YB[1], (QT, D), parts=T), 1.0 / WS,
                                                        bv[0:T].unsqueeze(1).to_broadcast([T, QT, D]), ALU.mult, ALU.add))
                    clip16(vq[0:T]).then_inc(s["a_v"], 1)

                @optional_stage
                def clip_qk(self):
                    dve.wait_ge(s["a_k16"], self.i + 1)
                    clip16(flat(qk)).then_inc(s["a_qk"], 1)

                @optional_stage
                def quantize_scores(self):
                    dve.wait_ge(s["a_s_ps"], self.i + 1)
                    self.ch.link(V.tensor_scalar(flat(sq[0:T]), bank(YB[0], (QT * S,), parts=T), float(D) ** -0.5, F16MAX,
                                                 ALU.mult, ALU.min))
                    self.ch.link(V.tensor_scalar(flat(sq[0:T]), flat(sq[0:T]), -F16MAX, None, ALU.max))
                    V.tensor_reduce(smA[0:T, 0:QT], sq[0:T], AX.X, ALU.max, negate=True).then_inc(s["a_nmx"], 1)

                @optional_stage
                def probs(self):
                    dve.wait_ge(s["a_exp"], self.i + 1)
                    self.ch.link(V.reciprocal(smA[0:T, 4:6], smA[0:T, 2:4]))
                    for t in range(QT):
                        last = V.tensor_scalar(att[0:T, t], ex[0:T, t], smA[0:T, 4 + t:5 + t], None, ALU.mult)
                    last.then_inc(s["a_att"], 1)

                @optional_stage
                def residual(self):
                    dve.wait_ge(s["a_av_ps"], self.i + 1)
                    h = H[0:T, ds(2 * self.i, QT), :]
                    V.tensor_tensor(h, h, bank(YB[0], (QT, D), parts=T), ALU.add).then_inc(s["a_h1"], 1)
                    self.ch.end()

            class StageB:
                def __init__(self, i):
                    self.i, self.ch_stats, self.ch = i, Chain(dve, s["q_dve"], i, 2), Chain(dve, s["r_dve"], i, 5)

                @optional_stage
                def stats(self):
                    dve.wait_ge(s["a_h1"], self.i + 1)
                    V.memset(gate_v[:, 1:2], 0.0)
                    stats(self.ch_stats, self.i, stB, mvB, smB, H, s["b_var"])
                    self.ch_stats.end()

                @optional_stage
                def norm(self):
                    dve.wait_ge(s["b_rstd"], self.i + 1)
                    normed(self.i, mvB, smB, H, y, s["b_y"])

                @optional_stage
                def second_part(self):
                    dve.wait_ge(s["b_yT_high"], self.i + 1)
                    V.tensor_tensor(flat(yTL), bank(YB[1], (DC * S,)), flat(yTH), ALU.subtract).then_inc(s["b_yT"], 1)

                @optional_stage
                def rope(self):
                    b, ch = self.i, self.ch
                    dve.wait_ge(s["b_qkv"], b + 1)
                    if later(b):
                        dve.wait_ge(s["b_T_ps"], b * 5)
                    heads = NH + NKV
                    hv = lambda a: a.rearrange("p t (h d) -> p t h d", d=HD)
                    cos = const_at("cos", T).rearrange("p (t d) -> p t d", t=QT).unsqueeze(2).to_broadcast([T, QT, heads, HD])
                    ch.link(V.tensor_tensor(hv(t1[0:T]), hv(qkv[0:T, :, 0:heads * HD]), cos, ALU.mult))
                    dve.wait_ge(s["b_sinpart"], b + 1)
                    two = lambda a: a.rearrange("p (t h) d -> p t (h d)", t=QT)
                    V.tensor_tensor(two(rok[0:T]), t1[0:T, :, NH * HD:], t2[0:T, :, NH * HD:], ALU.add)
                    ch.link(V.tensor_tensor(two(roq[0:T]), t1[0:T, :, 0:NH * HD], t2[0:T, :, 0:NH * HD], ALU.add))
                    Q = lambda n, m=1: qst[0:T, :, HD * n:HD * (n + m)]
                    K = lambda n, m=1: kst[0:T, :, HD * n:HD * (n + m)]
                    V.tensor_copy(Q(0), roq[0:T])
                    ch.link(V.tensor_copy(K(0), rok[0:T]))
                    V.tensor_tensor(dk[0:T], rok[0:T], K(0), ALU.subtract)
                    V.tensor_tensor(dq[0:T], roq[0:T], Q(0), ALU.subtract)
                    V.tensor_copy(Q(1), Q(0))
                    ch.link(V.tensor_copy(Q(2), Q(0)))
                    V.tensor_copy(K(1), dk[0:T])
                    ch.link(V.tensor_copy(Q(3), dq[0:T]))
                    V.tensor_tensor(K(2), dk[0:T], K(1), ALU.subtract)
                    V.tensor_tensor(Q(5), dq[0:T], Q(3), ALU.subtract)
                    V.tensor_copy(Q(4), Q(3))
                    V.tensor_copy(K(3, 2), K(0, 2))
                    V.tensor_copy(K(5), K(0)).then_inc(s["b_stacks"], 1)
                    ch.end()

            class StageZ:
                def __init__(self, i):
                    self.i, self.ch = i, Chain(dve, s["z_dve"], i, 5)

                @optional_stage
                def maxima(self, *units):
                    for n in units:
                        g = n // 3
                        dve.wait_ge(s["b_s_ps"], self.i * UNITS + (n + 1))
                        V.tensor_reduce(mxu[0:T, n % 3, REP * g:REP * (g + 1)], bank(RING[n % 2], (REP, T), parts=T), AX.X,
                                        ALU.max).then_inc(s["b_s_max"], 1)

                @optional_stage
                def negate_split_max(self):
                    z, ch = self.i, self.ch
                    dve.wait_ge(s["b_s_max"], z * UNITS + UNITS)
                    ch.link(V.tensor_tensor(mxu[0:T, 1], mxu[0:T, 1], mxu[0:T, 2], ALU.max))
                    part = lambda n: mx3[0:T, :, NH * n:NH * (n + 1)]
                    ch.link(V.tensor_scalar(nmx[0:T], mxu[0:T, 0:2], -1.0, None, ALU.mult))
                    ch.link(V.tensor_copy(part(0), nmx[0:T]))
                    ch.link(V.tensor_tensor(dmx[0:T], nmx[0:T], part(0), ALU.subtract))
                    ch.link(V.tensor_copy(part(1), dmx[0:T]))
                    V.tensor_tensor(part(2), dmx[0:T], part(1), ALU.subtract).then_inc(s["b_mx3"], 1)
                    ch.end()

                @optional_stage
                def spread_max(self):
                    dve.wait_ge(s["b_mx3T_ps"], self.i + 1)
                    n = 3 * NH
                    src = bank(CB[1], (QT, 128), bf16)[0:n, :, 0:T].unsqueeze(1).to_broadcast([n, REP, QT, T])
                    which = const_at("delta", n).unsqueeze(2).unsqueeze(3).to_broadcast([n, REP, QT, T])
                    V.tensor_tensor(Dm[0:n].rearrange("p j (t n) -> p j t n", t=QT), src, which,
                                    ALU.mult).then_inc(s["b_D"], 1)

                @optional_stage
                def copy_context(self):
                    dve.wait_ge(s["b_pv_ps"], self.i * UNITS + UNITS)
                    V.tensor_copy(CT[:, :, T:S], bank(VB[1], (REP, T))).then_inc(s["b_CT_dve"], 1)

            @optional
            def w_second_part(n):
                dve.wait_ge(s["w_high"], n + 1)
                part = lambda w: w[:, :, :, :].rearrange("p e c f -> p (e c) f")[:, ds(n, 1), :].rearrange("p o f -> p (o f)")
                V.scalar_tensor_tensor(part(WL), wraw, WS, part(WH), ALU.mult, ALU.subtract).then_inc(s["w_split"], 1)

            def d_second_part(z, n):
                if z is LAST:
                    dve.wait_ge(s["d_high"], n + 1)
                    part = lambda w: w[:, DOWN[n]].rearrange("p c d -> p (c d)")
                    V.scalar_tensor_tensor(part(WDL), DRAW[n % 2], WS, part(WDH), ALU.mult, ALU.subtract).then_inc(s["d_split"], 1)

            over_e = lambda a: a[0:T].unsqueeze(2).to_broadcast([T, QT, NE])
            over_t = lambda a: a.unsqueeze(1).to_broadcast([T, QT, NE])
            rev = over_t(const_at("rev", T))

            class StageC:
                def __init__(self, i):
                    self.i, self.ch = i, Chain(dve, s["c_dve"], i, 23)

                @optional_stage
                def divide_context(self):
                    c, ch = self.i, self.ch
                    for t in range(QT):
                        dve.wait_ge(s["b_ct_ps"], c * QT + (t + 1))
                        src = bank(VB[t], (REP, NKV, 32), parts=T)
                        rc = rcx[0:T, t].rearrange("p (j g) -> p j g", j=REP)
                        ch.link(V.reciprocal(rc, src[:, :, :, HD]))
                        last = V.tensor_tensor(cx[0:T, t].rearrange("p (g j d) -> p j g d", g=NKV, j=REP),
                                               src[:, :, :, 0:HD], rc.unsqueeze(3).to_broadcast([T, REP, NKV, HD]), ALU.mult)
                    last.then_inc(s["b_cx"], 1)

                @optional_stage
                def normed_input(self):
                    c = self.i
                    dve.wait_ge(s["c_stat"], c + 1)
                    dve.wait_ge(s["b_h2_st"], c * 16 + 16)
                    for t in range(QT):
                        last = V.tensor_scalar(h2[0:T, t], tile_of(H, 2 * c + t), smC[0:T, 8 + t:9 + t],
                                               smC[0:T, 10 + t:11 + t], ALU.subtract, ALU.mult)
                    last.then_inc(s["c_y"], 1)

                @optional_stage
                def residual(self):
                    c, ch = self.i, self.ch
                    dve.wait_ge(s["c_y"], c + 1)
                    dve.wait_ge(s["b_o_ps"], c + 1)
                    ch.link(V.tensor_tensor(h2[0:T], h2[0:T], bank(VB[1], (QT, D), parts=T), ALU.add))
                    V.tensor_scalar(h2[0:T], h2[0:T], CLIP, -CLIP, ALU.min, ALU.max).then_inc(s["b_h2"], 1)

                @optional_stage
                def second_norm(self):
                    dve.wait_ge(s["b_r2"], self.i + 1)
                    dve.wait_ge(s["b_hn_free"], self.i + 1)
                    for t in range(QT):
                        last = V.scalar_tensor_tensor(hn[0:T, t], h2[0:T, t], smC[0:T, 6 + t:7 + t], w2b[0:T],
                                                      ALU.mult, ALU.mult)
                    last.then_inc(s["b_hn"], 1)

                @optional_stage
                def logits(self):
                    lg = bank(VB[1], (QT, NE), parts=T)
                    dve.wait_ge(s["b_lg_ps"], self.i + 1)
                    self.ch.link(V.tensor_reduce(rmax[0:T], lg, AX.X, ALU.max))
                    V.tensor_tensor(lgx[0:T], lg, over_e(rmax), ALU.subtract).then_inc(s["b_lmx"], 1)

                @optional_stage
                def choose(self):
                    c, ch = self.i, self.ch
                    dve.wait_ge(s["b_lexp"], c + 1)
                    ch.link(V.tensor_reduce(rsm[0:T], prob[0:T], AX.X, ALU.add))
                    ch.link(V.reciprocal(rinv[0:T], rsm[0:T]))
                    ch.link(V.tensor_tensor(prob[0:T], prob[0:T], over_e(rinv), ALU.mult))

                    def best(p, top, one):
                        ch.link(V.tensor_reduce(top[0:T], p[0:T], AX.X, ALU.max))
                        ch.link(V.tensor_tensor(hit[0:T], p[0:T], over_e(top), ALU.is_equal))
                        ch.link(V.tensor_tensor(cand[0:T], hit[0:T], rev, ALU.mult))
                        ch.link(V.tensor_reduce(first[0:T], cand[0:T], AX.X, ALU.max))
                        ch.link(V.tensor_tensor(one[0:T], rev, over_e(first), ALU.is_equal))

                    best(prob, top1, one1)
                    ch.link(V.scalar_tensor_tensor(rest[0:T], one1[0:T], -2.0, prob[0:T], ALU.mult, ALU.add))
                    best(rest, top2, one2)
                    V.tensor_tensor(both[0:T], one1[0:T], one2[0:T], ALU.add).then_inc(s["b_both"], 1)
                    ch.link(V.tensor_tensor(topsum[0:T], top1[0:T], top2[0:T], ALU.add))
                    ch.link(V.reciprocal(topsum[0:T], topsum[0:T]))
                    V.tensor_tensor(wtop[0:T, ds(2 * c, QT), 0], top1[0:T], topsum[0:T], ALU.mult)
                    V.tensor_tensor(wtop[0:T, ds(2 * c, QT), 1], top2[0:T], topsum[0:T], ALU.mult)

                @optional_stage
                def place(self):
                    c, ch = self.i, self.ch
                    cn = bank(CB[0], (3, NE), parts=T)
                    dve.wait_ge(s["b_cnt_ps"], c + 1)
                    ch.link(V.tensor_tensor(posn[0:T], cn[:, 0:2], over_t(run[0:T]), ALU.add))
                    V.tensor_tensor(run[0:T], run[0:T], cn[:, 2], ALU.add)
                    V.tensor_tensor(one1[0:T], one1[0:T], posn[0:T], ALU.mult)
                    ch.link(V.tensor_tensor(one2[0:T], one2[0:T], posn[0:T], ALU.mult))
                    V.tensor_reduce(dsum[0:T, 0], one1[0:T], AX.X, ALU.add)
                    ch.link(V.tensor_reduce(dsum[0:T, 1], one2[0:T], AX.X, ALU.add))
                    V.tensor_copy(dest[0:T, :, ds(2 * c, QT)], dsum[0:T])
                    V.tensor_copy(dnow[0:T], dsum[0:T]).then_inc(s["b_dest"], 1)
                    ch.end()

            def step(z, c, b, a, n=None):
                A, B1, Z, C1 = StageA(a), StageB(b), StageZ(z), StageC(c)
                B1.norm()
                Z.maxima(0)
                C1.divide_context()
                Z.maxima(1, 2)
                B1.second_part()
                Z.maxima(3, 4)
                A.norm()
                Z.maxima(5)
                C1.residual()
                A.second_part()
                Z.maxima(6, 7)
                d_second_part(z, 0)
                C1.second_norm()
                Z.maxima(8, 9, 10, 11)
                Z.negate_split_max()
                A.clip_qk()
                Z.spread_max()
                C1.logits()
                d_second_part(z, 1)
                A.quantize_scores()
                A.values()
                C1.choose()
                d_second_part(z, 2)
                A.probs()
                B1.rope()
                d_second_part(z, 3)
                C1.place()
                d_second_part(z, 4)
                w_second_part(z)
                d_second_part(z, 5)
                StageA(n).stats()
                StageC(z).normed_input()
                A.residual()
                StageB(a).stats()
                d_second_part(z, 6)
                Z.copy_context()
                d_second_part(z, 7)

            dve.wait_ge(s["tok_h0"], NT // 2 + 1)
            dve.wait_ge(s["tok_h1"], NT // 2 + 1)
            V.memset(flat(Dm), 0.0)
            V.memset(flat(mx3), 0.0)
            StageA(0).stats()
            pipeline(dve, step)

            ch = Chain(dve, s["m_dve"], 0, 30)
            V.memset(zer, 0.0).then_inc(s["m_zero"], 1)
            V.memset(ones8[0:T], 1.0)
            ch.link(V.tensor_tensor(cnt[0:T], run[0:T], const_at("ebase", T), ALU.subtract))
            V.tensor_copy(counts[0:1], cnt[0:1]).then_inc(s["m_counts"], 1)
            ch.link(V.tensor_scalar(cnt_i[0:T], cnt[0:T], 127.0, None, ALU.add))
            ch.link(V.tensor_scalar(cnt_i[0:T], cnt_i[0:T], 7, None, ALU.arith_shift_right))
            ch.link(V.tensor_copy(ntil[0:T], cnt_i[0:T]))
            ch.link(V.tensor_tensor_scan(mend[0:T], ones8[0:T], ntil[0:T], 0.0, ALU.mult, ALU.add))
            tl = const_at("tile", 1)
            by_tile = tl.unsqueeze(2).to_broadcast([1, TILES, NE])
            by_e = lambda a: a[0:1].unsqueeze(1).to_broadcast([1, TILES, NE])
            ch.link(V.tensor_tensor(over[0:1], by_tile, by_e(mend), ALU.is_ge))
            ch.link(V.tensor_reduce(m_e[0:1], over[0:1], AX.X, ALU.add))
            ch.link(V.tensor_tensor(over2[0:1], over[0:1], by_e(ntil), ALU.mult))
            ch.link(V.tensor_reduce(m_st[0:1], over2[0:1], AX.X, ALU.add))
            V.tensor_scalar(tile_e[:], m_e[0:1], NE - 1.0, None, ALU.min)
            V.tensor_scalar(m_ok[0:1], m_e[0:1], NE - 0.5, None, ALU.is_lt)
            ch.link(V.tensor_tensor(m_st[0:1], tl, m_st[0:1], ALU.subtract))
            ch.link(V.tensor_scalar(m_e[0:1], m_e[0:1], float(REGION), None, ALU.mult))
            ch.link(V.scalar_tensor_tensor(m_row[0:1], m_st[0:1], 128.0, m_e[0:1], ALU.mult, ALU.add))
            ch.link(V.tensor_tensor(m_row[0:1], m_row[0:1], m_ok[0:1], ALU.mult))
            V.tensor_copy(tile_in[:], m_row[0:1]).then_inc(s["m_maps"], 1)

            def result_rows():
                nd = 2 * NT
                d = dest[0:T].rearrange("p k t -> p (k t)")
                ch.link(V.tensor_tensor(shift[0:T], mend[0:T], ntil[0:T], ALU.subtract))
                ch.link(V.scalar_tensor_tensor(shift[0:T], shift[0:T], 128.0, const_at("ebase", T), ALU.mult, ALU.subtract))
                V.tensor_copy(destf[0:T], d)
                V.tensor_copy(acc[0:T], d)
                ch.link(V.tensor_tensor(dshift[0:T, 1:NE], shift[0:T, 1:NE], shift[0:T, 0:NE - 1], ALU.subtract))
                for e in range(1, NE):
                    ch.link(V.tensor_scalar(term[0:T], destf[0:T], float(e * REGION), dshift[0:T, e:e + 1],
                                            ALU.is_ge, ALU.mult))
                    ch.link(V.tensor_tensor(acc[0:T], acc[0:T], term[0:T], ALU.add))
                V.tensor_copy(d, acc[0:T]).then_inc(s["m_dest"], 1)
                ch.end()

            def m_copy_x(par, use, i):
                dve.wait_ge((s["m_xT_ps0"], s["m_xT_ps1"])[par], use + 1)
                x_ps = bank(2, (DC * 128,))
                V.tensor_copy(flat(xTh[par]), x_ps).then_inc(s["m_xT_high"], 1)
                dve.wait_ge(s["m_xT_high"], i + 1)
                V.tensor_tensor(flat(xTl[par]), x_ps, flat(xTh[par]), ALU.subtract).then_inc(s["m_xT"], 1)

            def m_gate(i, par):
                dve.wait_ge(s["m_silu"], i + 1)
                dve.wait_ge(s["m_u_ps"], i + 1)
                V.scalar_tensor_tensor(ga[par], bank(1, (F,)), AS / WS, gs, ALU.mult, ALU.mult).then_inc(s["m_a"], 1)

            def m_copy_a(i):
                for n in range(2):
                    dve.wait_ge(s["m_aT_high"], i * 2 + (n + 1))
                    half = slice(2 * n, 2 * n + 2)
                    last = V.tensor_tensor(gaTl[:, half], bank((3, 5)[n], (2, 128)), gaTh[:, half], ALU.subtract)
                last.then_inc(s["m_aT"], 1)

            m_copy_x(0, 1, 0)
            m_copy_x(1, 1, 1)
            m_gate(0, 0)
            result_rows()
            with dve.Fori(0, (TILES - 2) // 2) as j:
                for par in (1, 0):
                    i = 2 * j + 2 - par
                    m_copy_a(i - 1)
                    m_copy_x(1 - par, j + 2, i + 1)
                    m_gate(i, par)
            m_copy_a(TILES - 2)
            m_gate(TILES - 1, 1)
            m_copy_a(TILES - 1)

            with dve.Fori(0, B // WAYS) as j:
                for par in range(WAYS):
                    landed, got = s[f"f_h{par}"], s[f"f_y{par}"]
                    i = WAYS * j + par
                    ch = Chain(dve, s["f_dve"], i, 3)
                    w = wnow[par]
                    V.tensor_copy(w[0:T], wtop[0:T, ds(2 * i, QT), :]).then_inc(s["f_w"], 1)
                    dve.wait_ge(s["f_w"], i + 1)
                    dve.wait_ge(landed, j * 16 + 16)
                    dve.wait_ge(got, j * (16 * 2 * QT) + 16 * 2 * QT)
                    h = h2b[par]
                    for t in range(QT):
                        last = V.scalar_tensor_tensor(y1[par][0:T, t], y1[par][0:T, t], w[0:T, t, 0:1], h[0:T, t],
                                                      ALU.mult, ALU.add)
                    ch.link(last)
                    for t in range(QT):
                        last = V.scalar_tensor_tensor(h[0:T, t], y2[par][0:T, t], w[0:T, t, 1:2], y1[par][0:T, t],
                                                      ALU.mult, ALU.add)
                    ch.link(last)
                    ch.link(V.tensor_scalar(h[0:T], h[0:T], CLIP, -CLIP, ALU.min, ALU.max))
                    V.tensor_tensor(h[0:T], h[0:T], H[0:T, ds(2 * i, QT), :], ALU.add).then_inc(s["f_out"], 1)
                    ch.end()

        @block.gpsimd
        def _(po):
            P = nc.gpsimd
            half_ = mhalf[0:T]

            def take_wait(word=0):
                P.tensor_tensor(gate_p[:, word:word + 1], mhalf[0:1, 0:1], mhalf[0:1, 0:1], ALU.add)

            def rstd(i, ready, sm, at, to, done):
                po.wait_ge(ready, i + 1)
                P.tensor_tensor(sm[0:T, to:to + 2], sm[0:T, at:at + 2], half_, ALU.pow).then_inc(done, 1)

            def rms(i, ready, sm, step_done, done, at, to, eps):
                po.wait_ge(ready, i + 1)
                P.tensor_tensor(sm[0:T, 12:14], sm[0:T, at:at + 2], eps, ALU.add).then_inc(step_done, 1)
                po.wait_ge(step_done, i + 1)
                P.tensor_tensor(sm[0:T, to:to + 2], sm[0:T, 12:14], half_, ALU.pow).then_inc(done, 1)

            @optional
            def z_values(z):
                po.wait_ge(s["b_qkv"], z + 1)
                if later(z):
                    po.wait_ge(s["b_pv_ps"], z * UNITS)
                take_wait(1)
                for g in range(NKV):
                    last = P.tensor_copy(vz[0:T, :, g, 32 * g:32 * g + HD],
                                         qkv[0:T, :, (NH + NKV + g) * HD:(NH + NKV + g + 1) * HD])
                last.then_inc(s["b_vz"], 1)

            @optional
            def b_rstd(b):
                rstd(b, s["b_var"], smB, 8, 10, s["b_rstd"])
                po.wait_ge(s["b_rstd"], b + 1)
                take_wait(2)
                P.tensor_copy(rstdB[0:T, ds(2 * b, QT)], smB[0:T, 10:12])
                P.tensor_copy(meanB[0:T, ds(2 * b, QT)], mvB[0:T, :, 0]).then_inc(s["b_mean"], 1)

            @optional
            def b_rms(b):
                rms(b, s["b_ms"], smB, s["q_pool"], s["b_r1"], 0, 2, epsc[0:T, 1])

            @optional
            def b_rope_sin(b):
                po.wait_ge(s["b_qkv"], b + 1)
                heads, hh = NH + NKV, HD // 2
                src = qkv[0:T, :, 0:heads * HD].rearrange("p t (h d) -> p t h d", d=HD)
                dst = t2[0:T].rearrange("p t (h d) -> p t h d", d=HD)
                sin = const_at("sin", T).rearrange("p (t d) -> p t d", t=QT)
                for lo, hi in ((0, hh), (hh, 0)):
                    tab = sin[:, :, lo:lo + hh].unsqueeze(2).to_broadcast([T, QT, heads, hh])
                    last = P.tensor_tensor(dst[:, :, :, lo:lo + hh], src[:, :, :, hi:hi + hh], tab, ALU.mult)
                last.then_inc(s["b_sinpart"], 1)

            @optional
            def a_rstd(a):
                rstd(a, s["a_var"], smA, 8, 10, s["a_rstd"])

            @optional
            def c_stat(c):
                po.wait_ge(s["b_mean"], c + 1)
                if later(c):
                    po.wait_ge(s["c_y"], c)
                take_wait(3)
                P.tensor_copy(smC[0:T, 8:10], meanB[0:T, ds(2 * c, QT)])
                P.tensor_copy(smC[0:T, 10:12], rstdB[0:T, ds(2 * c, QT)]).then_inc(s["c_stat"], 1)

            @optional
            def c_rms(c):
                rms(c, s["b_ms2"], smC, s["c_pool"], s["b_r2"], 0, 6, epsc[0:T, 0])

            @optional
            def c_scatter(c):
                po.wait_ge(s["b_dest"], c + 1)
                take_wait()
                for k in range(TOPK):
                    for t in range(QT):
                        P.indirect_dma_start(out=x_rows, out_offset=bass.IndirectOffsetOnAxis(ap=dnow[0:T, k, t:t + 1], axis=0),
                                             in_=hn[0:T, t], in_offset=None).then_inc(s["b_scat"], 16)

            def step(z, c, b, a, n=None):
                z_values(z)
                b_rms(b)
                c_stat(z)
                c_rms(c)
                b_rope_sin(b)
                c_scatter(c)
                a_rstd(n)
                b_rstd(a)

            po.wait_ge(s["tok_h0"], NT // 2 + 1)
            po.wait_ge(s["tok_h1"], NT // 2 + 1)
            P.memset(vz[0:T], 0.0).then_inc(s["zeroed"], 1)
            po.wait_ge(s["zeroed"], 1)
            for g in range(NKV):
                P.memset(vz[0:T, :, g, 32 * g + HD:32 * g + HD + 1], 1.0)
            a_rstd(0)
            pipeline(po, step)

            po.wait_ge(s["m_dest"], 1)
            po.wait_ge(s["m_st0"], 16 * (TILES // 2 + 1))
            po.wait_ge(s["m_st1"], 16 * (TILES // 2 + 1))
            with po.Fori(0, B // WAYS) as j:
                for par in range(WAYS):
                    got = s[f"f_y{par}"]
                    i = WAYS * j + par
                    po.wait_ge(s[f"f_st{par}"], j * 16 + 16)
                    P.tensor_copy(gidx[par][0:T], dest[0:T, :, ds(2 * i, QT)]).then_inc(s["f_idx"], 1)
                    po.wait_ge(s["f_idx"], i + 1)
                    take_wait()
                    for k, y_ in enumerate((y1, y2)):
                        for t in range(QT):
                            P.indirect_dma_start(out=y_[par][0:T, t], out_offset=None, in_=y_rows,
                                                 in_offset=bass.IndirectOffsetOnAxis(ap=gidx[par][0:T, k, t:t + 1], axis=0)
                                                 ).then_inc(got, 16)


_INS = ["x", "L0_tok_W_h", "L0_tok_b_h", "L0_tok_W_o", "L0_tok_b_o", "L0_tok_W_r", "L0_tok_b_r", "L0_attn_Wq",
        "L0_attn_bq", "L0_attn_Wk", "L0_attn_bk", "L0_attn_Wv", "L0_attn_bv", "L0_ffn_ln1_w", "L0_ffn_ln2_w",
        "L0_ffn_Wq", "L0_ffn_Wk", "L0_ffn_Wv", "L0_ffn_Wo", "L0_ffn_Wr", "L0_ffn_Wg", "L0_ffn_Wu", "L0_ffn_Wd"]


def kernel(**inputs):
    import concourse.bacc as _bacc
    from concourse.bass_utils import run_bass_kernel_spmd as _run

    nc = _bacc.Bacc("TRN2", target_bir_lowering=False, num_devices=1)
    arrays, args = {}, []
    for name in _INS:
        a = np.ascontiguousarray(inputs[name])
        arrays[f"in_{name}"] = a
        args.append(nc.dram_tensor(f"in_{name}", a.shape, mybir.dt.from_np(a.dtype), kind="ExternalInput").ap())
    table, _ = constants()
    arrays["in_const"] = table
    args.append(nc.dram_tensor("in_const", table.shape, mybir.dt.float32, kind="ExternalInput").ap())
    args.append(nc.dram_tensor("out", (B, S, D), mybir.dt.float32, kind="ExternalOutput").ap())
    build(nc, *args)
    r = _run(nc, [arrays], core_ids=[0])
    return r.results[0]["out"]
```
